# Optimizing a Trainium2 kernel written in Bass

```python
import numpy as np
import jax
import jax.numpy as jnp

def _softmax(x, axis=-1):
    return jax.nn.softmax(x, axis=axis)

def _gelu(x):
    return jax.nn.gelu(x, approximate=True)

def _silu(x):
    return jax.nn.silu(x)

def _sigmoid(x):
    return jax.nn.sigmoid(x)

def _layernorm(x, axis=-1, eps=1e-05):
    m = jnp.mean(x, axis=axis, keepdims=True)
    v = jnp.var(x, axis=axis, keepdims=True)
    return (x - m) / jnp.sqrt(v + eps)

def _scatter_add(tgt, idx, src, axis=0):
    return tgt.at[idx].add(src)

def _segment_sum(src, seg, n):
    return jax.ops.segment_sum(src, seg, n)
kernel_name = 'mk_decoder_postln_d2_seqx_r4_6eb10c'

def setup_inputs(seed: int=0):
    np.random.seed(seed)
    _w = jnp.asarray

    def _rec_inputs():
        import jax
        import jax.numpy as jnp
        _rk = jax.random.key(seed)
        x = -0.0005207 + 1.001 * jax.random.normal(jax.random.fold_in(_rk, 1), (8, 256, 256), jnp.float32)
        _lenS = 256 - jax.random.randint(jax.random.fold_in(_rk, 7), (8,), 0, max(1, 256 // 4) + 1, jnp.int32)
        _lenS2 = 256 - jax.random.randint(jax.random.fold_in(_rk, 8), (8,), 0, max(1, 256 // 4) + 1, jnp.int32)
        _ctx_1024P = jax.random.normal(jax.random.fold_in(_rk, 11), (8, 16, 256), jnp.float32)
        _ctx_1024c = jax.random.dirichlet(jax.random.fold_in(_rk, 511), 0.3 * jnp.ones((16,), jnp.float32), (8, 256))
        _ctx_1024t = jnp.einsum('bsk,bkd->bsd', _ctx_1024c, _ctx_1024P)
        _ctx_1024t = _ctx_1024t * jax.lax.rsqrt(jnp.mean(jnp.square(_ctx_1024t)) + 1e-12) * 0.953939
        ctx_1024 = 2.81802e-05 + 1.00001 * (_ctx_1024t + 0.3 * jax.random.normal(jax.random.fold_in(_rk, 611), (8, 256, 256), jnp.float32))
        fside_BxSxS2_0 = jax.random.uniform(jax.random.fold_in(_rk, 13), (8, 256, 256), jnp.float32, 0.0, 1)
        _validS = jnp.arange(256)[None, :] < _lenS[:, None]
        _validS2 = jnp.arange(256)[None, :] < _lenS2[:, None]
        _causal = jnp.tril(jnp.ones((256, 256), dtype=bool))
        mask_BxS2_bf1 = jnp.ones((8, 256), dtype=bool)
        mask_BxSxS2_ik1 = jnp.where(jnp.broadcast_to(_validS2[:, None, :], (8, 256, 256)), 1, 0).astype(jnp.int32)
        return (x, ctx_1024, fside_BxSxS2_0, mask_BxS2_bf1, mask_BxSxS2_ik1)
    x, ctx_1024, fside_BxSxS2_0, mask_BxS2_bf1, mask_BxSxS2_ik1 = _rec_inputs()

    def _L0_attn_setup():
        import jax, jax.numpy as jnp
        import numpy as np
        import math
        N_EMBD = 256
        N_HEAD = 16
        N_LAYER = 12
        key = jax.random.key(seed)
        kx, kw, kb = jax.random.split(key, 3)
        B, T, C = (4, 512, N_EMBD)
        x = jax.random.normal(kx, (B, T, C), dtype=jnp.float32)
        bound = 1.0 / math.sqrt(C)
        W = jax.random.uniform(kw, (3 * C, C), minval=-bound, maxval=bound, dtype=jnp.float32)
        W = W * (1.0 / math.sqrt(N_LAYER * 2))
        b = jax.random.uniform(kb, (3 * C,), minval=-bound, maxval=bound, dtype=jnp.float32)
        return {'x': x, 'W': W, 'b': b}
    _L0_attn_all = _L0_attn_setup()
    _L0_attn_in = {k: v for k, v in _L0_attn_all.items() if k in ('W', 'b')}
    del _L0_attn_all

    def _L0_xattn_setup():
        import jax, jax.numpy as jnp
        import numpy as np
        EMB = 256
        HEADS = 16
        HEAD_DIM = EMB // HEADS
        EPS = 1e-05

        def _layer_norm(x, gamma, beta):
            m = jnp.mean(x, axis=-1, keepdims=True)
            v = jnp.mean(jnp.square(x - m), axis=-1, keepdims=True)
            return (x - m) / jnp.sqrt(v + EPS) * gamma + beta
        key = jax.random.key(seed)
        ks = jax.random.split(key, 8)
        B, Tx, Tc = (2, 256, 2048)
        scale = 1.0 / np.sqrt(EMB)
        return {'x': jax.random.normal(ks[0], (B, Tx, EMB), dtype=jnp.float32), 'context': jax.random.normal(ks[1], (B, Tc, EMB), dtype=jnp.float32), 'context_mask': jnp.ones((B, Tc), dtype=bool), 'Wq': jax.random.normal(ks[2], (EMB, EMB), dtype=jnp.float32) * scale, 'Wk': jax.random.normal(ks[3], (EMB, EMB), dtype=jnp.float32) * scale, 'Wv': jax.random.normal(ks[4], (EMB, EMB), dtype=jnp.float32) * scale, 'Wo': jax.random.normal(ks[5], (EMB, EMB), dtype=jnp.float32) * scale, 'bo': jnp.zeros((EMB,), dtype=jnp.float32), 'g1': jnp.ones((EMB,), dtype=jnp.float32), 'b1': jnp.zeros((EMB,), dtype=jnp.float32), 'g2': jnp.ones((EMB,), dtype=jnp.float32), 'b2': jnp.zeros((EMB,), dtype=jnp.float32)}
    _L0_xattn_all = _L0_xattn_setup()
    _L0_xattn_in = {k: v for k, v in _L0_xattn_all.items() if k in ('Wq', 'Wk', 'Wv', 'Wo', 'bo', 'g1', 'b1', 'g2', 'b2')}
    del _L0_xattn_all

    def _L0_ffn_setup():
        import jax, jax.numpy as jnp
        import numpy as np
        DIM = 256
        HEADS = 16
        HD = DIM // HEADS
        M = 64
        E = 4
        K = 2
        HID = 512
        MID = 512
        LB = 0.01
        EPS = 1.1920929e-07

        def _rms(x, w):
            return x * jax.lax.rsqrt(jnp.mean(x * x, axis=-1, keepdims=True) + EPS) * w

        def _gelu(x):
            return jax.nn.gelu(x, approximate=False)
        key = jax.random.key(seed)
        ks = jax.random.split(key, 20)
        d = DIM
        w = lambda k, s: jax.random.normal(k, s, jnp.float32) * 0.02
        return {'x': jax.random.normal(ks[0], (4, 256, d), jnp.float32), 'n1_w': jnp.ones((d,), jnp.float32), 'n2_w': jnp.ones((d,), jnp.float32), 'wq': w(ks[1], (d, d)), 'wk': w(ks[2], (d, d)), 'wv': w(ks[3], (d, d)), 'wo': w(ks[4], (d, d)), 'qn_w': jnp.ones((HD,), jnp.float32), 'kn_w': jnp.ones((HD,), jnp.float32), 'gate_w': w(ks[5], (E, d)), 'e0_up': w(ks[6], (HID, d)), 'e0_down': w(ks[7], (d, HID)), 'e1_w1': w(ks[8], (HID, d)), 'e1_w2': w(ks[9], (HID, d)), 'e1_down': w(ks[10], (d, HID)), 'e2_l1': w(ks[11], (MID, d)), 'e2_l2': w(ks[12], (HID, MID)), 'e2_l3': w(ks[13], (MID, HID)), 'e2_l4': w(ks[14], (d, MID)), 'e3_down': w(ks[15], (d, d)), 'e3_up': w(ks[16], (HID, d)), 'e3_out': w(ks[17], (d, HID))}
    _L0_ffn_all = _L0_ffn_setup()
    _L0_ffn_in = {k: v for k, v in _L0_ffn_all.items() if k in ('n1_w', 'n2_w', 'wq', 'wk', 'wv', 'wo', 'qn_w', 'kn_w', 'gate_w', 'e0_up', 'e0_down', 'e1_w1', 'e1_w2', 'e1_down', 'e2_l1', 'e2_l2', 'e2_l3', 'e2_l4', 'e3_down', 'e3_up', 'e3_out')}
    del _L0_ffn_all

    def _L1_attn_setup():
        import jax, jax.numpy as jnp
        import numpy as np
        D_MODEL = 256
        NHEAD = 16
        HEAD_DIM = D_MODEL // NHEAD
        LN_EPS = 1e-05
        ROPE_BASE = 10000.0

        def _rope_cos_sin(n, head_dim):
            inv_freq = 1.0 / ROPE_BASE ** (jnp.arange(0, head_dim, 2, dtype=jnp.float32) / head_dim)
            t = jnp.arange(n, dtype=jnp.float32)
            freqs = jnp.outer(t, inv_freq)
            return (jnp.cos(freqs), jnp.sin(freqs))

        def _apply_rope(x, cos, sin):
            B, H, N, hd = x.shape
            xr = x.reshape(B, H, N, hd // 2, 2)
            x0, x1 = (xr[..., 0], xr[..., 1])
            c = cos[None, None]
            s = sin[None, None]
            rot = jnp.stack([x0 * c - x1 * s, x0 * s + x1 * c], axis=-1)
            return rot.reshape(B, H, N, hd)
        key = jax.random.key(seed)
        ks = jax.random.split(key, 6)
        D = D_MODEL
        scale = 1.0 / np.sqrt(D)
        x = jax.random.normal(ks[0], (2, 512, D), dtype=jnp.float32)
        Wq = jax.random.normal(ks[1], (D, D), dtype=jnp.float32) * scale
        Wk = jax.random.normal(ks[2], (D, D), dtype=jnp.float32) * scale
        Wv = jax.random.normal(ks[3], (D, D), dtype=jnp.float32) * scale
        Wo = jax.random.normal(ks[4], (D, D), dtype=jnp.float32) * scale
        bq = jnp.zeros((D,), jnp.float32)
        bk = jnp.zeros((D,), jnp.float32)
        bv = jnp.zeros((D,), jnp.float32)
        bo = jnp.zeros((D,), jnp.float32)
        ln_w = jnp.ones((D,), jnp.float32)
        ln_b = jnp.zeros((D,), jnp.float32)
        return {'x': x, 'ln_w': ln_w, 'ln_b': ln_b, 'Wq': Wq, 'bq': bq, 'Wk': Wk, 'bk': bk, 'Wv': Wv, 'bv': bv, 'Wo': Wo, 'bo': bo}
    _L1_attn_all = _L1_attn_setup()
    _L1_attn_in = {k: v for k, v in _L1_attn_all.items() if k in ('ln_w', 'ln_b', 'Wq', 'bq', 'Wk', 'bk', 'Wv', 'bv', 'Wo', 'bo')}
    del _L1_attn_all

    def _L1_xattn_setup():
        import jax, jax.numpy as jnp
        import numpy as np
        NUM_HEADS = 16
        HIDDEN = 256
        B, S = (2, 512)

        def _split_heads(x, H):
            b, s, d = x.shape
            return x.reshape(b, s, H, d // H).transpose(0, 2, 1, 3)
        key = jax.random.key(seed)
        ks = jax.random.split(key, 14)
        D = HIDDEN
        scale = 1.0 / np.sqrt(D)
        inp = {'query': jax.random.normal(ks[0], (B, S, D), jnp.float32), 'key_in': jax.random.normal(ks[1], (B, S, D), jnp.float32), 'value': jax.random.normal(ks[2], (B, S, D), jnp.float32), 'group_prob': jax.random.uniform(ks[3], (B, S, S), jnp.float32), 'mask': jax.random.randint(ks[4], (B, S, S), 0, 2, jnp.int32), 'wq_k': jax.random.normal(ks[5], (D, D), jnp.float32) * scale, 'wq_b': jnp.zeros((D,), jnp.float32), 'wk_k': jax.random.normal(ks[6], (D, D), jnp.float32) * scale, 'wk_b': jnp.zeros((D,), jnp.float32), 'wv_k': jax.random.normal(ks[7], (D, D), jnp.float32) * scale, 'wv_b': jnp.zeros((D,), jnp.float32), 'wo_k': jax.random.normal(ks[8], (D, D), jnp.float32) * scale, 'wo_b': jnp.zeros((D,), jnp.float32)}
        return inp
    _L1_xattn_all = _L1_xattn_setup()
    _L1_xattn_in = {k: v for k, v in _L1_xattn_all.items() if k in ('wq_k', 'wq_b', 'wk_k', 'wk_b', 'wv_k', 'wv_b', 'wo_k', 'wo_b')}
    del _L1_xattn_all

    def _L1_ffn_setup():
        import jax, jax.numpy as jnp
        import numpy as np
        B, S, M, E, DFF = (4, 512, 256, 8, 1024)
        CAPACITY_FACTOR = 1.25

        def _top1_gate(tokens, wg, capacity):
            gates = jax.nn.softmax(tokens @ wg)
            expert_idx = jnp.argmax(gates, axis=-1)
            mask1 = jax.nn.one_hot(expert_idx, gates.shape[-1], dtype=gates.dtype)
            pos = jnp.sum(jnp.cumsum(mask1, axis=0) * mask1, axis=-1).astype(jnp.int32) - 1
            keep = (pos < capacity).astype(gates.dtype)
            mask1c = mask1 * keep[:, None]
            gates1 = jnp.sum(gates * mask1c, axis=-1)
            loc_oh = jax.nn.one_hot(pos, capacity, dtype=gates.dtype)
            combine = gates1[:, None, None] * mask1c[:, :, None] * loc_oh[:, None, :]
            dispatch = (combine > 0).astype(tokens.dtype)
            return (combine, dispatch)
        key = jax.random.key(seed)
        k = jax.random.split(key, 5)
        x = jax.random.normal(k[0], (B, S, M), dtype=jnp.float32)
        wg = jax.random.normal(k[1], (M, E), dtype=jnp.float32) * 0.02
        w1 = jax.random.normal(k[2], (E, M, DFF), dtype=jnp.float32) * 0.02
        b1 = jnp.zeros((E, DFF), dtype=jnp.float32)
        w2 = jax.random.normal(k[3], (E, DFF, M), dtype=jnp.float32) * 0.02
        b2 = jnp.zeros((E, M), dtype=jnp.float32)
        return {'x': x, 'wg': wg, 'w1': w1, 'b1': b1, 'w2': w2, 'b2': b2}
    _L1_ffn_all = _L1_ffn_setup()
    _L1_ffn_in = {k: v for k, v in _L1_ffn_all.items() if k in ('wg', 'w1', 'b1', 'w2', 'b2')}
    del _L1_ffn_all
    return {'x': x, 'ctx_1024': ctx_1024, 'fside_BxSxS2_0': fside_BxSxS2_0, 'mask_BxS2_bf1': mask_BxS2_bf1, 'mask_BxSxS2_ik1': mask_BxSxS2_ik1, 'L0_attn_W': _L0_attn_in['W'], 'L0_attn_b': _L0_attn_in['b'], 'L0_xattn_Wq': _L0_xattn_in['Wq'], 'L0_xattn_Wk': _L0_xattn_in['Wk'], 'L0_xattn_Wv': _L0_xattn_in['Wv'], 'L0_xattn_Wo': _L0_xattn_in['Wo'], 'L0_xattn_bo': _L0_xattn_in['bo'], 'L0_xattn_g1': _L0_xattn_in['g1'], 'L0_xattn_b1': _L0_xattn_in['b1'], 'L0_xattn_g2': _L0_xattn_in['g2'], 'L0_xattn_b2': _L0_xattn_in['b2'], 'L0_ffn_n1_w': _L0_ffn_in['n1_w'], 'L0_ffn_n2_w': _L0_ffn_in['n2_w'], 'L0_ffn_wq': _L0_ffn_in['wq'], 'L0_ffn_wk': _L0_ffn_in['wk'], 'L0_ffn_wv': _L0_ffn_in['wv'], 'L0_ffn_wo': _L0_ffn_in['wo'], 'L0_ffn_qn_w': _L0_ffn_in['qn_w'], 'L0_ffn_kn_w': _L0_ffn_in['kn_w'], 'L0_ffn_gate_w': _L0_ffn_in['gate_w'], 'L0_ffn_e0_up': _L0_ffn_in['e0_up'], 'L0_ffn_e0_down': _L0_ffn_in['e0_down'], 'L0_ffn_e1_w1': _L0_ffn_in['e1_w1'], 'L0_ffn_e1_w2': _L0_ffn_in['e1_w2'], 'L0_ffn_e1_down': _L0_ffn_in['e1_down'], 'L0_ffn_e2_l1': _L0_ffn_in['e2_l1'], 'L0_ffn_e2_l2': _L0_ffn_in['e2_l2'], 'L0_ffn_e2_l3': _L0_ffn_in['e2_l3'], 'L0_ffn_e2_l4': _L0_ffn_in['e2_l4'], 'L0_ffn_e3_down': _L0_ffn_in['e3_down'], 'L0_ffn_e3_up': _L0_ffn_in['e3_up'], 'L0_ffn_e3_out': _L0_ffn_in['e3_out'], 'L1_attn_ln_w': _L1_attn_in['ln_w'], 'L1_attn_ln_b': _L1_attn_in['ln_b'], 'L1_attn_Wq': _L1_attn_in['Wq'], 'L1_attn_bq': _L1_attn_in['bq'], 'L1_attn_Wk': _L1_attn_in['Wk'], 'L1_attn_bk': _L1_attn_in['bk'], 'L1_attn_Wv': _L1_attn_in['Wv'], 'L1_attn_bv': _L1_attn_in['bv'], 'L1_attn_Wo': _L1_attn_in['Wo'], 'L1_attn_bo': _L1_attn_in['bo'], 'L1_xattn_wq_k': _L1_xattn_in['wq_k'], 'L1_xattn_wq_b': _L1_xattn_in['wq_b'], 'L1_xattn_wk_k': _L1_xattn_in['wk_k'], 'L1_xattn_wk_b': _L1_xattn_in['wk_b'], 'L1_xattn_wv_k': _L1_xattn_in['wv_k'], 'L1_xattn_wv_b': _L1_xattn_in['wv_b'], 'L1_xattn_wo_k': _L1_xattn_in['wo_k'], 'L1_xattn_wo_b': _L1_xattn_in['wo_b'], 'L1_ffn_wg': _L1_ffn_in['wg'], 'L1_ffn_w1': _L1_ffn_in['w1'], 'L1_ffn_b1': _L1_ffn_in['b1'], 'L1_ffn_w2': _L1_ffn_in['w2'], 'L1_ffn_b2': _L1_ffn_in['b2']}

def reference(x, ctx_1024, fside_BxSxS2_0, mask_BxS2_bf1, mask_BxSxS2_ik1, L0_attn_W, L0_attn_b, L0_xattn_Wq, L0_xattn_Wk, L0_xattn_Wv, L0_xattn_Wo, L0_xattn_bo, L0_xattn_g1, L0_xattn_b1, L0_xattn_g2, L0_xattn_b2, L0_ffn_n1_w, L0_ffn_n2_w, L0_ffn_wq, L0_ffn_wk, L0_ffn_wv, L0_ffn_wo, L0_ffn_qn_w, L0_ffn_kn_w, L0_ffn_gate_w, L0_ffn_e0_up, L0_ffn_e0_down, L0_ffn_e1_w1, L0_ffn_e1_w2, L0_ffn_e1_down, L0_ffn_e2_l1, L0_ffn_e2_l2, L0_ffn_e2_l3, L0_ffn_e2_l4, L0_ffn_e3_down, L0_ffn_e3_up, L0_ffn_e3_out, L1_attn_ln_w, L1_attn_ln_b, L1_attn_Wq, L1_attn_bq, L1_attn_Wk, L1_attn_bk, L1_attn_Wv, L1_attn_bv, L1_attn_Wo, L1_attn_bo, L1_xattn_wq_k, L1_xattn_wq_b, L1_xattn_wk_k, L1_xattn_wk_b, L1_xattn_wv_k, L1_xattn_wv_b, L1_xattn_wo_k, L1_xattn_wo_b, L1_ffn_wg, L1_ffn_w1, L1_ffn_b1, L1_ffn_w2, L1_ffn_b2):
    import jax
    import jax.numpy as jnp

    def _L0_attn_ref(x, W, b):
        import jax, jax.numpy as jnp
        import numpy as np
        import math
        N_EMBD = 256
        N_HEAD = 16
        N_LAYER = 12
        B, T, C = x.shape
        H = N_HEAD
        D = C // H
        qkv = jnp.einsum('btc,oc->bto', x, W) + b
        q, k, v = jnp.split(qkv, 3, axis=-1)
        q = q.reshape(B, T, H, D).transpose(0, 2, 1, 3)
        k = k.reshape(B, T, H, D).transpose(0, 2, 1, 3)
        v = v.reshape(B, T, H, D).transpose(0, 2, 1, 3)
        att = jnp.einsum('bhtd,bhsd->bhts', q, k) / math.sqrt(D)
        causal = jnp.tril(jnp.ones((T, T), dtype=bool))
        att = jnp.where(causal, att, -jnp.inf)
        att = jax.nn.softmax(att, axis=-1)
        y = jnp.einsum('bhts,bhsd->bhtd', att, v)
        return y.transpose(0, 2, 1, 3).reshape(B, T, C)

    def _L0_xattn_ref(x, context, context_mask, Wq, Wk, Wv, Wo, bo, g1, b1, g2, b2):
        import jax, jax.numpy as jnp
        import numpy as np
        EMB = 256
        HEADS = 16
        HEAD_DIM = EMB // HEADS
        EPS = 1e-05

        def _layer_norm(x, gamma, beta):
            m = jnp.mean(x, axis=-1, keepdims=True)
            v = jnp.mean(jnp.square(x - m), axis=-1, keepdims=True)
            return (x - m) / jnp.sqrt(v + EPS) * gamma + beta
        B, Tx, C = x.shape
        Tc = context.shape[1]
        xn = _layer_norm(x, g1, b1)
        cn = _layer_norm(context, g2, b2)
        q = (xn @ Wq.T).reshape(B, Tx, HEADS, HEAD_DIM)
        k = (cn @ Wk.T).reshape(B, Tc, HEADS, HEAD_DIM)
        v = (cn @ Wv.T).reshape(B, Tc, HEADS, HEAD_DIM)
        scores = jnp.einsum('bqhs,bkhs->bhqk', q, k) / np.sqrt(HEAD_DIM)
        scores = jnp.where(context_mask[:, None, None, :], scores, -jnp.inf)
        attn = jax.nn.softmax(scores, axis=-1)
        out = jnp.einsum('bhqk,bkhs->bqhs', attn, v).reshape(B, Tx, C)
        return out @ Wo.T + bo

    def _L0_ffn_ref(x, n1_w, n2_w, wq, wk, wv, wo, qn_w, kn_w, gate_w, e0_up, e0_down, e1_w1, e1_w2, e1_down, e2_l1, e2_l2, e2_l3, e2_l4, e3_down, e3_up, e3_out):
        import jax, jax.numpy as jnp
        import numpy as np
        DIM = 256
        HEADS = 16
        HD = DIM // HEADS
        M = 64
        E = 4
        K = 2
        HID = 512
        MID = 512
        LB = 0.01
        EPS = 1.1920929e-07

        def _rms(x, w):
            return x * jax.lax.rsqrt(jnp.mean(x * x, axis=-1, keepdims=True) + EPS) * w

        def _gelu(x):
            return jax.nn.gelu(x, approximate=False)
        B, T, C = x.shape
        h = _rms(x, n1_w)
        heads = lambda w_: (h @ w_.T).reshape(B, T, HEADS, HD).transpose(0, 2, 1, 3)
        q = _rms(heads(wq), qn_w)
        k = _rms(heads(wk), kn_w)
        v = heads(wv)
        scores = jnp.einsum('bhqd,bhkd->bhqk', q, k) * HD ** (-0.5)
        causal = jnp.tril(jnp.ones((T, T), bool))
        scores = jnp.where(causal[None, None], scores, -jnp.inf)
        attn = jax.nn.softmax(scores, axis=-1)
        ao = jnp.einsum('bhqk,bhkd->bhqd', attn, v).transpose(0, 2, 1, 3).reshape(B, T, C) @ wo.T
        ao = ao.at[:, :, :M].set(0.0)
        x = x + ao
        xf = _rms(x, n2_w).reshape(-1, C)
        N = xf.shape[0]
        logits = jnp.nan_to_num(xf @ gate_w.T)
        probs = jax.nn.softmax(logits, axis=-1)
        topv, topi = jax.lax.top_k(probs, K)
        topv = topv / (topv.sum(-1, keepdims=True) + 1e-08)
        wts = jnp.zeros((N, E), x.dtype).at[jnp.arange(N)[:, None], topi].add(topv)
        o0 = _gelu(xf @ e0_up.T) @ e0_down.T
        o1 = jax.nn.silu(xf @ e1_w1.T) * (xf @ e1_w2.T) @ e1_down.T
        o2 = _gelu(_gelu(_gelu(xf @ e2_l1.T) @ e2_l2.T) @ e2_l3.T) @ e2_l4.T
        o3 = _gelu(_gelu(xf @ e3_down.T) @ e3_up.T) @ e3_out.T
        moe = wts[:, 0:1] * o0 + wts[:, 1:2] * o1 + wts[:, 2:3] * o2 + wts[:, 3:4] * o3
        moe = moe.reshape(B, T, C).at[:, :, :M].set(0.0)
        return x + moe

    def _L1_attn_ref(x, ln_w, ln_b, Wq, bq, Wk, bk, Wv, bv, Wo, bo):
        import jax, jax.numpy as jnp
        import numpy as np
        D_MODEL = 256
        NHEAD = 16
        HEAD_DIM = D_MODEL // NHEAD
        LN_EPS = 1e-05
        ROPE_BASE = 10000.0

        def _rope_cos_sin(n, head_dim):
            inv_freq = 1.0 / ROPE_BASE ** (jnp.arange(0, head_dim, 2, dtype=jnp.float32) / head_dim)
            t = jnp.arange(n, dtype=jnp.float32)
            freqs = jnp.outer(t, inv_freq)
            return (jnp.cos(freqs), jnp.sin(freqs))

        def _apply_rope(x, cos, sin):
            B, H, N, hd = x.shape
            xr = x.reshape(B, H, N, hd // 2, 2)
            x0, x1 = (xr[..., 0], xr[..., 1])
            c = cos[None, None]
            s = sin[None, None]
            rot = jnp.stack([x0 * c - x1 * s, x0 * s + x1 * c], axis=-1)
            return rot.reshape(B, H, N, hd)
        B, N, D = x.shape
        H, hd = (NHEAD, HEAD_DIM)
        mu = jnp.mean(x, axis=-1, keepdims=True)
        var = jnp.mean(jnp.square(x - mu), axis=-1, keepdims=True)
        xn = (x - mu) * jax.lax.rsqrt(var + LN_EPS) * ln_w + ln_b

        def proj(W, b):
            return (xn @ W.T + b).reshape(B, N, H, hd).transpose(0, 2, 1, 3)
        q = proj(Wq, bq)
        k = proj(Wk, bk)
        v = proj(Wv, bv)
        cos, sin = _rope_cos_sin(N, hd)
        q = _apply_rope(q, cos, sin)
        k = _apply_rope(k, cos, sin)
        scores = jnp.einsum('bhqd,bhkd->bhqk', q, k) / jnp.sqrt(jnp.float32(hd))
        attn = jax.nn.softmax(scores, axis=-1)
        out = jnp.einsum('bhqk,bhkd->bhqd', attn, v)
        out = out.transpose(0, 2, 1, 3).reshape(B, N, D)
        return x + out @ Wo.T + bo

    def _L1_xattn_ref(query, key_in, value, group_prob, mask, wq_k, wq_b, wk_k, wk_b, wv_k, wv_b, wo_k, wo_b):
        import jax, jax.numpy as jnp
        import numpy as np
        NUM_HEADS = 16
        HIDDEN = 256
        B, S = (2, 512)

        def _split_heads(x, H):
            b, s, d = x.shape
            return x.reshape(b, s, H, d // H).transpose(0, 2, 1, 3)
        H = NUM_HEADS
        dh = query.shape[-1] // H
        q = _split_heads(query @ wq_k + wq_b, H)
        k = _split_heads(key_in @ wk_k + wk_b, H)
        v = _split_heads(value @ wv_k + wv_b, H)
        logits = jnp.einsum('bhqd,bhkd->bhqk', q, k) / jnp.sqrt(jnp.asarray(dh, q.dtype))
        neg = (1.0 - mask.astype(q.dtype)) * -1000000000.0
        logits = logits + neg[:, None, :, :]
        attn = jax.nn.softmax(logits, axis=-1)
        attn = attn * group_prob[:, None, :, :]
        out = jnp.einsum('bhqk,bhkd->bhqd', attn, v)
        out = out.transpose(0, 2, 1, 3).reshape(query.shape[0], -1, H * dh)
        return out @ wo_k + wo_b

    def _L1_ffn_ref(x, wg, w1, b1, w2, b2):
        import jax, jax.numpy as jnp
        import numpy as np
        B, S, M, E, DFF = (4, 512, 256, 8, 1024)
        CAPACITY_FACTOR = 1.25

        def _top1_gate(tokens, wg, capacity):
            gates = jax.nn.softmax(tokens @ wg)
            expert_idx = jnp.argmax(gates, axis=-1)
            mask1 = jax.nn.one_hot(expert_idx, gates.shape[-1], dtype=gates.dtype)
            pos = jnp.sum(jnp.cumsum(mask1, axis=0) * mask1, axis=-1).astype(jnp.int32) - 1
            keep = (pos < capacity).astype(gates.dtype)
            mask1c = mask1 * keep[:, None]
            gates1 = jnp.sum(gates * mask1c, axis=-1)
            loc_oh = jax.nn.one_hot(pos, capacity, dtype=gates.dtype)
            combine = gates1[:, None, None] * mask1c[:, :, None] * loc_oh[:, None, :]
            dispatch = (combine > 0).astype(tokens.dtype)
            return (combine, dispatch)
        d_model = x.shape[-1]
        tokens = x.reshape(-1, d_model)
        T = tokens.shape[0]
        num_experts = wg.shape[1]
        capacity = int(CAPACITY_FACTOR * T / num_experts)
        combine, dispatch = _top1_gate(tokens, wg, capacity)
        dispatched = jnp.einsum('sec,sm->ecm', dispatch, tokens)
        h = jax.nn.relu(jnp.einsum('ecm,emf->ecf', dispatched, w1) + b1[:, None, :])
        expert_out = jnp.einsum('ecf,efm->ecm', h, w2) + b2[:, None, :]
        combined = jnp.einsum('sec,ecm->sm', combine, expert_out)
        return combined.reshape(x.shape)
    x = _layernorm(x + _L0_attn_ref(x, L0_attn_W, L0_attn_b), axis=-1)
    x = _layernorm(x + _L0_xattn_ref(x, ctx_1024, mask_BxS2_bf1, L0_xattn_Wq, L0_xattn_Wk, L0_xattn_Wv, L0_xattn_Wo, L0_xattn_bo, L0_xattn_g1, L0_xattn_b1, L0_xattn_g2, L0_xattn_b2), axis=-1)
    x = _layernorm(x + _L0_ffn_ref(x, L0_ffn_n1_w, L0_ffn_n2_w, L0_ffn_wq, L0_ffn_wk, L0_ffn_wv, L0_ffn_wo, L0_ffn_qn_w, L0_ffn_kn_w, L0_ffn_gate_w, L0_ffn_e0_up, L0_ffn_e0_down, L0_ffn_e1_w1, L0_ffn_e1_w2, L0_ffn_e1_down, L0_ffn_e2_l1, L0_ffn_e2_l2, L0_ffn_e2_l3, L0_ffn_e2_l4, L0_ffn_e3_down, L0_ffn_e3_up, L0_ffn_e3_out), axis=-1)
    x = _layernorm(x + _L1_attn_ref(x, L1_attn_ln_w, L1_attn_ln_b, L1_attn_Wq, L1_attn_bq, L1_attn_Wk, L1_attn_bk, L1_attn_Wv, L1_attn_bv, L1_attn_Wo, L1_attn_bo), axis=-1)
    x = _layernorm(x + _L1_xattn_ref(x, ctx_1024, ctx_1024, fside_BxSxS2_0, mask_BxSxS2_ik1, L1_xattn_wq_k, L1_xattn_wq_b, L1_xattn_wk_k, L1_xattn_wk_b, L1_xattn_wv_k, L1_xattn_wv_b, L1_xattn_wo_k, L1_xattn_wo_b), axis=-1)
    x = _layernorm(x + _L1_ffn_ref(x, L1_ffn_wg, L1_ffn_w1, L1_ffn_b1, L1_ffn_w2, L1_ffn_b2), axis=-1)
    return x

_drawn_inputs = setup_inputs


def setup_inputs(seed=0):
    import zlib

    import numpy as np

    out = dict(_drawn_inputs(seed))
    spreads = {'L0_xattn_bo': (0.0, 0.1),
     'L0_xattn_g1': (1.0, 0.2),
     'L0_xattn_b1': (0.0, 0.474),
     'L0_xattn_g2': (1.0, 0.2),
     'L0_xattn_b2': (0.0, 0.1),
     'L0_ffn_n1_w': (1.0, 0.6),
     'L0_ffn_n2_w': (1.0, 0.6),
     'L0_ffn_qn_w': (1.0, 0.6),
     'L0_ffn_kn_w': (1.0, 0.6),
     'L1_attn_ln_w': (1.0, 0.2),
     'L1_attn_ln_b': (0.0, 0.1),
     'L1_attn_bq': (0.0, 0.8),
     'L1_attn_bk': (0.0, 0.8),
     'L1_attn_bv': (0.0, 0.1),
     'L1_attn_bo': (0.0, 0.1),
     'L1_xattn_wq_b': (0.0, 0.568),
     'L1_xattn_wk_b': (0.0, 0.8),
     'L1_xattn_wv_b': (0.0, 0.1),
     'L1_xattn_wo_b': (0.0, 0.1),
     'L1_ffn_b1': (0.0, 0.8),
     'L1_ffn_b2': (0.0, 0.447)}
    factors = {'L0_attn_W': 3.505,
     'L0_ffn_wq': 8.0,
     'L0_ffn_wk': 8.0,
     'L0_ffn_gate_w': 6.091,
     'L0_ffn_e0_up': 4.765,
     'L0_ffn_e0_down': 4.704,
     'L0_ffn_e1_w1': 8.0,
     'L0_ffn_e1_w2': 8.0,
     'L0_ffn_e1_down': 8.0,
     'L0_ffn_e2_l1': 8.0,
     'L0_ffn_e2_l2': 8.0,
     'L0_ffn_e2_l3': 8.0,
     'L0_ffn_e2_l4': 8.0,
     'L0_ffn_e3_down': 8.0,
     'L0_ffn_e3_up': 8.0,
     'L0_ffn_e3_out': 8.0}
    for name, (base, spread) in spreads.items():
        noise = np.random.default_rng([zlib.crc32(name.encode()), seed]).standard_normal(out[name].shape)
        drawn = base * np.exp(spread * noise) if base else spread * noise
        out[name] = jnp.asarray(drawn.astype(out[name].dtype))
    for name, factor in factors.items():
        out[name] = (out[name] * factor).astype(out[name].dtype)
    return out
```

```python
from contextlib import ExitStack

import numpy as np

import concourse.bass as bass
from concourse import mybir

F32 = mybir.dt.float32
BF16 = mybir.dt.bfloat16
I32 = mybir.dt.int32
U32 = mybir.dt.uint32
U8 = mybir.dt.uint8
ALU = mybir.AluOpType
ACT = mybir.ActivationFunctionType
AX = mybir.AxisListType

P = 128
B, S, C = 8, 256, 256
H, D = 16, 16
CC = C // P
TT = S // P
PAIRS = H // 2
LAYERS = 5
STREAMS = 2
HID = 512
E1, DFF, CAP = 8, 1024, int(1.25 * B * S / 8)
KEEP = 192
SKIP = C - KEEP
Q_PARTS = (0, 0, 1, 1, 0, 2)
K_PARTS = (0, 1, 0, 1, 2, 0)
ROWS = 16 * len(Q_PARTS)
SHIFT = 3
LOW = -1.0e30
CAUSAL = (0, 2)
SELF_LN = (1, 2, 3)


class Signal:

    def __init__(self, name, sem, known, step=1):
        self.name, self.sem, self.known, self.step, self.count = name, sem, known, step, 0

    def __call__(self, *label):
        self.count += self.step
        assert self.known["pass"] or not label or (self.name, label) not in self.known, label
        self.known[self.name, label] = self.count
        return self.sem, self.step

    def at(self, *label):
        assert not self.known["pass"] or (self.name, label) in self.known, (self.name, label)
        return self.sem, self.known.get((self.name, label), self.step)


def build(nc, t, known):
    outer = ExitStack()
    with outer:
        x5_dram = nc.dram_tensor("x5_rows", [B * S, C], F32, kind="Internal").ap()
        slots_dram = nc.dram_tensor("slot_rows", [E1 * CAP, C], F32, kind="Internal").ap()
        expert_dram = nc.dram_tensor("expert_rows", [E1 * CAP, C], F32, kind="Internal").ap()
        with ExitStack() as ctx:
            attention_layers(nc, ctx, t, known, x5_dram)
        with ExitStack() as ctx:
            routed_mixture(nc, ctx, t, known, x5_dram, slots_dram, expert_dram)


def attention_layers(nc, ctx, t, known, x5_dram):
    def sb(name, shape, dt=F32):
        return ctx.enter_context(nc.sbuf_tensor(name, shape, dt))

    work = []

    def signal(name, step=1):
        sem = ctx.enter_context(nc.semaphore(name))
        work.append(sem)
        return Signal(name, sem, known, step)

    ident = sb("ident", [P, P])
    ident_b = sb("ident_b", [P, P], BF16)
    causal_q = sb("causal_q", [P, P], BF16)
    causal_k = sb("causal_k", [P, P], BF16)
    rope_swap = sb("rope_swap", [P, P])
    head_ones = sb("head_ones", [P, P])
    rope_cos = sb("rope_cos", [P, S])
    rope_sin = sb("rope_sin", [P, S])
    ones_row = sb("ones_row", [1, P], BF16)
    sum_cols = sb("sum_cols", [P, 32])
    neg_half = sb("neg_half", [P, TT])
    eps_col = sb("eps_col", [P, 1])
    cols = sb("cols", [P, 32])
    rows = sb("rows", [P, 6, C])
    proj = sb("proj", [P, 19, CC, C])
    up0 = sb("up0", [P, 2, HID])
    up1a = sb("up1a", [P, 2, HID])
    up1b = sb("up1b", [P, 2, HID])
    l1 = sb("l1", [P, 2, HID])
    l2 = sb("l2", [P, 4, HID])
    l3 = sb("l3", [P, 4, HID])
    down3 = sb("down3", [P, 2, C])
    up3 = sb("up3", [P, 2, HID])
    downs = sb("downs", [P, 4, 4, KEEP])
    gate = sb("gate", [P, CC, 4])
    prefer = sb("prefer", [P, TT, 4])

    X = [sb(f"x{s}", [P, TT, C]) for s in range(STREAMS)]
    HB = [sb(f"h{s}", [P, TT, C]) for s in range(STREAMS)]
    HT = [sb(f"hT{s}", [P, CC, S]) for s in range(STREAMS)]
    T = [sb(f"t{s}", [P, TT, C]) for s in range(STREAMS)]
    QK = [sb(f"qk{s}", [P, 2, CC, S]) for s in range(STREAMS)]
    SP = [sb(f"split{s}", [P, 2, 3, CC * S], BF16) for s in range(STREAMS)]
    QS = [sb(f"qstack{s}", [ROWS + SHIFT, H, S], BF16) for s in range(STREAMS)]
    KS = [sb(f"kstack{s}", [ROWS + SHIFT, H, S], BF16) for s in range(STREAMS)]
    V = [sb(f"v{s}", [P, TT, H, 32]) for s in range(STREAMS)]
    GP = [sb(f"gp{s}", [P, TT, S]) for s in range(STREAMS)]
    NQ = [sb(f"nq{s}", [P, TT, S], BF16) for s in range(STREAMS)]
    NK = [sb(f"nk{s}", [P, TT, S], BF16) for s in range(STREAMS)]
    PR = sb("probs", [P, 5, 2, TT, S])
    HIDDEN = [[PR[:, 2 * s + k, :, :, :].rearrange("p a b c -> p (a b) c") for k in range(2)]
              for s in range(STREAMS)]
    m_u8 = [sb(f"m_u8{s}", [P, TT], U8) for s in range(STREAMS)]
    mr_u8 = [sb(f"mr_u8{s}", [1, S], U8) for s in range(STREAMS)]
    m_col = [sb(f"m_col{s}", [P, TT]) for s in range(STREAMS)]
    m_row = [sb(f"m_row{s}", [1, S], BF16) for s in range(STREAMS)]
    ST = [sb(f"st{s}", [P, TT, 6]) for s in range(STREAMS)]
    MV = [sb(f"mv{s}", [P, TT, 2]) for s in range(STREAMS)]
    VE = [sb(f"ve{s}", [P, TT]) for s in range(STREAMS)]
    RSTD = [sb(f"rstd{s}", [P, TT]) for s in range(STREAMS)]
    MX = [sb(f"mx{s}", [P, H, TT]) for s in range(STREAMS)]
    MB = [sb(f"max_parts{s}", [P, TT, SHIFT, H], BF16) for s in range(STREAMS)]
    MT = [sb(f"mT{s}", [SHIFT * H, S], BF16) for s in range(STREAMS)]
    RS = [sb(f"rs{s}", [P, TT, H]) for s in range(STREAMS)]
    GT = [sb(f"gt{s}", [P, 10, TT, 4]) for s in range(STREAMS)]
    GM = [sb(f"gmx{s}", [P, 6, TT]) for s in range(STREAMS)]

    SLOT = [ctx.enter_context(nc.psum_tensor(f"slot{i}", [P, 2, TT, S], F32)) for i in range(3)]
    BANK = [ctx.enter_context(nc.psum_tensor(f"bank{i}", [P, 2, S], F32)) for i in range(2)]

    bank_filled = signal("bank_filled")
    slot_filled = signal("slot_filled")
    mixed = signal("mixed")
    act_read = signal("act_read")
    dve_read = signal("dve_read")
    exped = signal("exped")
    maxed = signal("maxed")
    dve_step = signal("dve_step")
    act_step = signal("act_step")
    pool_step = signal("pool_step")
    dve_chain = signal("dve_chain")
    pool_chain = signal("pool_chain")
    x_in = [signal(f"x_in{s}", 16) for s in range(STREAMS)]
    mask_in = [signal(f"mask_in{s}", 16) for s in range(STREAMS)]
    ctx_in = [signal(f"ctx_in{s}", 16) for s in range(STREAMS)]
    stack_in = [signal(f"stack_in{s}", 16) for s in range(STREAMS)]
    shift_in = [signal(f"shift_in{s}", 16) for s in range(STREAMS)]
    x_out = signal("x_out", 16)
    setup_in = ctx.enter_context(nc.semaphore("setup_in"))
    setup_done = ctx.enter_context(nc.semaphore("setup_done"))
    arrived = ctx.enter_context(nc.semaphore("arrived"))
    rounds_ended = ctx.enter_context(nc.semaphore("rounds_ended"))
    released = ctx.enter_context(nc.semaphore("released"))

    COL = {n: i for i, n in enumerate(
        ["g1", "b1", "g2", "b2", "n1", "n2", "lw", "lb", "bqA", "bkA", "bqD", "bkD", "bqE", "bkE", "qn"])}
    GAIN = {1: ("g1", "b1"), 2: ("n1", None), 3: ("lw", "lb")}
    QB = {0: "bqA", 3: "bqD", 4: "bqE"}
    KB = {0: "bkA", 3: "bkD", 4: "bkE"}

    def col(name, c=0):
        i = 2 * COL[name] + c
        return cols[:, i:i + 1]

    VROW = {0: 0, 3: 2, 4: 4}
    OROW = {1: 1, 3: 3, 4: 5}
    wq = lambda l: 3 * l
    wk = lambda l: 3 * l + 1
    wv = lambda l: 3 * l + 2
    wo = lambda l: 14 + l

    SETUP = [(ident, "ident"), (rope_swap, "rope_swap"), (head_ones, "head_ones"), (rope_cos, "rope_cos"),
             (rope_sin, "rope_sin"), (cols, "cols"), (rows, "rows"), (proj, "proj"), (up0, "up0"),
             (up1a, "up1a"), (up1b, "up1b"), (l1, "l1"), (l2, "l2"), (l3, "l3"), (down3, "down3"),
             (up3, "up3"), (downs, "downs"), (gate, "gate"), (prefer, "prefer")]
    with nc.Block() as block:
        @block.sync
        def _(sp):
            for dst, name in SETUP:
                sp.dma_start(dst.ap(), t[name])\
                    .then_inc(setup_in, 16)
            sp.dma_start(X[0][:, 0, 0:P], t["causal_q"]).then_inc(setup_in, 16)
            sp.dma_start(X[0][:, 1, 0:P], t["causal_k"]).then_inc(setup_in, 16)
            sp.wait_ge(setup_in, 16 * (len(SETUP) + 2))

        @block.gpsimd
        def _(pool):
            pool.memset(neg_half[:, :], -0.5)
            pool.memset(eps_col[:, :], 1.1920929e-07)
            pool.memset(sum_cols[:, 0:D], 0.0)
            pool.memset(sum_cols[:, D:32], 1.0)

        @block.vector
        def _(dve):
            dve.wait_ge(setup_in, 16 * (len(SETUP) + 2))
            for s in range(STREAMS):
                dve.memset(KS[s][ROWS:ROWS + SHIFT, :, :], 1.0)
            dve.memset(ones_row[:, :], 1.0)
            dve.tensor_copy(ident_b[:, :], ident[:, :])
            dve.tensor_copy(causal_q[:, :], X[0][:, 0, 0:P])
            dve.tensor_copy(causal_k[:, :], X[0][:, 1, 0:P])
            for name in ("bqA", "bqD", "bqE", "qn"):
                dve.tensor_scalar(cols[:, 2 * COL[name]:2 * COL[name] + (1 if name == "qn" else 2)],
                                  cols[:, 2 * COL[name]:2 * COL[name] + (1 if name == "qn" else 2)],
                                  0.25, None, ALU.mult)

    block = ctx.enter_context(nc.Block())
    ROUNDS = B // STREAMS

    def finish(eng, i):
        eng.drain()
        eng.sem_inc(arrived, 1)
        eng.wait_ge(released, i + 1)

    last_in_bank = [None, None]
    bank_turn = [0]
    last_in_slot = [None, None, None]
    slot_turn = [0]
    READER = {"T": act_read, "TC": act_read, "q": act_read, "k": act_read, "v": dve_read, "q2": None, "k2": None,
              "neg": act_read, "o": dve_read, "y": dve_read, "yT": act_read, "w": dve_read,
              "Tf": act_read, "g": dve_read, "e0": act_read, "e1a": act_read, "e1b": dve_read, "e2a": act_read,
              "e2b": act_read, "e2c": act_read, "e3a": act_read, "e3b": act_read, "down": dve_read}

    def reader(label):
        kind, s, l = label[:3]
        if kind in ("q2", "k2"):
            return act_read if l == 2 else dve_read
        return READER[kind]

    @block.tensor
    def _(pe):
        def bank(*label):
            b = bank_turn[0] % 2
            bank_turn[0] += 1
            if last_in_bank[b] is not None:
                pe.wait_ge(*reader(last_in_bank[b]).at(*last_in_bank[b]))
            last_in_bank[b] = label
            known["bank", label] = b
            return BANK[b]

        def slot(phase, *label):
            k = slot_turn[0] % 3
            slot_turn[0] += 1
            if last_in_slot[k] is not None:
                was, lab = last_in_slot[k]
                pe.wait_ge(*(maxed if was == "max" else exped).at(*lab))
            last_in_slot[k] = (phase, label)
            known["slot", (phase, *label)] = k
            return SLOT[k]

        def transposes(label, src):
            ps = bank(*label)
            for c in range(CC):
                for tt in range(TT):
                    mm = pe.transpose(ps[:, c, tt * P:(tt + 1) * P], src[:, tt, c * P:(c + 1) * P], ident[:, :])
            mm.then_inc(*bank_filled(*label))

        def turn(s, l):
            if l == 0:
                pe.wait_ge(*x_in[s].at())
            elif l in SELF_LN:
                pe.wait_ge(*dve_step.at("h", s, l))
            else:
                pe.wait_ge(*dve_step.at("x", s, l))
            transposes(("T", s, l), HB[s] if l in SELF_LN else X[s])

        def turn_context(s, l):
            if l == 1:
                pe.wait_ge(*dve_step.at("hc", s, l))
            else:
                pe.wait_ge(*ctx_in[s].at(l))
            transposes(("TC", s, l), HB[s] if l == 1 else T[s])

        def project(s, l):
            pe.wait_ge(*act_read.at("T", s, l))
            src = HT[s]
            for kind, w in (("q", wq(l)), ("k", wk(l))):
                ps = bank(kind, s, l)
                if kind == "k" and l in (1, 4):
                    pe.wait_ge(*act_read.at("TC", s, l))
                    src = T[s]
                for co in range(CC):
                    for ci in range(CC):
                        mm = pe.matmul(ps[:, co, :], proj[:, w, ci, co * P:(co + 1) * P], src[:, ci, :],
                                       start=ci == 0, stop=ci == CC - 1)
                mm.then_inc(*bank_filled(kind, s, l))
            ps = bank("v", s, l)
            for tt in range(TT):
                for ci in range(CC):
                    mm = pe.matmul(ps[:, tt, :], src[:, ci, tt * P:(tt + 1) * P], proj[:, wv(l), ci, :],
                                   start=ci == 0, stop=ci == CC - 1)
            mm.then_inc(*bank_filled("v", s, l))

        def project_again(s, l):
            for n, kind in enumerate(("q", "k")):
                ps = bank(kind + "2", s, l)
                if l == 2:
                    pe.wait_ge(*pool_step.at("sq" + kind, s, l))
                    src = (HB, T)[n][s]
                    mm = pe.matmul(ps[:, :, :], head_ones[:, :], src[:, :, :], start=True, stop=True)
                else:
                    pe.wait_ge(*act_read.at(kind, s, l))
                    mm = pe.matmul(ps[:, :, :], rope_swap[:, :], QK[s][:, n, :, :], start=True, stop=True)
                mm.then_inc(*bank_filled(kind + "2", s, l))

        def scores_for_max(s, l, pairs):
            for p in pairs:
                ps = slot("max", s, l, p)
                if p == 0:
                    pe.wait_ge(*stack_in[s].at(l, "k", 5))
                for a in range(2):
                    h = 2 * p + a
                    for qt in range(TT):
                        n = (qt + 1) * P if l in CAUSAL else S
                        masked = l in CAUSAL or l in (1, 4)
                        mm = pe.matmul(ps[:, a, qt, 0:n], QS[s][0:ROWS, h, qt * P:(qt + 1) * P],
                                       KS[s][0:ROWS, h, 0:n], start=True, stop=not masked)
                        if l in CAUSAL:
                            mm = pe.matmul(ps[:, a, qt, qt * P:n], ident_b[:, :], causal_q[:, :],
                                           start=False, stop=True)
                        elif l == 1:
                            mm = pe.matmul(ps[:, a, qt, :], ones_row[:, :], m_row[s][:, :], start=False, stop=True)
                        elif l == 4:
                            mm = pe.matmul(ps[:, a, qt, :], ident_b[:, :], NQ[s][:, qt, :], start=False, stop=True)
                mm.then_inc(*slot_filled("max", s, l, p))

        def turn_maxima(s, l):
            ps = bank("neg", s, l)
            out = ps[:, 0, :].bitcast(BF16)
            pe.wait_ge(*dve_step.at("mb", s, l))
            for qt in range(TT):
                mm = pe.transpose(out[0:SHIFT * H, qt * P:(qt + 1) * P],
                                  MB[s][:, qt, :, :].rearrange("p a b -> p (a b)"), ident_b[:, :])
            mm.then_inc(*bank_filled("neg", s, l))

        def scores_for_exp(s, l, p):
            ps = slot("exp", s, l, p)
            if p == 0:
                pe.wait_ge(*shift_in[s].at(l))
            for a in range(2):
                h = 2 * p + a
                for kt in range(TT):
                    q0 = kt * P if l in CAUSAL else 0
                    masked = l in CAUSAL or l == 4
                    mm = pe.matmul(ps[:, a, kt, q0:S], KS[s][0:ROWS + SHIFT, h, kt * P:(kt + 1) * P],
                                   QS[s][0:ROWS + SHIFT, h, q0:S], start=True, stop=not masked)
                    if l in CAUSAL:
                        mm = pe.matmul(ps[:, a, kt, kt * P:(kt + 1) * P], ident_b[:, :], causal_k[:, :],
                                       start=False, stop=True)
                    elif l == 4:
                        mm = pe.matmul(ps[:, a, kt, :], ident_b[:, :], NK[s][:, kt, :], start=False, stop=True)
            mm.then_inc(*slot_filled("exp", s, l, p))

        def mix_values(s, l, p):
            if p % 2 == 0:
                mix_values.ps = bank("o", s, l, p // 2)
            ps = mix_values.ps
            if p == 0:
                pe.wait_ge(*dve_read.at("v", s, l))
            pe.wait_ge(*exped.at(s, l, p))
            if l == 4:
                pe.wait_ge(*dve_step.at("pg", s, l, p))
            k = p % 3
            for a in range(2):
                h = 2 * p + a
                row = 32 * (h % 4)
                out = ps[row:row + 32, 0, :]
                if l == 4:
                    for kt in range(TT):
                        pe.matmul(out, sum_cols[:, :], PR[:, k, a, kt, :], start=kt == 0, stop=False)
                    for kt in range(TT):
                        mm = pe.matmul(out, V[s][:, kt, h, :], PR[:, 3 + p % 2, a, kt, :], start=False,
                                       stop=kt == TT - 1)
                else:
                    for kt in range(TT):
                        q0 = kt * P if l in CAUSAL else 0
                        mm = pe.matmul(out[:, q0:S], V[s][:, kt, h, :], PR[:, k, a, kt, q0:S],
                                       start=kt == 0, stop=kt == TT - 1)
            if p % 2 == 0:
                mm.then_inc(*mixed(s, l, p))
            else:
                mm.then_inc(*bank_filled("o", s, l, p // 2))

        def turn_outputs(s, l):
            pe.wait_ge(*dve_read.at("o", s, l, PAIRS // 2 - 1))
            O = QK[s][:, :, :, :].rearrange("p a b c -> p (a b) c")
            for qt in range(TT):
                ps = bank("y", s, l, qt)
                for g in range(4):
                    mm = pe.transpose(ps[:, g // 2, (g % 2) * P:(g % 2 + 1) * P], O[:, g, qt * P:(qt + 1) * P],
                                      ident[:, :])
                mm.then_inc(*bank_filled("y", s, l, qt))

        def out_project(s, l):
            pe.wait_ge(*dve_read.at("y", s, l, TT - 1))
            transposes(("yT", s, l), HB[s])
            ps = bank("w", s, l)
            pe.wait_ge(*act_read.at("yT", s, l))
            for tt in range(TT):
                for ci in range(CC):
                    mm = pe.matmul(ps[:, tt, :], HT[s][:, ci, tt * P:(tt + 1) * P], proj[:, wo(l), ci, :],
                                   start=ci == 0, stop=ci == CC - 1)
            mm.then_inc(*bank_filled("w", s, l))

        def expert_up(kind, s, w, src, kc):
            for half in range(2):
                ps = bank(kind, s, 2, half)
                for j in range(2):
                    o = (2 * half + j) * P
                    for k in range(kc):
                        mm = pe.matmul(ps[:, j, :], w[:, k, o:o + P], src[:, k, :], start=k == 0, stop=k == kc - 1)
                mm.then_inc(*bank_filled(kind, s, 2, half))

        def expert_down(e, s, src):
            ps = bank("down", s, 2, e)
            for tt in range(TT):
                for k in range(4):
                    mm = pe.matmul(ps[:, tt, 0:KEEP], src[:, k, tt * P:(tt + 1) * P], downs[:, e, k, :],
                                   start=k == 0, stop=k == 3)
            mm.then_inc(*bank_filled("down", s, 2, e))

        def mixture():
            for s in range(STREAMS):
                pe.wait_ge(*dve_step.at("hf", s, 2))
                transposes(("Tf", s, 2), HB[s])
            for s in range(STREAMS):
                ps = bank("g", s, 2)
                pe.wait_ge(*act_read.at("Tf", s, 2))
                for tt in range(TT):
                    for ci in range(CC):
                        mm = pe.matmul(ps[:, tt, 0:4], HT[s][:, ci, tt * P:(tt + 1) * P], gate[:, ci, :],
                                       start=ci == 0, stop=ci == CC - 1)
                mm.then_inc(*bank_filled("g", s, 2))
            for s in range(STREAMS):
                expert_up("e0", s, up0, HT[s], 2)
            for s in range(STREAMS):
                pe.wait_ge(*act_read.at("e0", s, 2, 1))
                expert_down(0, s, HIDDEN[s][0])
                expert_up("e2a", s, l1, HT[s], 2)
            for s in range(STREAMS):
                pe.wait_ge(*act_read.at("e2a", s, 2, 1))
                expert_up("e2b", s, l2, HIDDEN[s][1], 4)
            for s in range(STREAMS):
                pe.wait_ge(*act_read.at("e2b", s, 2, 1))
                expert_up("e2c", s, l3, HIDDEN[s][0], 4)
            for s in range(STREAMS):
                pe.wait_ge(*act_read.at("e2c", s, 2, 1))
                expert_down(2, s, HIDDEN[s][1])
                ps = bank("e3a", s, 2)
                for j in range(2):
                    for k in range(2):
                        mm = pe.matmul(ps[:, j, :], down3[:, k, j * P:(j + 1) * P], HT[s][:, k, :],
                                       start=k == 0, stop=k == 1)
                mm.then_inc(*bank_filled("e3a", s, 2))
            for s in range(STREAMS):
                pe.wait_ge(*act_read.at("e3a", s, 2))
                expert_up("e3b", s, up3, HIDDEN[s][0], 2)
            for s in range(STREAMS):
                pe.wait_ge(*act_read.at("e3b", s, 2, 1))
                expert_down(3, s, HIDDEN[s][1])
                expert_up("e1a", s, up1a, HT[s], 2)
                expert_up("e1b", s, up1b, HT[s], 2)
            for s in range(STREAMS):
                pe.wait_ge(*dve_read.at("e1b", s, 2, 1))
                expert_down(1, s, HIDDEN[s][0])

        with pe.Fori(0, ROUNDS) as i:
            for l in range(LAYERS):
                for s in range(STREAMS):
                    turn(s, l)
                if l in (1, 4):
                    for s in range(STREAMS):
                        turn_context(s, l)
                for s in range(STREAMS):
                    project(s, l)
                if l in (2, 3):
                    for s in range(STREAMS):
                        project_again(s, l)
                if l == 4:
                    pe.wait_ge(*pool_step.at("nk", 1))
                if l == 1:
                    pe.wait_ge(*pool_step.at("m_row", 1))
                scores_for_max(0, l, range(PAIRS))
                scores_for_max(1, l, range(PAIRS // 2))
                turn_maxima(0, l)
                scores_for_max(1, l, range(PAIRS // 2, PAIRS))
                for s in range(STREAMS):
                    for p in range(PAIRS):
                        scores_for_exp(s, l, p)
                        if s == 0 and p == 3:
                            turn_maxima(1, l)
                        if p >= 2:
                            mix_values(s, l, p - 2)
                    mix_values(s, l, PAIRS - 2)
                    mix_values(s, l, PAIRS - 1)
                for s in range(STREAMS):
                    turn_outputs(s, l)
                if l > 0:
                    for s in range(STREAMS):
                        out_project(s, l)
                if l == 2:
                    mixture()
            finish(pe, i)

    def bank_of(*label):
        return BANK[known.get(("bank", label), 0)]

    def slot_of(*label):
        return SLOT[known.get(("slot", label), 0)]

    @block.scalar
    def _(act):
        def read_turned(kind, s, l, dst, names):
            act.wait_ge(*bank_filled.at(kind, s, l))
            ps = bank_of(kind, s, l)
            if names is None:
                act.activation(dst[:, :, :], ps[:, :, :], ACT.Copy).then_inc(*act_read(kind, s, l))
                return
            gain, bias = names
            for c in range(CC):
                a = act.activation(dst[:, c, :], ps[:, c, :], ACT.Identity, scale=col(gain, c),
                                   bias=col(bias, c) if bias else 0.0)
            a.then_inc(*act_read(kind, s, l))

        def read_projected(s, l):
            for n, kind in enumerate(("q", "k")):
                act.wait_ge(*bank_filled.at(kind, s, l))
                if kind == "q" and l == 0:
                    act.wait_ge(*pool_step.at("nk", s))
                ps = bank_of(kind, s, l)
                scale = 0.25 if kind == "q" and l != 2 else 1.0
                bias = (QB, KB)[n].get(l)
                if bias is None:
                    a = act.activation(QK[s][:, n, :, :], ps[:, :, :], ACT.Copy, scale=scale)
                else:
                    for c in range(CC):
                        a = act.activation(QK[s][:, n, c, :], ps[:, c, :], ACT.Identity, bias=col(bias, c),
                                           scale=scale)
                a.then_inc(*act_read(kind, s, l))

        def root_squares(s, l):
            for n, kind in enumerate(("q", "k")):
                act.wait_ge(*bank_filled.at(kind + "2", s, l))
                act.activation((HB, T)[n][s][:, :, :], bank_of(kind + "2", s, l)[:, :, :], ACT.Sqrt,
                               bias=eps_col[:, :], scale=1.0 / D).then_inc(*act_read(kind + "2", s, l))

        def read_maxima(s, l):
            act.wait_ge(*bank_filled.at("neg", s, l))
            src = bank_of("neg", s, l)[:, 0, :].bitcast(BF16)[0:SHIFT * H, 0:S]
            act.activation(MT[s][:, :], src, ACT.Copy).then_inc(*act_read("neg", s, l))

        def exponentials(s, l, p):
            if p >= 3:
                q = p - 3
                act.wait_ge(*(mixed.at(s, l, q) if q % 2 == 0 else bank_filled.at("o", s, l, q // 2)))
            elif s or l:
                s0, l0 = (0, l) if s else (1, l - 1)
                q = (7, 7, 7)[p]
                act.wait_ge(*bank_filled.at("o", s0, l0, q // 2))
            act.wait_ge(*slot_filled.at("exp", s, l, p))
            ps = slot_of("exp", s, l, p)
            dst = PR[:, p % 3, :, :, :]
            if l in CAUSAL or l == 1:
                for kt in range(TT):
                    q0 = kt * P if l in CAUSAL else 0
                    a = act.activation(dst[:, :, kt, q0:S], ps[:, :, kt, q0:S], ACT.Exp,
                                       bias=m_col[s][:, kt:kt + 1] if l == 1 else 0.0)
            else:
                a = act.activation(dst, ps[:, :, :, :], ACT.Exp)
            a.then_inc(*exped(s, l, p))

        def hidden(kind, s, dst, func, halves=2):
            for half in range(halves):
                label = (kind, s, 2, half) if halves == 2 else (kind, s, 2)
                act.wait_ge(*bank_filled.at(*label))
                act.activation(dst[:, 2 * half:2 * half + 2, :], bank_of(*label)[:, :, :], func)\
                   .then_inc(*act_read(*label))

        def mixture():
            for s in range(STREAMS):
                read_turned("Tf", s, 2, HT[s], ("n2", None))
            for s in range(STREAMS):
                act.wait_ge(*dve_step.at("gate_sub", s))
                act.activation(GT[s][:, 1, :, :], GT[s][:, 0, :, :], ACT.Exp).then_inc(*act_step("gate_exp", s))
            for s in range(STREAMS):
                hidden("e0", s, HIDDEN[s][0], ACT.Gelu)
            for s in range(STREAMS):
                hidden("e2a", s, HIDDEN[s][1], ACT.Gelu)
            for s in range(STREAMS):
                hidden("e2b", s, HIDDEN[s][0], ACT.Gelu)
            for s in range(STREAMS):
                hidden("e2c", s, HIDDEN[s][1], ACT.Gelu)
            for s in range(STREAMS):
                hidden("e3a", s, HIDDEN[s][0], ACT.Gelu, 1)
            for s in range(STREAMS):
                hidden("e3b", s, HIDDEN[s][1], ACT.Gelu)
            for s in range(STREAMS):
                hidden("e1a", s, HIDDEN[s][0], ACT.Silu)

        with act.Fori(0, ROUNDS) as i:
            for l in range(LAYERS):
                for s in range(STREAMS):
                    read_turned("T", s, l, HT[s], GAIN.get(l))
                if l in (1, 4):
                    for s in range(STREAMS):
                        read_turned("TC", s, l, T[s], ("g2", "b2") if l == 1 else None)
                for s in range(STREAMS):
                    read_projected(s, l)
                if l == 2:
                    for s in range(STREAMS):
                        root_squares(s, l)
                read_maxima(0, l)
                for s in range(STREAMS):
                    for p in range(PAIRS):
                        exponentials(s, l, p)
                        if s == 0 and p == 3:
                            read_maxima(1, l)
                if l > 0:
                    for s in range(STREAMS):
                        read_turned("yT", s, l, HT[s], None)
                if l == 2:
                    mixture()
            finish(act, i)

    @block.vector
    def _(dve):
        def then(ins):
            ins.then_inc(*dve_chain())
            dve.wait_ge(dve_chain.sem, dve_chain.count)

        def statistics(tag, s, l, src, mean_square):
            for tt in range(TT):
                a = dve.bn_stats(ST[s][:, tt, :], src[:, tt, :])
            then(a)
            for tt in range(TT):
                a = dve.bn_aggr(MV[s][:, tt, :], ST[s][:, tt, :])
            if mean_square:
                then(a)
                then(dve.tensor_tensor(VE[s][:, :], MV[s][:, :, 0], MV[s][:, :, 0], ALU.mult))
                a = dve.tensor_tensor(MV[s][:, :, 1], VE[s][:, :], MV[s][:, :, 1], ALU.add)
            a.then_inc(*dve_step("stat" + tag, s, l))

        def normalise(tag, s, l, src, dst, centre, out, shift=0):
            dve.wait_ge(*pool_step.at("rstd" + tag, s, l))
            for tt in range(TT):
                if centre:
                    a = dve.tensor_scalar(dst[:, tt, :], src[:, tt, :], MV[s][:, tt, 0:1], RSTD[s][:, tt:tt + 1],
                                          ALU.subtract, ALU.mult)
                else:
                    a = dve.tensor_scalar(dst[:, tt, :], src[:, tt, :], RSTD[s][:, tt:tt + 1], None, ALU.mult)
            a.then_inc(*dve_step(out, s, l + shift))

        def read_values(s, l):
            dve.wait_ge(*bank_filled.at("v", s, l))
            ps = bank_of("v", s, l)
            if l == 0:
                dve.wait_ge(*pool_step.at("v_ones", s))
            if l == 4:
                dve.wait_ge(*pool_step.at("v_zeros", s))
            for tt in range(TT):
                src = ps[:, tt, :].rearrange("p (h d) -> p h d", d=D)
                if l in VROW:
                    a = dve.tensor_tensor(V[s][:, tt, :, 0:D], src,
                                          rows[:, VROW[l], :].rearrange("p (h d) -> p h d", d=D), ALU.add)
                else:
                    a = dve.tensor_copy(V[s][:, tt, :, 0:D], src)
            a.then_inc(*dve_read("v", s, l))

        def rotate(s, l):
            for n, kind in enumerate(("q", "k")):
                dve.wait_ge(*bank_filled.at(kind + "2", s, l))
                sin = rope_sin[:, :].unsqueeze(1).to_broadcast([P, CC, S])
                a = dve.tensor_tensor((HB, T)[n][s][:, :, :], bank_of(kind + "2", s, l)[:, :, :], sin, ALU.mult)
                a.then_inc(*dve_read(kind + "2", s, l))
            for n, kind in enumerate(("q", "k")):
                dve.wait_ge(*dve_read.at(kind + "2", s, l))
                dve.wait_ge(*pool_step.at("cos" + kind, s, l))
                then(dve.tensor_tensor(QK[s][:, n, :, :], QK[s][:, n, :, :], (HB, T)[n][s][:, :, :], ALU.add))

        def normalise_heads(s, l):
            for n, kind in enumerate(("q", "k")):
                r = (HB, T)[n][s]
                dve.wait_ge(*act_read.at(kind + "2", s, l))
                then(dve.reciprocal(r[:, :, :], r[:, :, :]))
                then(dve.scalar_tensor_tensor(out=QK[s][:, n, :, :], in0=QK[s][:, n, :, :], scalar=col("qn", n),
                                              in1=r[:, :, :], op0=ALU.mult, op1=ALU.mult))

        def split(s, l):
            for n, kind in enumerate(("q", "k")):
                if l in (0, 1, 4):
                    dve.wait_ge(*act_read.at(kind, s, l))
                full = QK[s][:, n, :, :].rearrange("p a b -> p (a b)")
                part = [SP[s][:, n, j, :] for j in range(3)]
                then(dve.tensor_copy(part[0], full))
                then(dve.tensor_tensor(full, full, part[0], ALU.subtract))
                then(dve.tensor_copy(part[1], full))
                dve.tensor_tensor(part[2], full, part[1], ALU.subtract).then_inc(*dve_step("split" + kind, s, l))

        def maxima(s, l):
            for p in range(PAIRS):
                dve.wait_ge(*slot_filled.at("max", s, l, p))
                ps = slot_of("max", s, l, p)
                if l in CAUSAL:
                    for qt in range(TT):
                        a = dve.tensor_reduce(MX[s][:, 2 * p:2 * p + 2, qt], ps[:, :, qt, 0:(qt + 1) * P], AX.X, ALU.max)
                else:
                    a = dve.tensor_reduce(MX[s][:, 2 * p:2 * p + 2, :], ps[:, :, :, :], AX.X, ALU.max)
                a.then_inc(*maxed(s, l, p))
            m = MX[s][:, :, :]
            mv = MX[s][:, :, :].rearrange("p h q -> p q h")
            dve.wait_ge(*maxed.at(s, l, PAIRS - 1))
            then(dve.tensor_scalar(m, m, -1.0, None, ALU.mult))
            then(dve.tensor_copy(MB[s][:, :, 0, :], mv))
            then(dve.tensor_tensor(mv, mv, MB[s][:, :, 0, :], ALU.subtract))
            then(dve.tensor_copy(MB[s][:, :, 1, :], mv))
            dve.tensor_tensor(MB[s][:, :, 2, :], mv, MB[s][:, :, 1, :], ALU.subtract).then_inc(*dve_step("mb", s, l))

        def weigh(s, l, p):
            dve.wait_ge(*exped.at(s, l, p))
            if p >= 2:
                q = p - 2
                dve.wait_ge(*(mixed.at(s, l, q) if q % 2 == 0 else bank_filled.at("o", s, l, q // 2)))
            elif s:
                dve.wait_ge(*bank_filled.at("o", 0, l, PAIRS // 2 - 1))
            for a in range(2):
                ins = dve.tensor_tensor(PR[:, 3 + p % 2, a, :, :], PR[:, p % 3, a, :, :], GP[s][:, :, :], ALU.mult)
            ins.then_inc(*dve_step("pg", s, l, p))

        def read_mixed(s, l, g):
            dve.wait_ge(*bank_filled.at("o", s, l, g))
            O = QK[s][:, :, :, :].rearrange("p a b c -> p (a b) c")
            dve.tensor_copy(O[:, g, :], bank_of("o", s, l, g)[:, 0, :]).then_inc(*dve_read("o", s, l, g))

        def outputs(s, l):
            for qt in range(TT):
                dve.wait_ge(*bank_filled.at("y", s, l, qt))
                ps = bank_of("y", s, l, qt)[:, :, :].rearrange("p a (b e) -> p (a b) e", e=32)
                then(dve.reciprocal(RS[s][:, qt, :].unsqueeze(2), ps[:, :, D:D + 1]))
                dst = HB[s][:, qt, :].rearrange("p (h d) -> p h d", d=D)
                dve.tensor_tensor(dst, ps[:, :, 0:D], RS[s][:, qt, :].unsqueeze(2).to_broadcast([P, H, D]), ALU.mult)\
                   .then_inc(*dve_read("y", s, l, qt))

        def residual(s, l):
            t_, x_ = T[s][:, :, :], X[s][:, :, :]
            if l == 0:
                dve.wait_ge(*dve_read.at("y", s, l, TT - 1))
                then(dve.tensor_tensor(t_, x_, HB[s][:, :, :], ALU.add))
                return
            dve.wait_ge(*bank_filled.at("w", s, l))
            ps = bank_of("w", s, l)
            if l == 2:
                dve.tensor_copy(T[s][:, :, 0:SKIP], X[s][:, :, 0:SKIP])
                dve.tensor_tensor(T[s][:, :, SKIP:C], ps[:, :, SKIP:C], X[s][:, :, SKIP:C], ALU.add)\
                   .then_inc(*dve_read("w", s, l))
            else:
                dve.wait_ge(*pool_step.at("xb", s, l))
                dve.tensor_tensor(t_, ps[:, :, :], x_, ALU.add).then_inc(*dve_read("w", s, l))
            dve.wait_ge(*dve_read.at("w", s, l))

        def routing(s):
            g = lambda k: GT[s][:, k, :, :]
            m = lambda k: GM[s][:, k, :]
            wide = lambda k: GM[s][:, k, :].unsqueeze(2).to_broadcast([P, TT, 4])
            dve.wait_ge(*bank_filled.at("g", s, 2))
            dve.tensor_scalar(g(2), bank_of("g", s, 2)[:, :, 0:4], 3.4028235e38, -3.4028235e38, ALU.min, ALU.max)\
               .then_inc(*dve_read("g", s, 2))
            dve.wait_ge(*dve_read.at("g", s, 2))
            then(dve.tensor_reduce(m(0), g(2), AX.X, ALU.max))
            dve.tensor_tensor(g(0), g(2), wide(0), ALU.subtract).then_inc(*dve_step("gate_sub", s))
            then(dve.tensor_tensor(g(3), g(2), wide(0), ALU.is_equal))
            then(dve.tensor_tensor(g(3), g(3), prefer[:, :, :], ALU.mult))
            then(dve.tensor_reduce(m(1), g(3), AX.X, ALU.max))
            then(dve.tensor_tensor(g(4), prefer[:, :, :], wide(1), ALU.is_equal))
            then(dve.tensor_scalar(g(5), g(4), -3.4028235e38, None, ALU.mult))
            then(dve.tensor_tensor(g(5), g(0), g(5), ALU.add))
            then(dve.tensor_reduce(m(2), g(5), AX.X, ALU.max))
            then(dve.tensor_tensor(g(6), g(5), wide(2), ALU.is_equal))
            then(dve.tensor_tensor(g(6), g(6), prefer[:, :, :], ALU.mult))
            then(dve.tensor_reduce(m(3), g(6), AX.X, ALU.max))
            then(dve.tensor_tensor(g(7), prefer[:, :, :], wide(3), ALU.is_equal))
            then(dve.tensor_tensor(g(7), g(7), g(4), ALU.add))
            dve.wait_ge(*act_step.at("gate_exp", s))
            then(dve.tensor_reduce(m(4), g(1), AX.X, ALU.add))
            then(dve.reciprocal(m(4), m(4)))
            then(dve.tensor_tensor(g(8), g(1), wide(4), ALU.mult))
            then(dve.tensor_tensor(g(8), g(8), g(7), ALU.mult))
            then(dve.tensor_reduce(m(5), g(8), AX.X, ALU.add))
            then(dve.tensor_scalar(m(5), m(5), 1e-8, None, ALU.add))
            then(dve.reciprocal(m(5), m(5)))
            then(dve.tensor_tensor(g(9), g(8), wide(5), ALU.mult))

        def add_expert(s, e, first):
            dve.wait_ge(*bank_filled.at("down", s, 2, e))
            ps = bank_of("down", s, 2, e)
            for tt in range(TT):
                acc = HB[s][:, tt, SKIP:C]
                w = GT[s][:, 9, tt, e:e + 1]
                if first:
                    a = dve.tensor_scalar(acc, ps[:, tt, 0:KEEP], w, None, ALU.mult)
                else:
                    a = dve.scalar_tensor_tensor(out=acc, in0=ps[:, tt, 0:KEEP], scalar=w, in1=acc,
                                                 op0=ALU.mult, op1=ALU.add)
            a.then_inc(*dve_read("down", s, 2, e))
            dve.wait_ge(*dve_read.at("down", s, 2, e))

        def mixture():
            for s in range(STREAMS):
                statistics("f", s, 2, T[s], True)
            for s in range(STREAMS):
                normalise("f", s, 2, T[s], HB[s], False, "hf")
            for s in range(STREAMS):
                routing(s)
            for s in range(STREAMS):
                dve.wait_ge(*bank_filled.at("Tf", s, 2))
                add_expert(s, 0, True)
            for s in range(STREAMS):
                add_expert(s, 2, False)
            for s in range(STREAMS):
                add_expert(s, 3, False)
                for half in range(2):
                    dve.wait_ge(*bank_filled.at("e1b", s, 2, half))
                    dve.wait_ge(*act_read.at("e1a", s, 2, half))
                    hid = HIDDEN[s][0][:, 2 * half:2 * half + 2, :]
                    dve.tensor_tensor(hid, bank_of("e1b", s, 2, half)[:, :, :], hid, ALU.mult)\
                       .then_inc(*dve_read("e1b", s, 2, half))
            for s in range(STREAMS):
                add_expert(s, 1, False)
            for s in range(STREAMS):
                then(dve.tensor_tensor(T[s][:, :, SKIP:C], T[s][:, :, SKIP:C], HB[s][:, :, SKIP:C], ALU.add))
                then(dve.tensor_tensor(T[s][:, :, :], T[s][:, :, :], X[s][:, :, :], ALU.add))

        with dve.Fori(0, ROUNDS) as i:
            for l in range(LAYERS):
                if l in SELF_LN:
                    for s in range(STREAMS):
                        dve.wait_ge(*dve_step.at("x", s, l))
                        statistics("h", s, l, X[s], l == 2)
                    for s in range(STREAMS):
                        normalise("h", s, l, X[s], HB[s], l != 2, "h")
                if l == 1:
                    for s in range(STREAMS):
                        dve.wait_ge(*ctx_in[s].at(l))
                        statistics("c", s, l, T[s], False)
                    for s in range(STREAMS):
                        dve.wait_ge(*bank_filled.at("T", s, l))
                        normalise("c", s, l, T[s], HB[s], True, "hc")
                for s in range(STREAMS):
                    read_values(s, l)
                    if l in (0, 1, 4):
                        split(s, l)
                if l in (2, 3):
                    for s in range(STREAMS):
                        (normalise_heads if l == 2 else rotate)(s, l)
                        split(s, l)
                for s in range(STREAMS):
                    maxima(s, l)
                for s in range(STREAMS):
                    for p in range(PAIRS):
                        if l == 4:
                            weigh(s, l, p)
                        if p % 2 == 1 and p >= 3:
                            read_mixed(s, l, (p - 3) // 2)
                    read_mixed(s, l, PAIRS // 2 - 1)
                for s in range(STREAMS):
                    outputs(s, l)
                for s in range(STREAMS):
                    residual(s, l)
                if l == 2:
                    mixture()
                for s in range(STREAMS):
                    statistics("x", s, l, T[s], False)
                for s in range(STREAMS):
                    normalise("x", s, l, T[s], X[s], True, "x", 1)
            finish(dve, i)

    @block.gpsimd
    def _(pool):
        def then(ins):
            ins.then_inc(*pool_chain())
            pool.wait_ge(pool_chain.sem, pool_chain.count)

        def inverse_root(tag, s, l, eps):
            pool.wait_ge(*dve_step.at("stat" + tag, s, l))
            then(pool.tensor_scalar(VE[s][:, :], MV[s][:, :, 1], eps, None, ALU.add))
            pool.tensor_tensor(RSTD[s][:, :], VE[s][:, :], neg_half[:, :], ALU.pow)\
                .then_inc(*pool_step("rstd" + tag, s, l))

        with pool.Fori(0, ROUNDS) as i:
            for s in range(STREAMS):
                pool.memset(V[s][:, :, :, D:32], 1.0).then_inc(*pool_step("v_ones", s))
                pool.wait_ge(*mask_in[s].at("all"))
                for dst, src in ((NQ[s], QK[s][:, 0, :, :]), (NK[s], QK[s][:, 1, :, :])):
                    a = pool.tensor_scalar(dst[:, :, :], src.bitcast(I32), 1.0e9, -1.0e9, ALU.mult, ALU.add)
                a.then_inc(*pool_step("nk", s))
                then(pool.tensor_scalar(m_col[s][:, :], m_u8[s][:, :], -LOW, LOW, ALU.mult, ALU.add))
                pool.tensor_scalar(m_row[s][:, :], mr_u8[s][:, :], -LOW, LOW, ALU.mult, ALU.add)\
                    .then_inc(*pool_step("m_row", s))
                pool.wait_ge(*pool_step.at("m_row", s))
            for l in range(LAYERS):
                if l in SELF_LN:
                    for s in range(STREAMS):
                        inverse_root("h", s, l, 1.1920929e-07 if l == 2 else 1e-5)
                if l == 1:
                    for s in range(STREAMS):
                        inverse_root("c", s, l, 1e-5)
                if l == 4:
                    for s in range(STREAMS):
                        pool.wait_ge(*bank_filled.at("o", s, 3, PAIRS // 2 - 1))
                        pool.memset(V[s][:, :, :, D:32], 0.0).then_inc(*pool_step("v_zeros", s))
                if l in (2, 3):
                    for s in range(STREAMS):
                        for n, kind in enumerate(("q", "k")):
                            qk = QK[s][:, n, :, :]
                            pool.wait_ge(*act_read.at(kind, s, l))
                            if l == 2:
                                pool.wait_ge(*bank_filled.at("T", s, l))
                                pool.tensor_tensor((HB, T)[n][s][:, :, :], qk, qk, ALU.mult)\
                                    .then_inc(*pool_step("sq" + kind, s, l))
                            else:
                                pool.wait_ge(*bank_filled.at(kind + "2", s, l))
                                pool.tensor_tensor(qk, qk, rope_cos[:, :].unsqueeze(1).to_broadcast([P, CC, S]),
                                                   ALU.mult).then_inc(*pool_step("cos" + kind, s, l))
                if l in OROW:
                    for s in range(STREAMS):
                        pool.wait_ge(*dve_step.at("x", s, l))
                        pool.wait_ge(*bank_filled.at("k", s, l))
                        x_ = X[s][:, :, :]
                        if l == 3:
                            then(pool.tensor_tensor(x_, x_, x_, ALU.add))
                        b_ = rows[:, OROW[l], :].unsqueeze(1).to_broadcast([P, TT, C])
                        pool.tensor_tensor(x_, x_, b_, ALU.add).then_inc(*pool_step("xb", s, l))
                if l == 2:
                    for s in range(STREAMS):
                        inverse_root("f", s, l, 1.1920929e-07)
                for s in range(STREAMS):
                    inverse_root("x", s, l, 1e-5)
            finish(pool, i)

    @block.sync
    def _(sp):
        def stack(s, l):
            for n, (kind, parts, dst) in enumerate((("q", Q_PARTS, QS), ("k", K_PARTS, KS))):
                sp.wait_ge(*dve_step.at("split" + kind, s, l))
                for j, part in enumerate(parts):
                    sp.dma_start(dst[s][D * j:D * (j + 1), :, :], SP[s][:, n, part, :])\
                        .then_inc(*stack_in[s](l, kind, j))

        def shift(s, l):
            sp.wait_ge(*act_read.at("neg", s, l))
            sp.dma_start(QS[s][ROWS:ROWS + SHIFT, :, :], MT[s][:, :]).then_inc(*shift_in[s](l))

        def context(s, l, i):
            sp.wait_ge(*dve_step.at("x", s, l))
            sp.dma_start(T[s][:, :, :], t["ctx"][bass.ds(2 * i + s, 1)].rearrange("b p t c -> (b p) t c"))\
                .then_inc(*ctx_in[s](l))

        with sp.Fori(0, ROUNDS) as i:
            for s in range(STREAMS):
                at = bass.ds(2 * i + s, 1)
                sp.dma_start(X[s][:, :, :], t["x"][at].rearrange("b p t c -> (b p) t c")).then_inc(*x_in[s]())
            for s in range(STREAMS):
                at = bass.ds(2 * i + s, 1)
                flat = "b p t c -> (b p) t c"
                sp.dma_start(QK[s][:, 0, :, :].bitcast(I32), t["mask"][at].rearrange(flat)).then_inc(*mask_in[s]("q"))
                sp.dma_start(QK[s][:, 1, :, :].bitcast(I32), t["maskT"][at].rearrange(flat)).then_inc(*mask_in[s]("k"))
                sp.dma_start(GP[s][:, :, :], t["gpT"][at].rearrange(flat)).then_inc(*mask_in[s]("g"))
                sp.dma_start(m_u8[s][:, :], t["m_cols"][at].rearrange("b p t -> (b p) t")).then_inc(*mask_in[s]("c"))
                sp.dma_start(mr_u8[s][:, :], t["m_rows"][at].rearrange("b o t -> (b o) t"))\
                    .then_inc(*mask_in[s]("all"))
            for l in range(LAYERS):
                if l in (1, 4):
                    for s in range(STREAMS):
                        context(s, l, i)
                for s in range(STREAMS):
                    stack(s, l)
                for s in range(STREAMS):
                    shift(s, l)
            for s in range(STREAMS):
                sp.wait_ge(*dve_step.at("x", s, LAYERS))
                rows_out = x5_dram.rearrange("(b t p) c -> b p t c", t=TT, p=P)[bass.ds(2 * i + s, 1)]
                sp.dma_start(rows_out.rearrange("b p t c -> (b p) t c"), X[s][:, :, :]).then_inc(*x_out(s))
            sp.wait_ge(*x_out.at(1))
            sp.wait_ge(arrived, 4 * i + 4)
            sp.sem_inc(rounds_ended, 1)
            for sem in work:
                sp.sem_clear(sem)
            sp.sem_inc(released, 1)


def routed_mixture(nc, ctx, t, known, x5_dram, slots_dram, expert_dram):
    def sb(name, shape, dt=F32):
        return ctx.enter_context(nc.sbuf_tensor(name, shape, dt))

    def signal(name, step=1):
        return Signal(name, ctx.enter_context(nc.semaphore(name)), known, step)

    G = B * S // P
    SLOTS = E1 * CAP
    ST = SLOTS // P
    CH = [(0, P), (P, P), (2 * P, CAP - 2 * P)]
    FC = DFF // P

    x5 = sb("x5", [P, G, C])
    xt = sb("xt", [P, 2, CC, P])
    ident = sb("ident2", [P, P])
    upto = sb("upto", [P, P])
    upto_b = sb("upto_b", [P, P], BF16)
    ones_b = sb("ones_b", [P, P], BF16)
    wg = sb("wg", [P, CC, E1])
    prefer = sb("prefer8", [P, G, E1])
    zero = sb("zero", [P, C])
    lg = sb("lg", [P, 5, G, E1])
    oh = sb("oh", [P, G, E1], BF16)
    run = sb("run", [P, 2, G, E1])
    tot = sb("tot", [P, G, E1])
    red = sb("red", [P, 8, G])
    idx = sb("idx", [P, G], U32)
    w1 = [sb(f"w1_{k}", [P, CC, DFF]) for k in range(2)]
    w2 = [sb(f"w2_{k}", [P, FC, C]) for k in range(2)]
    b1 = sb("b1", [P, E1, FC])
    b2 = sb("b2", [P, E1, C])
    rows = sb("slot_rows_sb", [P, ST, C])
    xs = sb("xs", [P, CC, SLOTS])
    hid = [sb(f"hid{k}", [P, FC, CAP]) for k in range(2)]
    eo = sb("eo", [P, 3, C])
    back = sb("back", [P, G, C])
    st = sb("st2", [P, G, 6])
    mv = sb("mv2", [P, G, 2])
    ve = sb("ve2", [P, G])
    rstd = sb("rstd2", [P, G])
    half = sb("neg_half2", [P, G])
    BANK = [ctx.enter_context(nc.psum_tensor(f"pbank{i}", [P, 512], F32)) for i in range(8)]

    x_in = signal("x5_in", 16)
    const_in = signal("const_in", 16)
    cleared = signal("slots_cleared", 16)
    scattered = signal("scattered", 16)
    slots_in = [signal(f"slots_in{k}", 16) for k in range(4)]
    w_in = [signal(f"w_in{k}", 16) for k in range(2)]
    expert_out = [signal(f"expert_out{k}", 16) for k in range(3)]
    gathered = signal("gathered", 16)
    written = signal("written", 16)
    pe_turned = signal("pe_turned")
    pe_logits = signal("pe_logits")
    pe_counts = signal("pe_counts")
    pe_rows = signal("pe_rows")
    pe_up = signal("pe_up")
    pe_down = signal("pe_down")
    act_turned = signal("act_turned")
    act_exp = signal("act_exp")
    act_rows = signal("act_rows")
    act_up = signal("act_up")
    dve_chain = signal("dve_chain2")
    dve_done = signal("dve_done")
    dve_down = signal("dve_down")
    dve_out = signal("dve_out")
    pool_done = signal("pool_done")
    pool_chain = signal("pool_chain2")

    block = ctx.enter_context(nc.Block())
    UPS = [BANK[k] for k in range(2, 5)]
    DOWNS = [BANK[k] for k in range(5, 8)]

    @block.sync
    def _(sp):
        xv = x5_dram.rearrange("(g p) c -> p g c", p=P)
        for k in range(4):
            sp.dma_start(x5[:, 4 * k:4 * k + 4, :], xv[:, 4 * k:4 * k + 4, :]).then_inc(*x_in(k))
        for dst, name in ((ident, "ident"), (upto, "upto"), (wg, "wg"), (prefer, "prefer8"), (b1, "b1"), (b2, "b2")):
            sp.dma_start(dst.ap(), t[name]).then_inc(*const_in(name))

        def weights(e):
            if e >= 2:
                sp.wait_ge(*pe_down.at(e - 2, 2))
            sp.dma_start(w1[e % 2][:, :, :], t["w1"][e]).then_inc(*w_in[e % 2](e, 1))
            sp.dma_start(w2[e % 2][:, :, :], t["w2"][e]).then_inc(*w_in[e % 2](e, 2))

        weights(0)
        weights(1)
        sp.wait_ge(*scattered.at(G - 1))
        sv = slots_dram.rearrange("(n p) c -> p n c", p=P)
        for k in range(4):
            sp.dma_start(rows[:, 5 * k:5 * k + 5, :], sv[:, 5 * k:5 * k + 5, :]).then_inc(*slots_in[k]("in"))
        for e in range(E1):
            for j, (c0, m) in enumerate(CH):
                sp.wait_ge(*dve_down.at(e, j))
                sp.dma_start(expert_dram[e * CAP + c0:e * CAP + c0 + m, :], eo[0:m, j, :])\
                    .then_inc(*expert_out[j](e))
            if e + 2 < E1:
                weights(e + 2)
        for g in range(G):
            sp.wait_ge(*dve_out.at(g))
            sp.dma_start(t["out"].rearrange("(g p) c -> g p c", p=P)[g], back[:, g, :]).then_inc(*written(g))
        sp.wait_ge(*written.at(G - 1))

    def logits(pe, g):
        pe.wait_ge(*act_turned.at(g))
        for ci in range(CC):
            mm = pe.matmul(BANK[2][:, g * E1:(g + 1) * E1], xt[:, g % 2, ci, :], wg[:, ci, :],
                           start=ci == 0, stop=ci == CC - 1)
        mm.then_inc(*pe_logits(g))

    @block.tensor
    def _(pe):
        pe.wait_ge(*const_in.at("b2"))
        for g in range(G):
            pe.wait_ge(*x_in.at(3))
            if g >= 2:
                pe.wait_ge(*act_turned.at(g - 2))
            for c in range(CC):
                mm = pe.transpose(BANK[g % 2][:, c * P:(c + 1) * P], x5[:, g, c * P:(c + 1) * P], ident[:, :])
            mm.then_inc(*pe_turned(g))
            if g >= 1:
                logits(pe, g - 1)
        logits(pe, G - 1)
        pe.wait_ge(*dve_done.at("onehot"))
        flat = oh[:, :, :].rearrange("p g e -> p (g e)")
        pe.matmul(BANK[3][:, 0:P], upto_b[:, :], flat, start=True, stop=True)
        pe.matmul(BANK[4][:, 0:P], ones_b[:, :], flat, start=True, stop=True).then_inc(*pe_counts("all"))
        for n in range(ST // 2):
            pe.wait_ge(*slots_in[(2 * n) // 5].at("in"))
            pe.wait_ge(*slots_in[(2 * n + 1) // 5].at("in"))
            if n >= 2:
                pe.wait_ge(*act_rows.at(n - 2))
            for c in range(CC):
                for k in range(2):
                    mm = pe.transpose(BANK[n % 2][:, (2 * c + k) * P:(2 * c + k + 1) * P],
                                      rows[:, 2 * n + k, c * P:(c + 1) * P], ident[:, :])
            mm.then_inc(*pe_rows(n))
        ups = 0
        for e in range(E1):
            pe.wait_ge(*act_rows.at(min(ST // 2 - 1, ((e + 1) * CAP - 1) // (2 * P))))
            pe.wait_ge(*w_in[e % 2].at(e, 2))
            for f in range(FC):
                if ups >= 3:
                    pe.wait_ge(*act_up.at(*divmod(ups - 3, FC)))
                elif ups in (1, 2):
                    pe.wait_ge(*dve_done.at("counted"))
                for ci in range(CC):
                    mm = pe.matmul(UPS[ups % 3][:, 0:CAP], w1[e % 2][:, ci, f * P:(f + 1) * P],
                                   xs[:, ci, e * CAP:(e + 1) * CAP], start=ci == 0, stop=ci == CC - 1)
                mm.then_inc(*pe_up(e, f))
                ups += 1
            pe.wait_ge(*act_up.at(e, FC - 1))
            for j, (c0, m) in enumerate(CH):
                if e >= 1:
                    pe.wait_ge(*dve_down.at(e - 1, j))
                for f in range(FC):
                    mm = pe.matmul(DOWNS[j][0:m, 0:C], hid[e % 2][:, f, c0:c0 + m], w2[e % 2][:, f, :],
                                   start=f == 0, stop=f == FC - 1)
                mm.then_inc(*pe_down(e, j))

    @block.scalar
    def _(act):
        for g in range(G):
            act.wait_ge(*pe_turned.at(g))
            if g >= 2:
                act.wait_ge(*pe_logits.at(g - 2))
            act.activation(xt[:, g % 2, :, :].rearrange("p a b -> p (a b)"), BANK[g % 2][:, 0:2 * P], ACT.Copy)\
               .then_inc(*act_turned(g))
        act.wait_ge(*dve_done.at("sub"))
        act.activation(lg[:, 1, :, :], lg[:, 0, :, :], ACT.Exp).then_inc(*act_exp("e"))
        for n in range(ST // 2):
            act.wait_ge(*pe_rows.at(n))
            act.activation(xs[:, :, 2 * n * P:(2 * n + 2) * P], BANK[n % 2][:, :].rearrange("p (a b) -> p a b", a=CC),
                           ACT.Copy).then_inc(*act_rows(n))
        for e in range(E1):
            for f in range(FC):
                act.wait_ge(*pe_up.at(e, f))
                if e >= 2:
                    act.wait_ge(*pe_down.at(e - 2, 2))
                act.activation(hid[e % 2][:, f, :], UPS[(e * FC + f) % 3][:, 0:CAP], ACT.Relu,
                               bias=b1[:, e, f:f + 1]).then_inc(*act_up(e, f))

    @block.vector
    def _(dve):
        def then(ins):
            ins.then_inc(*dve_chain())
            dve.wait_ge(dve_chain.sem, dve_chain.count)

        def wide(k):
            return red[:, k, :].unsqueeze(2).to_broadcast([P, G, E1])

        L = lambda k: lg[:, k, :, :]
        R = lambda k: red[:, k, :]
        dve.memset(zero[:, :], 0.0).then_inc(*dve_done("zero"))
        dve.memset(ones_b[:, :], 1.0)
        dve.memset(back[:, :, :], 0.0).then_inc(*dve_done("back"))
        dve.memset(half[:, :], -0.5).then_inc(*dve_done("half"))
        dve.wait_ge(*const_in.at("b2"))
        then(dve.tensor_copy(upto_b[:, :], upto[:, :]))
        dve.wait_ge(*pe_logits.at(G - 1))
        then(dve.tensor_copy(L(2), BANK[2][:, 0:P].rearrange("p (g e) -> p g e", e=E1)))
        then(dve.tensor_reduce(R(0), L(2), AX.X, ALU.max))
        dve.tensor_tensor(L(0), L(2), wide(0), ALU.subtract).then_inc(*dve_done("sub"))
        then(dve.tensor_tensor(L(3), L(2), wide(0), ALU.is_equal))
        then(dve.tensor_tensor(L(3), L(3), prefer[:, :, :], ALU.mult))
        then(dve.tensor_reduce(R(1), L(3), AX.X, ALU.max))
        then(dve.tensor_tensor(L(4), prefer[:, :, :], wide(1), ALU.is_equal))
        dve.tensor_copy(oh[:, :, :], L(4)).then_inc(*dve_done("onehot"))
        dve.wait_ge(*act_exp.at("e"))
        then(dve.tensor_reduce(R(2), L(1), AX.X, ALU.add))
        then(dve.reciprocal(R(2), R(2)))
        dve.wait_ge(*pe_counts.at("all"))
        tv = BANK[4][:, 0:P].rearrange("p (g e) -> p g e", e=E1)
        then(dve.tensor_copy(tot[:, :, :], tv))
        src, k, n = tot[:, :, :], 1, 0
        while k < G:
            dst = run[:, n % 2, :, :]
            dve.tensor_copy(dst[:, 0:k, :], src[:, 0:k, :])
            then(dve.tensor_tensor(dst[:, k:G, :], src[:, k:G, :], src[:, 0:G - k, :], ALU.add))
            src, k, n = dst, 2 * k, n + 1
        then(dve.tensor_tensor(src, src, tot[:, :, :], ALU.subtract))
        then(dve.tensor_tensor(src, src, BANK[3][:, 0:P].rearrange("p (g e) -> p g e", e=E1), ALU.add))
        then(dve.tensor_tensor(src, src, L(4), ALU.mult))
        a = dve.tensor_reduce(R(3), src, AX.X, ALU.add)
        a.then_inc(*dve_done("counted"))
        dve.wait_ge(*dve_done.at("counted"))
        then(dve.tensor_scalar(R(4), R(1), -float(CAP), float(E1 * CAP - 1), ALU.mult, ALU.add))
        then(dve.tensor_tensor(R(4), R(4), R(3), ALU.add))
        then(dve.tensor_scalar(R(5), R(3), float(CAP), float(2 * SLOTS), ALU.is_gt, ALU.mult))
        then(dve.tensor_tensor(R(4), R(4), R(5), ALU.add))
        dve.tensor_copy(idx[:, :], R(4)).then_inc(*dve_done("idx"))
        for e in range(E1):
            for j, (c0, m) in enumerate(CH):
                dve.wait_ge(*pe_down.at(e, j))
                if e >= 1:
                    dve.wait_ge(*expert_out[j].at(e - 1))
                dve.tensor_tensor(eo[0:m, j, :], DOWNS[j][0:m, 0:C], b2[0:m, e, :], ALU.add)\
                   .then_inc(*dve_down(e, j))
        dve.wait_ge(*gathered.at(G - 1))
        for g in range(G):
            a = dve.scalar_tensor_tensor(out=x5[:, g, :], in0=back[:, g, :], scalar=red[:, 2, g:g + 1],
                                         in1=x5[:, g, :], op0=ALU.mult, op1=ALU.add)
        then(a)
        for g in range(G):
            a = dve.bn_stats(st[:, g, :], x5[:, g, :])
        then(a)
        for g in range(G):
            a = dve.bn_aggr(mv[:, g, :], st[:, g, :])
        a.then_inc(*dve_done("stats"))
        dve.wait_ge(*pool_done.at("rstd"))
        for g in range(G):
            dve.tensor_scalar(back[:, g, :], x5[:, g, :], mv[:, g, 0:1], rstd[:, g:g + 1], ALU.subtract, ALU.mult)\
               .then_inc(*dve_out(g))

    @block.gpsimd
    def _(pool):
        pool.wait_ge(*dve_done.at("zero"))
        for n in range(ST):
            pool.dma_start(slots_dram[n * P:(n + 1) * P, :], zero[:, :]).then_inc(*cleared(n))
        pool.wait_ge(*cleared.at(ST - 1))
        pool.wait_ge(*dve_done.at("idx"))
        for g in range(G):
            pool.indirect_dma_start(slots_dram, bass.IndirectOffsetOnAxis(ap=idx[:, g:g + 1], axis=0), x5[:, g, :],
                                    None, bounds_check=SLOTS - 1, oob_is_err=False).then_inc(*scattered(g))
        for j in range(3):
            pool.wait_ge(*expert_out[j].at(E1 - 1))
        pool.wait_ge(*dve_done.at("back"))
        for g in range(G):
            pool.indirect_dma_start(back[:, g, :], None, expert_dram,
                                    bass.IndirectOffsetOnAxis(ap=idx[:, g:g + 1], axis=0),
                                    bounds_check=SLOTS - 1, oob_is_err=False).then_inc(*gathered(g))
        pool.wait_ge(*dve_done.at("stats"))
        a = pool.tensor_scalar(ve[:, :], mv[:, :, 1], 1e-5, None, ALU.add)
        a.then_inc(*pool_chain())
        pool.wait_ge(pool_chain.sem, pool_chain.count)
        pool.tensor_tensor(rstd[:, :], ve[:, :], half[:, :], ALU.pow).then_inc(*pool_done("rstd"))


def layouts(inp):
    a = {k: np.asarray(v) for k, v in inp.items()}
    f = np.float32
    order = np.array([(hh * 2 + c) * D + d for c in range(CC) for d in range(D) for hh in range(H // CC)])
    chunked = lambda w: w.reshape(-1, P, w.shape[1]).transpose(1, 0, 2)
    w0 = a["L0_attn_W"]
    qkv = [(w0[:C].T, w0[C:2 * C].T, w0[2 * C:].T),
           (a["L0_xattn_Wq"].T, a["L0_xattn_Wk"].T, a["L0_xattn_Wv"].T),
           (a["L0_ffn_wq"].T, a["L0_ffn_wk"].T, a["L0_ffn_wv"].T),
           (a["L1_attn_Wq"].T, a["L1_attn_Wk"].T, a["L1_attn_Wv"].T),
           (a["L1_xattn_wq_k"], a["L1_xattn_wk_k"], a["L1_xattn_wv_k"])]
    ws = []
    for q, k, v in qkv:
        ws += [q[:, order], k[:, order], v]
    ws += [a["L0_xattn_Wo"].T, a["L0_ffn_wo"].T, a["L1_attn_Wo"].T, a["L1_xattn_wo_k"]]
    out = {"proj": np.stack([chunked(w) for w in ws], 1)}
    two = lambda v: v.reshape(2, P).T
    b0 = a["L0_attn_b"]
    cs = [two(a["L0_xattn_g1"]), two(a["L0_xattn_b1"]), two(a["L0_xattn_g2"]), two(a["L0_xattn_b2"]),
          two(a["L0_ffn_n1_w"]), two(a["L0_ffn_n2_w"]), two(a["L1_attn_ln_w"]), two(a["L1_attn_ln_b"]),
          two(b0[:C][order]), two(b0[C:2 * C][order]), two(a["L1_attn_bq"][order]), two(a["L1_attn_bk"][order]),
          two(a["L1_xattn_wq_b"][order]), two(a["L1_xattn_wk_b"][order]),
          np.stack([np.repeat(a["L0_ffn_qn_w"], 8), np.repeat(a["L0_ffn_kn_w"], 8)], 1)]
    cs.append(np.zeros((P, 32 - 2 * len(cs)), f))
    out["cols"] = np.concatenate(cs, 1)
    rs = [b0[2 * C:], a["L0_xattn_bo"], a["L1_attn_bv"], a["L1_attn_bo"], a["L1_xattn_wv_b"], a["L1_xattn_wo_b"]]
    out["rows"] = np.broadcast_to(np.stack(rs)[None], (P, 6, C))
    for name, src in (("up0", "e0_up"), ("up1a", "e1_w1"), ("up1b", "e1_w2"), ("l1", "e2_l1"), ("l2", "e2_l2"),
                      ("l3", "e2_l3"), ("down3", "e3_down"), ("up3", "e3_up"), ("gate", "gate_w")):
        out[name] = chunked(a["L0_ffn_" + src].T)
    out["downs"] = np.stack([chunked(a["L0_ffn_" + n].T[:, SKIP:]) for n in ("e0_down", "e1_down", "e2_l4", "e3_out")], 1)
    out["x"], out["ctx"] = a["x"], a["ctx_1024"]
    m = a["mask_BxSxS2_ik1"]
    tiles = lambda v: v.reshape(B, TT, P, S).transpose(0, 2, 1, 3)
    out["mask"] = tiles(m)
    out["maskT"] = tiles(m.transpose(0, 2, 1))
    out["gpT"] = tiles(a["fside_BxSxS2_0"].transpose(0, 2, 1))
    mb = np.ascontiguousarray(a["mask_BxS2_bf1"]).view(np.uint8)
    out["m_cols"] = mb.reshape(B, TT, P).transpose(0, 2, 1)
    out["m_rows"] = mb.reshape(B, 1, S)
    out["wg"] = chunked(a["L1_ffn_wg"])
    out["w1"] = a["L1_ffn_w1"].reshape(E1, CC, P, DFF).transpose(0, 2, 1, 3)
    out["w2"] = a["L1_ffn_w2"].reshape(E1, DFF // P, P, C).transpose(0, 2, 1, 3)
    out["b1"] = a["L1_ffn_b1"].reshape(E1, DFF // P, P).transpose(2, 0, 1)
    out["b2"] = np.broadcast_to(a["L1_ffn_b2"][None], (P, E1, C))
    i = np.arange(P)
    out["ident"] = np.eye(P, dtype=f)
    out["rope_swap"] = (i[:, None] == (i[None, :] ^ (H // CC))).astype(f)
    out["head_ones"] = (i[:, None] % (H // CC) == i[None, :] % (H // CC)).astype(f)
    out["causal_q"] = np.where(i[None, :] > i[:, None], f(LOW), f(0)).astype(f)
    out["causal_k"] = np.ascontiguousarray(out["causal_q"].T)
    out["upto"] = (i[:, None] <= i[None, :]).astype(f)
    freq = (f(1.0) / np.power(f(10000.0), np.arange(0, D, 2, dtype=f) / f(D))).astype(f)
    angle = (np.arange(S, dtype=f)[None, :] * freq[:, None]).astype(f)
    d = i // (H // CC)
    out["rope_cos"] = np.cos(angle)[d // 2].astype(f)
    out["rope_sin"] = (np.sin(angle)[d // 2] * np.where(d % 2 == 0, -1.0, 1.0)[:, None]).astype(f)
    out["prefer"] = np.broadcast_to(np.array([4, 3, 2, 1], f), (P, TT, 4))
    out["prefer8"] = np.broadcast_to(np.arange(E1, 0, -1).astype(f), (P, B * S // P, E1))
    return {k: np.ascontiguousarray(v) for k, v in out.items()}


def program(nc, arrays, known):
    t = {}
    for name, v in arrays.items():
        t[name] = nc.dram_tensor(f"in_{name}", v.shape, mybir.dt.from_np(v.dtype), kind="ExternalInput").ap()
    t["out"] = nc.dram_tensor("out_x", [B * S, C], F32, kind="ExternalOutput").ap()
    for name in ("x", "ctx"):
        t[name] = t[name].rearrange("b (t p) c -> b p t c", p=P)
    build(nc, t, known)
    return nc


def kernel(**inputs):
    import concourse.bacc as bacc
    from concourse.bass_utils import run_bass_kernel_spmd
    arrays = layouts(inputs)
    known = {"pass": False}
    program(bacc.Bacc("TRN2", target_bir_lowering=False, num_devices=1), arrays, known)
    known["pass"] = True
    nc = program(bacc.Bacc("TRN2", target_bir_lowering=False, num_devices=1), arrays, known)
    r = run_bass_kernel_spmd(nc, [{f"in_{k}": v for k, v in arrays.items()}], core_ids=[0])
    return r.results[0]["out_x"].reshape(B, S, C)
```

```python
from contextlib import ExitStack

import numpy as np

import concourse.bass as bass
from concourse import mybir

F32 = mybir.dt.float32
BF16 = mybir.dt.bfloat16
I32 = mybir.dt.int32
U32 = mybir.dt.uint32
U8 = mybir.dt.uint8
ALU = mybir.AluOpType
ACT = mybir.ActivationFunctionType
AX = mybir.AxisListType

P = 128
B, S, C = 8, 256, 256
H, D = 16, 16
CC = C // P
TT = S // P
PAIRS = H // 2
LAYERS = 5
STREAMS = 2
HID = 512
E1, DFF, CAP = 8, 1024, int(1.25 * B * S / 8)
KEEP = 192
SKIP = C - KEEP
Q_PARTS = (0, 0, 1, 1, 0, 2)
K_PARTS = (0, 1, 0, 1, 2, 0)
ROWS = 16 * len(Q_PARTS)
SHIFT = 3
LOW = -1.0e30
CAUSAL = (0, 2)
SELF_LN = (1, 2, 3)


class Signal:

    def __init__(self, name, sem, known, step=1):
        self.name, self.sem, self.known, self.step, self.count = name, sem, known, step, 0

    def __call__(self, *label):
        self.count += self.step
        assert self.known["pass"] or not label or (self.name, label) not in self.known, label
        self.known[self.name, label] = self.count
        return self.sem, self.step

    def at(self, *label):
        assert not self.known["pass"] or (self.name, label) in self.known, (self.name, label)
        return self.sem, self.known.get((self.name, label), self.step)


def build(nc, t, known):
    outer = ExitStack()
    with outer:
        x5_dram = nc.dram_tensor("x5_rows", [B * S, C], F32, kind="Internal").ap()
        slots_dram = nc.dram_tensor("slot_rows", [E1 * CAP, C], F32, kind="Internal").ap()
        expert_dram = nc.dram_tensor("expert_rows", [E1 * CAP, C], F32, kind="Internal").ap()
        with ExitStack() as ctx:
            attention_layers(nc, ctx, t, known, x5_dram)
        with ExitStack() as ctx:
            routed_mixture(nc, ctx, t, known, x5_dram, slots_dram, expert_dram)


def schedule():
    def between(s, l):
        at = {0: [("y", s, l, 0)], 1: [("y", s, l, 1)], 4: [("stat", s, l, 0)], 5: [("norm", s, l, 0)]}
        if l > 0:
            at[2] = [("yT", s, l, 0)]
            at[3] = [("w", s, l, 0)]
        else:
            at[2] = [("w", s, l, 0)]
            at[3] = [("k", s, 1, 0)]
            at[4] += [("v", s, 1, 0)]
        if l == 2:
            at[6] = [("T", s, "f", 0), ("gate", s, 2, 0)]
            at["parts"] = [("e0", s, 2, 0), ("route", s, 2, 0)]
            at["shift"] = [("e3a", s, 2, 0)]
            at["exp0"] = [("down", s, 2, 0)]
        elif l == 0:
            at[7] = [("T", s, 1, 0)]
            at["parts"] = [("q", s, 1, 0)]
            at["exp0"] = [("split", s, 1, 0)]
        elif l < LAYERS - 1:
            at[7] = [("T", s, l + 1, 0)]
            at["parts"] = [("q", s, l + 1, 0)]
            at["shift"] = [("k", s, l + 1, 0), ("v", s, l + 1, 0)]
            at["exp0"] = [("again", s, l + 1, 0)]
            at["exp1"] = [("split", s, l + 1, 0)]
        else:
            at[7] = [("out", s, l, 0)]
        return at

    def begin(s):
        return {0: [("context", s, 0, 0), ("T", s, 0, 0)], 1: [("q", s, 0, 0)],
                "parts": [("k", s, 0, 0)], "shift": [("v", s, 0, 0), ("split", s, 0, 0)]}

    def after_experts(s):
        return {0: [("stat", s, "f", 0)], 1: [("norm", s, "f", 0)], 3: [("T", s, 3, 0)], 4: [("q", s, 3, 0)],
                "parts": [("k", s, 3, 0)], "shift": [("v", s, 3, 0)], "exp0": [("again", s, 3, 0)],
                "exp1": [("split", s, 3, 0)]}

    def attend(s, l, other):
        for p in range(PAIRS):
            yield ("max", s, l, p)
            yield from other.get(p, ())
        yield ("parts", s, l, 0)
        yield from other.get("parts", ())
        yield ("shift", s, l, 0)
        yield from other.get("shift", ())
        for p in range(PAIRS):
            yield ("exp", s, l, p)
            if p >= 2:
                yield ("mix", s, l, p - 2)
            yield from other.get(f"exp{p}", ())
        yield ("mix", s, l, PAIRS - 2)
        yield ("mix", s, l, PAIRS - 1)

    def experts(s, other, names):
        places = PLACES[len(names)]
        for n, (name, e) in enumerate(names):
            yield (name, s, 2, e)
            for k in places[n]:
                yield from other.get(k, ())

    FIRST = [("e2a", 0), ("e3b", 0), ("e2b", 0), ("down", 3), ("e2c", 0), ("e1a", 0), ("down", 2), ("e1b", 0),
             ("down", 1)]
    SECOND = [("e0", 0), ("e2a", 0), ("e3a", 0), ("down", 0), ("e2b", 0), ("e3b", 0), ("e2c", 0), ("down", 3),
              ("e1a", 0), ("down", 2), ("e1b", 0), ("down", 1)]
    PLACES = {9: [[0, 1], [2], [3], [4, 5], [6, 7, "parts"], ["shift"], ["exp0"], ["exp1"], []],
              12: [[0], [1], [], [3], [4], ["parts"], ["shift"], ["exp0"], [], ["exp1"], [], []]}
    order = []
    for steps in begin(0).values():
        order += steps
    order += attend(0, 0, begin(1))
    order += attend(1, 0, between(0, 0))
    for l in (1, 2):
        order += attend(0, l, between(1, l - 1))
        order += attend(1, l, between(0, l))
    order += experts(0, {k: v for k, v in between(1, 2).items() if k not in ("parts", "shift", "exp0")}
                     | {"parts": [("route", 1, 2, 0)]}, FIRST)
    order += experts(1, after_experts(0), SECOND)
    order += attend(0, 3, after_experts(1))
    order += attend(1, 3, between(0, 3))
    order += attend(0, 4, between(1, 3))
    order += attend(1, 4, between(0, 4))
    for _, steps in sorted(between(1, 4).items()):
        order += steps
    return order


def attention_layers(nc, ctx, t, known, x5_dram):
    def sb(name, shape, dt=F32):
        return ctx.enter_context(nc.sbuf_tensor(name, shape, dt))

    work = []

    def signal(name, step=1):
        sem = ctx.enter_context(nc.semaphore(name))
        work.append(sem)
        return Signal(name, sem, known, step)

    ident = sb("ident", [P, P])
    ident_b = sb("ident_b", [P, P], BF16)
    causal_q = sb("causal_q", [P, P], BF16)
    causal_k = sb("causal_k", [P, P], BF16)
    rope_swap = sb("rope_swap", [P, P])
    head_ones = sb("head_ones", [P, P])
    rope_cos = sb("rope_cos", [P, S])
    rope_sin = sb("rope_sin", [P, S])
    ones_row = sb("ones_row", [1, P], BF16)
    sum_cols = sb("sum_cols", [P, 32])
    neg_half = sb("neg_half", [P, 2, TT])
    eps_col = sb("eps_col", [P, 1])
    cols = sb("cols", [P, 32])
    rows = sb("rows", [P, 6, C])
    proj = sb("proj", [P, 19, CC, C])
    up0 = sb("up0", [P, 2, HID])
    up1a = sb("up1a", [P, 2, HID])
    up1b = sb("up1b", [P, 2, HID])
    l1 = sb("l1", [P, 2, HID])
    l2 = sb("l2", [P, 4, HID])
    l3 = sb("l3", [P, 4, HID])
    down3 = sb("down3", [P, 2, C])
    up3 = sb("up3", [P, 2, HID])
    downs = sb("downs", [P, 4, 4, KEEP])
    gate = sb("gate", [P, CC, 4])
    prefer = sb("prefer", [P, TT, 4])

    X = [sb(f"x{s}", [P, TT, C]) for s in range(STREAMS)]
    HB = [sb(f"h{s}", [P, TT, C]) for s in range(STREAMS)]
    HT = [sb(f"hT{s}", [P, CC, S]) for s in range(STREAMS)]
    T = [sb(f"t{s}", [P, TT, C]) for s in range(STREAMS)]
    QK = [sb(f"qk{s}", [P, 2, CC, S]) for s in range(STREAMS)]
    SP = [sb(f"split{s}", [P, 6, CC * S], BF16) for s in range(STREAMS)]
    QKS = [sb(f"stack{s}", [ROWS + SHIFT, H // 2, 2, 2, S], BF16) for s in range(STREAMS)]
    V = [sb(f"v{s}", [P, TT, H, 32]) for s in range(STREAMS)]
    GP = [sb(f"gp{s}", [P, TT, S]) for s in range(STREAMS)]
    NQ = [sb(f"nq{s}", [P, TT, S], BF16) for s in range(STREAMS)]
    NK = [sb(f"nk{s}", [P, TT, S], BF16) for s in range(STREAMS)]
    PR = sb("probs", [P, 5, 2, TT, S])
    HIDDEN = [PR[:, k, :, :, :].rearrange("p a b c -> p (a b) c") for k in range(5)]
    m_u8 = [sb(f"m_u8{s}", [P, TT], U8) for s in range(STREAMS)]
    mr_u8 = [sb(f"mr_u8{s}", [1, S], U8) for s in range(STREAMS)]
    m_col = [sb(f"m_col{s}", [P, TT]) for s in range(STREAMS)]
    m_row = [sb(f"m_row{s}", [1, S], BF16) for s in range(STREAMS)]
    ST = [sb(f"st{s}", [P, TT, 6]) for s in range(STREAMS)]
    MV = [sb(f"mv{s}", [P, TT, 2]) for s in range(STREAMS)]
    VE = [sb(f"ve{s}", [P, 2, TT]) for s in range(STREAMS)]
    RSTD = [sb(f"rstd{s}", [P, 2, TT]) for s in range(STREAMS)]
    MX = [sb(f"mx{s}", [P, H, TT]) for s in range(STREAMS)]
    MB = [sb(f"max_parts{s}", [P, TT, 2, SHIFT, H // 2], BF16) for s in range(STREAMS)]
    MT = [sb(f"mT{s}", [SHIFT * H, S], BF16) for s in range(STREAMS)]
    RS = [sb(f"rs{s}", [P, TT, H]) for s in range(STREAMS)]
    GT = [sb(f"gt{s}", [P, 10, TT, 4]) for s in range(STREAMS)]
    GM = [sb(f"gmx{s}", [P, 6, TT]) for s in range(STREAMS)]

    SLOT = [ctx.enter_context(nc.psum_tensor(f"slot{i}", [P, 2, TT, S], F32)) for i in range(2)]
    BANK = [ctx.enter_context(nc.psum_tensor(f"bank{i}", [P, 2, S], F32)) for i in range(4)]

    bank_filled = signal("bank_filled")
    slot_filled = signal("slot_filled")
    mixed = signal("mixed")
    act_read = signal("act_read")
    dve_read = signal("dve_read")
    exped = signal("exped")
    maxed = signal("maxed")
    dve_step = signal("dve_step")
    act_step = signal("act_step")
    pool_step = signal("pool_step")
    dve_chain = signal("dve_chain")
    pool_chain = signal("pool_chain")
    x_in = [signal(f"x_in{s}", 16) for s in range(STREAMS)]
    mask_in = [signal(f"mask_in{s}", 16) for s in range(STREAMS)]
    ctx_in = [signal(f"ctx_in{s}", 16) for s in range(STREAMS)]
    group_in = [signal(f"group_in{s}", 16) for s in range(STREAMS)]
    stack_in = [signal(f"stack_in{s}", 16) for s in range(STREAMS)]
    shift_in = [signal(f"shift_in{s}", 16) for s in range(STREAMS)]
    x_out = signal("x_out", 16)
    consts_in = ctx.enter_context(nc.semaphore("consts_in"))
    weights_in = [ctx.enter_context(nc.semaphore(f"weights_in{l}")) for l in range(LAYERS + 1)]
    arrived = ctx.enter_context(nc.semaphore("arrived"))
    rounds_ended = ctx.enter_context(nc.semaphore("rounds_ended"))
    released = ctx.enter_context(nc.semaphore("released"))

    COL = {n: i for i, n in enumerate(
        ["g1", "b1", "g2", "b2", "n1", "n2", "lw", "lb", "bqA", "bkA", "bqD", "bkD", "bqE", "bkE", "qn"])}
    GAIN = {1: ("g1", "b1"), 2: ("n1", None), 3: ("lw", "lb"), "f": ("n2", None)}
    QB = {0: "bqA", 3: "bqD", 4: "bqE"}
    KB = {0: "bkA", 3: "bkD", 4: "bkE"}

    def col(name, c=0):
        i = 2 * COL[name] + c
        return cols[:, i:i + 1]

    VROW = {0: 0, 3: 2, 4: 4}
    OROW = {1: 1, 3: 3, 4: 5}
    wq = lambda l: 3 * l
    wk = lambda l: 3 * l + 1
    wv = lambda l: 3 * l + 2
    wo = lambda l: 14 + l
    queries = lambda s, h: QKS[s][:, h // 2, 0, h % 2, :]
    keys = lambda s, h: QKS[s][:, h // 2, 1, h % 2, :]
    eps_f, eps_n = 1.1920929e-07, 1e-5

    CONSTS = [(ident, "ident"), (rope_swap, "rope_swap"), (head_ones, "head_ones"), (rope_cos, "rope_cos"),
              (rope_sin, "rope_sin"), (cols, "cols"), (rows, "rows"), (gate, "gate"), (prefer, "prefer")]
    EXPERTS = [(up0, "up0"), (l1, "l1"), (l2, "l2"), (downs, "downs"), (down3, "down3"), (l3, "l3"), (up3, "up3"),
               (up1a, "up1a"), (up1b, "up1b")]
    with nc.Block() as block:
        @block.sync
        def _(sp):
            sp.dma_start(X[0][:, 0, 0:P], t["causal_q"]).then_inc(consts_in, 16)
            sp.dma_start(X[0][:, 1, 0:P], t["causal_k"]).then_inc(consts_in, 16)
            for dst, name in CONSTS:
                sp.dma_start(dst.ap(), t[name]).then_inc(consts_in, 16)
            for l in range(LAYERS):
                sp.dma_start(proj[:, 3 * l:3 * l + 3, :, :], t["proj"][:, 3 * l:3 * l + 3, :, :])\
                    .then_inc(weights_in[l], 16)
                if l:
                    sp.dma_start(proj[:, wo(l), :, :], t["proj"][:, wo(l), :, :]).then_inc(weights_in[l], 16)
                if l == 2:
                    for dst, name in EXPERTS:
                        sp.dma_start(dst.ap(), t[name]).then_inc(weights_in[LAYERS], 16)
            sp.wait_ge(consts_in, 16 * (len(CONSTS) + 2))

        @block.gpsimd
        def _(pool):
            pool.memset(neg_half[:, :, :], -0.5)
            pool.memset(eps_col[:, :], eps_f)
            pool.memset(sum_cols[:, 0:D], 0.0)
            pool.memset(sum_cols[:, D:32], 1.0)

        @block.vector
        def _(dve):
            for s in range(STREAMS):
                dve.memset(QKS[s][ROWS:ROWS + SHIFT, :, 1, :, :], 1.0)
            dve.memset(ones_row[:, :], 1.0)
            dve.wait_ge(consts_in, 16 * (len(CONSTS) + 2))
            dve.tensor_copy(ident_b[:, :], ident[:, :])
            dve.tensor_copy(causal_q[:, :], X[0][:, 0, 0:P])
            dve.tensor_copy(causal_k[:, :], X[0][:, 1, 0:P])
            for name in ("bqA", "bqD", "bqE", "qn"):
                at = cols[:, 2 * COL[name]:2 * COL[name] + (1 if name == "qn" else 2)]
                dve.tensor_scalar(at, at, 0.25, None, ALU.mult)

    block = ctx.enter_context(nc.Block())
    ROUNDS = B // STREAMS
    SCHEDULE = schedule()

    def finish(eng, i):
        eng.drain()
        eng.sem_inc(arrived, 1)
        eng.wait_ge(released, i + 1)

    def bank_of(*label):
        return BANK[known.get(("bank", label), 0)]

    def slot_of(*label):
        return SLOT[known.get(("slot", label), 0)]

    def mixing(s, l, p):
        return mixed.at(s, l, p) if p % 2 == 0 else bank_filled.at("o", s, l, p // 2)

    READER = {"T": act_read, "TC": act_read, "q": act_read, "k": act_read, "neg": act_read, "o": act_read,
              "y": dve_read, "yT": act_read, "w": dve_read, "gate": dve_read, "e0": act_read, "e1a": act_read,
              "e1b": dve_read, "e2a": act_read, "e2b": act_read, "e2c": act_read, "e3a": act_read, "e3b": act_read,
              "down": dve_read}

    def reader(label):
        kind, s, l = label[:3]
        if kind in ("q2", "k2"):
            return act_read if l == 2 else dve_read
        if kind == "v":
            return dve_read if l in VROW else act_read
        return READER[kind]

    @block.tensor
    def _(pe):
        last_in_bank = [None] * 4
        last_in_slot = [None] * 2
        turns = {"bank": 0, "slot": 0}

        def bank(*label):
            at = turns["bank"] % 4
            turns["bank"] += 1
            if last_in_bank[at] is not None:
                pe.wait_ge(*reader(last_in_bank[at]).at(*last_in_bank[at]))
            last_in_bank[at] = label
            known["bank", label] = at
            return BANK[at]

        def slot(phase, *label):
            k = turns["slot"] % 2
            turns["slot"] += 1
            if last_in_slot[k] is not None:
                was, lab = last_in_slot[k]
                pe.wait_ge(*(maxed if was == "max" else exped).at(*lab))
            last_in_slot[k] = (phase, label)
            known["slot", (phase, *label)] = k
            return SLOT[k]

        def transposes(label, src):
            ps = bank(*label)
            for c in range(CC):
                for tt in range(TT):
                    mm = pe.transpose(ps[:, c, tt * P:(tt + 1) * P], src[:, tt, c * P:(c + 1) * P], ident[:, :])
            mm.then_inc(*bank_filled(*label))

        def turn(s, l):
            if l == 0:
                pe.wait_ge(*x_in[s].at())
                transposes(("T", s, l), X[s])
                return
            pe.wait_ge(*dve_step.at("h", s, l))
            transposes(("T", s, l), X[s] if l == 4 else HB[s])

        def turn_context(s):
            pe.wait_ge(*dve_step.at("hc", s))
            transposes(("TC", s, 0), HB[s])

        def source(s, l):
            if l == 1:
                pe.wait_ge(*act_read.at("TC", s, 0))
                return GP[s]
            if l == 4:
                pe.wait_ge(*ctx_in[s].at(4))
                return T[s]
            return HT[s]

        def project(kind, s, l, w, src):
            ps = bank(kind, s, l)
            for co in range(CC):
                for ci in range(CC):
                    mm = pe.matmul(ps[:, co, :], proj[:, w, ci, co * P:(co + 1) * P], src[:, ci, :],
                                   start=ci == 0, stop=ci == CC - 1)
            mm.then_inc(*bank_filled(kind, s, l))

        def project_rows(kind, s, l, w, src):
            ps = bank(kind, s, l)
            for tt in range(TT):
                for ci in range(CC):
                    mm = pe.matmul(ps[:, tt, :], src[:, ci, tt * P:(tt + 1) * P], proj[:, w, ci, :],
                                   start=ci == 0, stop=ci == CC - 1)
            mm.then_inc(*bank_filled(kind, s, l))

        def project_again(s, l):
            for n, kind in enumerate(("q", "k")):
                if l == 2:
                    pe.wait_ge(*act_step.at("sq" + kind, s))
                else:
                    pe.wait_ge(*act_read.at(kind, s, l))
                ps = bank(kind + "2", s, l)
                if l == 2:
                    mm = pe.matmul(ps[:, :, :], head_ones[:, :], (HB, T)[n][s][:, :, :], start=True, stop=True)
                else:
                    mm = pe.matmul(ps[:, :, :], rope_swap[:, :], QK[s][:, n, :, :], start=True, stop=True)
                mm.then_inc(*bank_filled(kind + "2", s, l))

        def scores_for_max(s, l, p):
            ps = slot("max", s, l, p)
            if p == 0:
                pe.wait_ge(*stack_in[s].at(l, len(Q_PARTS) - 1))
                if l == 1:
                    pe.wait_ge(*pool_step.at("m_row", s))
            for a in range(2):
                h = 2 * p + a
                for qt in range(TT):
                    n = (qt + 1) * P if l in CAUSAL else S
                    masked = l in CAUSAL or l in (1, 4)
                    mm = pe.matmul(ps[:, a, qt, 0:n], queries(s, h)[0:ROWS, qt * P:(qt + 1) * P],
                                   keys(s, h)[0:ROWS, 0:n], start=True, stop=not masked)
                    if l in CAUSAL:
                        mm = pe.matmul(ps[:, a, qt, qt * P:n], ident_b[:, :], causal_q[:, :],
                                       start=False, stop=True)
                    elif l == 1:
                        mm = pe.matmul(ps[:, a, qt, :], ones_row[:, :], m_row[s][:, :], start=False, stop=True)
                    elif l == 4:
                        mm = pe.matmul(ps[:, a, qt, :], ident_b[:, :], NQ[s][:, qt, :], start=False, stop=True)
            mm.then_inc(*slot_filled("max", s, l, p))

        def turn_maxima(s, l):
            ps = bank("neg", s, l)
            out = ps[:, 0, :].bitcast(BF16)
            pe.wait_ge(*dve_step.at("parts", s, l))
            for qt in range(TT):
                mm = pe.transpose(out[0:SHIFT * H, qt * P:(qt + 1) * P],
                                  MB[s][:, qt, :, :, :].rearrange("p a b c -> p (a b c)"), ident_b[:, :])
            mm.then_inc(*bank_filled("neg", s, l))

        def scores_for_exp(s, l, p):
            ps = slot("exp", s, l, p)
            if p == 0:
                pe.wait_ge(*shift_in[s].at(l, 1))
            for a in range(2):
                h = 2 * p + a
                for kt in range(TT):
                    q0 = kt * P if l in CAUSAL else 0
                    masked = l in CAUSAL or l == 4
                    mm = pe.matmul(ps[:, a, kt, q0:S], keys(s, h)[:, kt * P:(kt + 1) * P],
                                   queries(s, h)[:, q0:S], start=True, stop=not masked)
                    if l in CAUSAL:
                        mm = pe.matmul(ps[:, a, kt, kt * P:(kt + 1) * P], ident_b[:, :], causal_k[:, :],
                                       start=False, stop=True)
                    elif l == 4:
                        mm = pe.matmul(ps[:, a, kt, :], ident_b[:, :], NK[s][:, kt, :], start=False, stop=True)
            mm.then_inc(*slot_filled("exp", s, l, p))

        def mix_values(s, l, p):
            if p == 0:
                pe.wait_ge(*reader(("v", s, l)).at("v", s, l))
            if p % 2 == 0:
                bank("o", s, l, p // 2)
            pe.wait_ge(*exped.at(s, l, p))
            if l == 4:
                pe.wait_ge(*dve_step.at("weighted", s, p))
                pe.wait_ge(*pool_step.at("weighted", s, p))
            k = p % 3
            for a in range(2):
                h = 2 * p + a
                row = 32 * (h % 4)
                out = bank_of("o", s, l, p // 2)[row:row + 32, 0, :]
                if l == 4:
                    for kt in range(TT):
                        pe.matmul(out, sum_cols[:, :], PR[:, k, a, kt, :], start=kt == 0, stop=False)
                    for kt in range(TT):
                        mm = pe.matmul(out, V[s][:, kt, h, :], PR[:, 3 + p % 2, a, kt, :], start=False,
                                       stop=kt == TT - 1)
                else:
                    for kt in range(TT):
                        q0 = kt * P if l in CAUSAL else 0
                        mm = pe.matmul(out[:, q0:S], V[s][:, kt, h, :], PR[:, k, a, kt, q0:S],
                                       start=kt == 0, stop=kt == TT - 1)
            if p % 2 == 0:
                mm.then_inc(*mixed(s, l, p))
            else:
                mm.then_inc(*bank_filled("o", s, l, p // 2))

        def turn_outputs(s, l, qt):
            if qt == 0:
                pe.wait_ge(*act_read.at("o", s, l, PAIRS // 2 - 1))
            O = QK[s][:, :, :, :].rearrange("p a b c -> p (a b) c")
            ps = bank("y", s, l, qt)
            for g in range(4):
                mm = pe.transpose(ps[:, g // 2, (g % 2) * P:(g % 2 + 1) * P], O[:, g, qt * P:(qt + 1) * P],
                                  ident[:, :])
            mm.then_inc(*bank_filled("y", s, l, qt))

        def expert(kind, s, w, src, kc, halves=2):
            for half in range(halves):
                ps = bank(kind, s, 2, half)
                for j in range(2):
                    o = (2 * half + j) * P
                    for k in range(kc):
                        mm = pe.matmul(ps[:, j, :], w[:, k, o:o + P], src[:, k, :], start=k == 0, stop=k == kc - 1)
                mm.then_inc(*bank_filled(kind, s, 2, half))

        def expert_down(s, e, src):
            ps = bank("down", s, 2, e)
            for tt in range(TT):
                for k in range(4):
                    mm = pe.matmul(ps[:, tt, 0:KEEP], src[:, k, tt * P:(tt + 1) * P], downs[:, e, k, :],
                                   start=k == 0, stop=k == 3)
            mm.then_inc(*bank_filled("down", s, 2, e))

        with pe.Fori(0, ROUNDS) as i:
            for step, s, l, n in SCHEDULE:
                if step == "T":
                    turn(s, l)
                elif step == "context":
                    turn_context(s)
                elif step == "q":
                    pe.wait_ge(weights_in[l], 16 * (1 + (l > 0)))
                    pe.wait_ge(*act_read.at("T", s, l))
                    project("q", s, l, wq(l), HT[s])
                elif step == "k":
                    project("k", s, l, wk(l), source(s, l))
                elif step == "v":
                    project_rows("v", s, l, wv(l), source(s, l))
                elif step == "again" and l in (2, 3):
                    project_again(s, l)
                elif step == "max":
                    scores_for_max(s, l, n)
                elif step == "shift":
                    turn_maxima(s, l)
                elif step == "exp":
                    scores_for_exp(s, l, n)
                elif step == "mix":
                    mix_values(s, l, n)
                elif step == "y":
                    turn_outputs(s, l, n)
                elif step == "yT":
                    pe.wait_ge(*dve_read.at("y", s, l, TT - 1))
                    transposes(("yT", s, l), HB[s])
                elif step == "w" and l > 0:
                    pe.wait_ge(*act_read.at("yT", s, l))
                    project_rows("w", s, l, wo(l), HT[s])
                elif step == "gate":
                    pe.wait_ge(weights_in[LAYERS], 16 * len(EXPERTS))
                    pe.wait_ge(*act_read.at("T", s, "f"))
                    ps = bank("gate", s, 2)
                    for tt in range(TT):
                        for ci in range(CC):
                            mm = pe.matmul(ps[:, tt, 0:4], HT[s][:, ci, tt * P:(tt + 1) * P], gate[:, ci, :],
                                           start=ci == 0, stop=ci == CC - 1)
                    mm.then_inc(*bank_filled("gate", s, 2))
                elif step == "e0":
                    expert("e0", s, up0, HT[s], 2)
                elif step == "e2a":
                    expert("e2a", s, l1, HT[s], 2)
                elif step == "e2b":
                    pe.wait_ge(*act_read.at("e2a", s, 2, 1))
                    expert("e2b", s, l2, HIDDEN[0], 4)
                elif step == "e2c":
                    pe.wait_ge(*act_read.at("e2b", s, 2, 1))
                    expert("e2c", s, l3, HIDDEN[1], 4)
                elif step == "e3a":
                    expert("e3a", s, down3, HT[s], 2, 1)
                elif step == "e3b":
                    pe.wait_ge(*act_read.at("e3a", s, 2, 0))
                    expert("e3b", s, up3, HIDDEN[4], 2)
                elif step == "e1a":
                    expert("e1a", s, up1a, HT[s], 2)
                elif step == "e1b":
                    expert("e1b", s, up1b, HT[s], 2)
                elif step == "down":
                    src, made = {0: (3, act_read.at("e0", s, 2, 1)), 2: (0, act_read.at("e2c", s, 2, 1)),
                                 3: (2, act_read.at("e3b", s, 2, 1)), 1: (3, dve_read.at("e1b", s, 2, 1))}[n]
                    pe.wait_ge(*made)
                    expert_down(s, n, HIDDEN[src])
            finish(pe, i)

    @block.scalar
    def _(act):
        free = {k: None for k in range(5)}

        def take(k, reader_is_through):
            if free[k] is not None:
                act.wait_ge(*free[k])
            free[k] = reader_is_through

        def read_turned(kind, s, l, dst, names):
            act.wait_ge(*bank_filled.at(kind, s, l))
            ps = bank_of(kind, s, l)
            if names is None:
                act.activation(dst[:, :, :], ps[:, :, :], ACT.Copy).then_inc(*act_read(kind, s, l))
                return
            gain, bias = names
            for c in range(CC):
                a = act.activation(dst[:, c, :], ps[:, c, :], ACT.Identity, scale=col(gain, c),
                                   bias=col(bias, c) if bias else 0.0)
            a.then_inc(*act_read(kind, s, l))

        def read_projected(kind, s, l):
            n = "qk".index(kind)
            act.wait_ge(*bank_filled.at(kind, s, l))
            if l == 0:
                act.wait_ge(*pool_step.at("nk", s))
            ps = bank_of(kind, s, l)
            scale = 0.25 if kind == "q" and l != 2 else 1.0
            bias = (QB, KB)[n].get(l)
            part = SP[s][:, 3 * n, :].rearrange("p (c t) -> p c t", c=CC)
            if l == 2:
                act.wait_ge(*dve_step.at("x", s, l))
                act.activation((HB, T)[n][s][:, :, :], ps[:, :, :], ACT.Square).then_inc(*act_step("sq" + kind, s))
            if bias is None:
                if l == 2:
                    scale = col("qn", n)
                else:
                    act.activation(part, ps[:, :, :], ACT.Identity, scale=scale)
                a = act.activation(QK[s][:, n, :, :], ps[:, :, :], ACT.Identity, scale=scale)
            else:
                for c in range(CC):
                    if l != 3:
                        act.activation(part[:, c, :], ps[:, c, :], ACT.Identity, bias=col(bias, c), scale=scale)
                    a = act.activation(QK[s][:, n, c, :], ps[:, c, :], ACT.Identity, bias=col(bias, c), scale=scale)
            a.then_inc(*act_read(kind, s, l))

        def exponentials(s, l, p):
            take(p % 3, mixing(s, l, p))
            act.wait_ge(*slot_filled.at("exp", s, l, p))
            ps = slot_of("exp", s, l, p)
            dst = PR[:, p % 3, :, :, :]
            if l in CAUSAL or l == 1:
                for kt in range(TT):
                    q0 = kt * P if l in CAUSAL else 0
                    a = act.activation(dst[:, :, kt, q0:S], ps[:, :, kt, q0:S], ACT.Exp,
                                       bias=m_col[s][:, kt:kt + 1] if l == 1 else 0.0)
            else:
                a = act.activation(dst, ps[:, :, :, :], ACT.Exp)
            a.then_inc(*exped(s, l, p))

        def hidden(kind, s, k, func, through, halves=2):
            take(k, through)
            for half in range(halves):
                act.wait_ge(*bank_filled.at(kind, s, 2, half))
                act.activation(HIDDEN[k][:, 2 * half:2 * half + 2, :], bank_of(kind, s, 2, half)[:, :, :], func)\
                   .then_inc(*act_read(kind, s, 2, half))

        with act.Fori(0, ROUNDS) as i:
            for step, s, l, n in SCHEDULE:
                if step == "T":
                    read_turned("T", s, l, HT[s], GAIN.get(l))
                elif step == "context":
                    read_turned("TC", s, 0, GP[s], ("g2", "b2"))
                elif step in ("q", "k"):
                    read_projected(step, s, l)
                elif step == "v" and l not in VROW:
                    act.wait_ge(*bank_filled.at("v", s, l))
                    for tt in range(TT):
                        a = act.activation(V[s][:, tt, :, 0:D],
                                           bank_of("v", s, l)[:, tt, :].rearrange("p (h d) -> p h d", d=D), ACT.Copy)
                    a.then_inc(*act_read("v", s, l))
                elif step == "again" and l == 2:
                    for k, kind in enumerate(("q", "k")):
                        act.wait_ge(*bank_filled.at(kind + "2", s, l))
                        act.activation((HB, T)[k][s][:, :, :], bank_of(kind + "2", s, l)[:, :, :], ACT.Sqrt,
                                       bias=eps_col[:, :], scale=1.0 / D).then_inc(*act_read(kind + "2", s, l))
                elif step == "shift":
                    act.wait_ge(*bank_filled.at("neg", s, l))
                    src = bank_of("neg", s, l)[:, 0, :].bitcast(BF16)[0:SHIFT * H, 0:S]
                    act.activation(MT[s][:, :], src, ACT.Copy).then_inc(*act_read("neg", s, l))
                elif step == "exp":
                    exponentials(s, l, n)
                elif step == "mix" and n % 2 == 1:
                    act.wait_ge(*bank_filled.at("o", s, l, n // 2))
                    O = QK[s][:, :, :, :].rearrange("p a b c -> p (a b) c")
                    act.activation(O[:, n // 2, :], bank_of("o", s, l, n // 2)[:, 0, :], ACT.Copy).then_inc(*act_read("o", s, l, n // 2))
                elif step == "yT":
                    read_turned("yT", s, l, HT[s], None)
                elif step == "route":
                    act.wait_ge(*dve_step.at("gate_sub", s))
                    act.activation(GT[s][:, 1, :, :], GT[s][:, 0, :, :], ACT.Exp).then_inc(*act_step("gate_exp", s))
                elif step == "e0":
                    hidden("e0", s, 3, ACT.Gelu, bank_filled.at("down", s, 2, 0))
                elif step == "e2a":
                    hidden("e2a", s, 0, ACT.Gelu, bank_filled.at("e2b", s, 2, 1))
                elif step == "e2b":
                    hidden("e2b", s, 1, ACT.Gelu, bank_filled.at("e2c", s, 2, 1))
                elif step == "e2c":
                    hidden("e2c", s, 0, ACT.Gelu, bank_filled.at("down", s, 2, 2))
                elif step == "e3a":
                    hidden("e3a", s, 4, ACT.Gelu, bank_filled.at("e3b", s, 2, 1), 1)
                elif step == "e3b":
                    hidden("e3b", s, 2, ACT.Gelu, bank_filled.at("down", s, 2, 3))
                elif step == "e1a":
                    hidden("e1a", s, 3, ACT.Silu, bank_filled.at("down", s, 2, 1))
            finish(act, i)

    @block.vector
    def _(dve):
        def then(ins):
            ins.then_inc(*dve_chain())
            dve.wait_ge(dve_chain.sem, dve_chain.count)

        def later(ins):
            ins.then_inc(*dve_chain())
            return dve_chain.count

        def read(count):
            dve.wait_ge(dve_chain.sem, count)

        def statistics(s, src, label, mean_square):
            for tt in range(TT):
                a = dve.bn_stats(ST[s][:, tt, :], src[:, tt, :])
            then(a)
            for tt in range(TT):
                a = dve.bn_aggr(MV[s][:, tt, :], ST[s][:, tt, :])
            if mean_square:
                then(a)
                then(dve.tensor_tensor(VE[s][:, 0, :], MV[s][:, :, 0], MV[s][:, :, 0], ALU.mult))
                a = dve.tensor_tensor(MV[s][:, :, 1], VE[s][:, 0, :], MV[s][:, :, 1], ALU.add)
            a.then_inc(*dve_step("stat", *label))

        def centred(s, src, dst, which):
            for tt in range(TT):
                a = dve.tensor_scalar(dst[:, tt, :], src[:, tt, :], MV[s][:, tt, 0:1], RSTD[s][:, which, tt:tt + 1],
                                      ALU.subtract, ALU.mult)
            return a

        def normalise(s, l, after):
            dve.wait_ge(*pool_step.at("rstd", s, l))
            if after in SELF_LN:
                centred(s, T[s], HB[s], 1).then_inc(*dve_step("h", s, after))
                centred(s, T[s], X[s], 0).then_inc(*dve_step("x", s, after))
            else:
                centred(s, T[s], X[s], 0).then_inc(*dve_step("h", s, after))

        def read_values(s, l):
            dve.wait_ge(*bank_filled.at("v", s, l))
            ps = bank_of("v", s, l)
            dve.wait_ge(*pool_step.at("v_zeros" if l == 4 else "v_ones", s))
            for tt in range(TT):
                a = dve.tensor_tensor(V[s][:, tt, :, 0:D], ps[:, tt, :].rearrange("p (h d) -> p h d", d=D),
                                      rows[:, VROW[l], :].rearrange("p (h d) -> p h d", d=D), ALU.add)
            a.then_inc(*dve_read("v", s, l))

        def partners(s, l):
            for n, kind in enumerate(("q", "k")):
                dve.wait_ge(*bank_filled.at(kind + "2", s, l))
                sin = rope_sin[:, :].unsqueeze(1).to_broadcast([P, CC, S])
                dve.tensor_tensor((HB, T)[n][s][:, :, :], bank_of(kind + "2", s, l)[:, :, :], sin, ALU.mult)\
                   .then_inc(*dve_read(kind + "2", s, l))

        def rotate(s, l):
            done = []
            for n, kind in enumerate(("q", "k")):
                dve.wait_ge(*dve_read.at(kind + "2", s, l))
                dve.wait_ge(*pool_step.at("cos" + kind, s, l))
                done.append(later(dve.tensor_tensor(QK[s][:, n, :, :], QK[s][:, n, :, :], (HB, T)[n][s][:, :, :],
                                                    ALU.add)))
            return done

        def normalise_heads(s, l):
            inverse, done = [], []
            for n, kind in enumerate(("q", "k")):
                dve.wait_ge(*act_read.at(kind + "2", s, l))
                root = (HB, T)[n][s][:, :, :]
                inverse.append(later(dve.reciprocal(root, root)))
            for n in range(2):
                read(inverse[n])
                done.append(later(dve.tensor_tensor(QK[s][:, n, :, :], QK[s][:, n, :, :], (HB, T)[n][s][:, :, :],
                                                    ALU.mult)))
            return done

        def split(s, l, done):
            full = [QK[s][:, n, :, :].rearrange("p a b -> p (a b)") for n in range(2)]
            part = [[SP[s][:, 3 * n + j, :] for j in range(3)] for n in range(2)]
            if done is None:
                for kind in "qk":
                    dve.wait_ge(*act_read.at(kind, s, l))
            else:
                for n in range(2):
                    read(done[n])
                    done[n] = later(dve.tensor_copy(part[n][0], full[n]))
            rest = []
            for n in range(2):
                if done is not None:
                    read(done[n])
                rest.append(later(dve.tensor_tensor(full[n], full[n], part[n][0], ALU.subtract)))
            second = []
            for n in range(2):
                read(rest[n])
                second.append(later(dve.tensor_copy(part[n][1], full[n])))
            for n in range(2):
                read(second[n])
                a = dve.tensor_tensor(part[n][2], full[n], part[n][1], ALU.subtract)
            a.then_inc(*dve_step("split", s, l))

        def maximum(s, l, p):
            dve.wait_ge(*slot_filled.at("max", s, l, p))
            ps = slot_of("max", s, l, p)
            if l in CAUSAL:
                for qt in range(TT):
                    a = dve.tensor_reduce(MX[s][:, 2 * p:2 * p + 2, qt], ps[:, :, qt, 0:(qt + 1) * P], AX.X, ALU.max)
            else:
                a = dve.tensor_reduce(MX[s][:, 2 * p:2 * p + 2, :], ps[:, :, :, :], AX.X, ALU.max)
            a.then_inc(*maxed(s, l, p))

        def maxima_parts(s, l):
            m = MX[s][:, :, :].rearrange("p (h a) q -> p q a h", a=2)
            dve.wait_ge(*maxed.at(s, l, PAIRS - 1))
            then(dve.tensor_scalar(MB[s][:, :, :, 0, :], m, -1.0, None, ALU.mult))
            then(dve.tensor_tensor(m, m, MB[s][:, :, :, 0, :], ALU.add))
            then(dve.tensor_scalar(MB[s][:, :, :, 1, :], m, -1.0, None, ALU.mult))
            then(dve.tensor_tensor(m, m, MB[s][:, :, :, 1, :], ALU.add))
            dve.tensor_scalar(MB[s][:, :, :, 2, :], m, -1.0, None, ALU.mult).then_inc(*dve_step("parts", s, l))

        def outputs(s, l, qt):
            dve.wait_ge(*bank_filled.at("y", s, l, qt))
            ps = bank_of("y", s, l, qt)[:, :, :].rearrange("p a (b e) -> p (a b) e", e=32)
            then(dve.reciprocal(RS[s][:, qt, :].unsqueeze(2), ps[:, :, D:D + 1]))
            dst = HB[s][:, qt, :].rearrange("p (h d) -> p h d", d=D)
            dve.tensor_tensor(dst, ps[:, :, 0:D], RS[s][:, qt, :].unsqueeze(2).to_broadcast([P, H, D]), ALU.mult)\
               .then_inc(*dve_read("y", s, l, qt))

        def residual(s, l):
            t_, x_ = T[s][:, :, :], X[s][:, :, :]
            if l == 0:
                dve.wait_ge(*dve_read.at("y", s, l, TT - 1))
                then(dve.tensor_tensor(t_, x_, HB[s][:, :, :], ALU.add))
                return
            dve.wait_ge(*bank_filled.at("w", s, l))
            ps = bank_of("w", s, l)
            if l == 2:
                dve.tensor_copy(T[s][:, :, 0:SKIP], X[s][:, :, 0:SKIP])
                dve.tensor_tensor(T[s][:, :, SKIP:C], ps[:, :, SKIP:C], X[s][:, :, SKIP:C], ALU.add)\
                   .then_inc(*dve_read("w", s, l))
            else:
                dve.wait_ge(*pool_step.at("xb", s, l))
                dve.tensor_tensor(t_, ps[:, :, :], x_, ALU.add).then_inc(*dve_read("w", s, l))
            dve.wait_ge(*dve_read.at("w", s, l))

        def routing(s):
            g = lambda k: GT[s][:, k, :, :]
            m = lambda k: GM[s][:, k, :]
            wide = lambda k: GM[s][:, k, :].unsqueeze(2).to_broadcast([P, TT, 4])
            dve.wait_ge(*dve_read.at("gate", s, 2))
            then(dve.tensor_tensor(g(3), g(2), wide(0), ALU.is_equal))
            then(dve.tensor_tensor(g(3), g(3), prefer[:, :, :], ALU.mult))
            then(dve.tensor_reduce(m(1), g(3), AX.X, ALU.max))
            then(dve.tensor_tensor(g(4), prefer[:, :, :], wide(1), ALU.is_equal))
            then(dve.tensor_scalar(g(5), g(4), -3.4028235e38, None, ALU.mult))
            then(dve.tensor_tensor(g(5), g(0), g(5), ALU.add))
            then(dve.tensor_reduce(m(2), g(5), AX.X, ALU.max))
            then(dve.tensor_tensor(g(6), g(5), wide(2), ALU.is_equal))
            then(dve.tensor_tensor(g(6), g(6), prefer[:, :, :], ALU.mult))
            then(dve.tensor_reduce(m(3), g(6), AX.X, ALU.max))
            then(dve.tensor_tensor(g(7), prefer[:, :, :], wide(3), ALU.is_equal))
            then(dve.tensor_tensor(g(7), g(7), g(4), ALU.add))
            dve.wait_ge(*act_step.at("gate_exp", s))
            then(dve.tensor_reduce(m(4), g(1), AX.X, ALU.add))
            then(dve.reciprocal(m(4), m(4)))
            then(dve.tensor_tensor(g(8), g(1), wide(4), ALU.mult))
            then(dve.tensor_tensor(g(8), g(8), g(7), ALU.mult))
            then(dve.tensor_reduce(m(5), g(8), AX.X, ALU.add))
            then(dve.tensor_scalar(m(5), m(5), 1e-8, None, ALU.add))
            then(dve.reciprocal(m(5), m(5)))
            then(dve.tensor_tensor(g(9), g(8), wide(5), ALU.mult))

        def read_gate(s):
            dve.wait_ge(*bank_filled.at("gate", s, 2))
            dve.tensor_scalar(GT[s][:, 2, :, :], bank_of("gate", s, 2)[:, :, 0:4], 3.4028235e38, -3.4028235e38,
                              ALU.min, ALU.max).then_inc(*dve_read("gate", s, 2))
            dve.wait_ge(*dve_read.at("gate", s, 2))
            then(dve.tensor_reduce(GM[s][:, 0, :], GT[s][:, 2, :, :], AX.X, ALU.max))
            dve.tensor_tensor(GT[s][:, 0, :, :], GT[s][:, 2, :, :],
                              GM[s][:, 0, :].unsqueeze(2).to_broadcast([P, TT, 4]), ALU.subtract)\
               .then_inc(*dve_step("gate_sub", s))

        def add_expert(s, e):
            dve.wait_ge(*bank_filled.at("down", s, 2, e))
            ps = bank_of("down", s, 2, e)
            for tt in range(TT):
                acc = T[s][:, tt, SKIP:C]
                a = dve.scalar_tensor_tensor(out=acc, in0=ps[:, tt, 0:KEEP], scalar=GT[s][:, 9, tt, e:e + 1], in1=acc,
                                             op0=ALU.mult, op1=ALU.add)
            a.then_inc(*dve_read("down", s, 2, e))
            dve.wait_ge(*dve_read.at("down", s, 2, e))

        with dve.Fori(0, ROUNDS) as i:
            for step, s, l, n in SCHEDULE:
                if step == "context":
                    dve.wait_ge(*ctx_in[s].at(0))
                    statistics(s, HB[s], (s, "c"), False)
                    dve.wait_ge(*pool_step.at("rstd", s, "c"))
                    centred(s, HB[s], HB[s], 0).then_inc(*dve_step("hc", s))
                elif step == "v" and l in VROW:
                    read_values(s, l)
                elif step == "again" and l == 3:
                    partners(s, l)
                elif step == "split":
                    split(s, l, normalise_heads(s, l) if l == 2 else rotate(s, l) if l == 3 else None)
                elif step == "max":
                    maximum(s, l, n)
                elif step == "parts":
                    maxima_parts(s, l)
                elif step == "exp" and l == 4:
                    dve.wait_ge(*exped.at(s, l, n))
                    dve.wait_ge(*group_in[s].at())
                    if n >= 2:
                        dve.wait_ge(*mixing(s, l, n - 2))
                    elif s == 1:
                        dve.wait_ge(*mixing(0, l, PAIRS - 2 + n))
                    dve.tensor_tensor(PR[:, 3 + n % 2, 0, :, :], PR[:, n % 3, 0, :, :], GP[s][:, :, :], ALU.mult)\
                       .then_inc(*dve_step("weighted", s, n))
                elif step == "y":
                    outputs(s, l, n)
                elif step == "w":
                    residual(s, l)
                elif step == "stat":
                    statistics(s, T[s], (s, l), l == 2)
                elif step == "norm" and l == 2:
                    dve.wait_ge(*pool_step.at("rstd", s, 2))
                    for tt in range(TT):
                        a = dve.tensor_scalar(HB[s][:, tt, :], T[s][:, tt, :], RSTD[s][:, 0, tt:tt + 1], None, ALU.mult)
                    a.then_inc(*dve_step("h", s, "f"))
                    dve.wait_ge(*dve_step.at("h", s, "f"))
                    then(dve.tensor_tensor(T[s][:, :, :], T[s][:, :, :], X[s][:, :, :], ALU.add))
                elif step == "norm":
                    normalise(s, l, 3 if l == "f" else l + 1)
                elif step == "gate":
                    read_gate(s)
                elif step == "route":
                    routing(s)
                elif step == "e1b":
                    for half in range(2):
                        dve.wait_ge(*bank_filled.at("e1b", s, 2, half))
                        dve.wait_ge(*act_read.at("e1a", s, 2, half))
                        hid = HIDDEN[3][:, 2 * half:2 * half + 2, :]
                        dve.tensor_tensor(hid, bank_of("e1b", s, 2, half)[:, :, :], hid, ALU.mult)\
                           .then_inc(*dve_read("e1b", s, 2, half))
                elif step == "down":
                    add_expert(s, n)
            finish(dve, i)

    @block.gpsimd
    def _(pool):
        def then(ins):
            ins.then_inc(*pool_chain())
            pool.wait_ge(pool_chain.sem, pool_chain.count)

        def inverse_roots(s, l, eps, again=None):
            pool.wait_ge(*dve_step.at("stat", s, l))
            a = pool.tensor_scalar(VE[s][:, 0, :], MV[s][:, :, 1], eps, None, ALU.add)
            n = 1
            if again is not None:
                a = pool.tensor_scalar(VE[s][:, 1, :], MV[s][:, :, 1], 1.0 + again, eps * again, ALU.mult, ALU.add)
                n = 2
            then(a)
            pool.tensor_tensor(RSTD[s][:, 0:n, :], VE[s][:, 0:n, :], neg_half[:, 0:n, :], ALU.pow)\
                .then_inc(*pool_step("rstd", s, l))

        with pool.Fori(0, ROUNDS) as i:
            for s in range(STREAMS):
                pool.memset(V[s][:, :, :, D:32], 1.0).then_inc(*pool_step("v_ones", s))
            for step, s, l, n in SCHEDULE:
                if step == "context":
                    inverse_roots(s, "c", eps_n)
                    pool.wait_ge(*mask_in[s].at("all"))
                    for dst, src in ((NQ[s], QK[s][:, 0, :, :]), (NK[s], QK[s][:, 1, :, :])):
                        a = pool.tensor_scalar(dst[:, :, :], src.bitcast(I32), 1.0e9, -1.0e9, ALU.mult, ALU.add)
                    a.then_inc(*pool_step("nk", s))
                    then(pool.tensor_scalar(m_col[s][:, :], m_u8[s][:, :], -LOW, LOW, ALU.mult, ALU.add))
                    pool.tensor_scalar(m_row[s][:, :], mr_u8[s][:, :], -LOW, LOW, ALU.mult, ALU.add)\
                        .then_inc(*pool_step("m_row", s))
                    pool.wait_ge(*pool_step.at("m_row", s))
                elif step == "stat":
                    if l == 2:
                        inverse_roots(s, l, eps_f)
                    else:
                        inverse_roots(s, l, eps_n, {0: eps_n, 1: eps_f, "f": eps_n}.get(l))
                elif step == "q" and l == 4:
                    pool.wait_ge(*mixing(s, 3, PAIRS - 1))
                    pool.memset(V[s][:, :, :, D:32], 0.0).then_inc(*pool_step("v_zeros", s))
                elif step == "again" and l == 3:
                    for k, kind in enumerate(("q", "k")):
                        pool.wait_ge(*bank_filled.at(kind + "2", s, l))
                        qk = QK[s][:, k, :, :]
                        pool.tensor_tensor(qk, qk, rope_cos[:, :].unsqueeze(1).to_broadcast([P, CC, S]), ALU.mult)\
                            .then_inc(*pool_step("cos" + kind, s, l))
                elif step == "exp" and l == 4:
                    pool.wait_ge(*exped.at(s, l, n))
                    pool.wait_ge(*group_in[s].at())
                    if n >= 2:
                        pool.wait_ge(*mixing(s, l, n - 2))
                    elif s == 1:
                        pool.wait_ge(*mixing(0, l, PAIRS - 2 + n))
                    pool.tensor_tensor(PR[:, 3 + n % 2, 1, :, :], PR[:, n % 3, 1, :, :], GP[s][:, :, :], ALU.mult)\
                        .then_inc(*pool_step("weighted", s, n))
                elif step == "split" and l in OROW:
                    pool.wait_ge(*dve_step.at("h" if l == 4 else "x", s, l))
                    pool.wait_ge(*bank_filled.at("T", s, l))
                    x_ = X[s][:, :, :]
                    if l == 3:
                        then(pool.tensor_tensor(x_, x_, x_, ALU.add))
                    b_ = rows[:, OROW[l], :].unsqueeze(1).to_broadcast([P, TT, C])
                    pool.tensor_tensor(x_, x_, b_, ALU.add).then_inc(*pool_step("xb", s, l))
            finish(pool, i)

    @block.sync
    def _(sp):
        flat = "b p t c -> (b p) t c"

        def stack(s, l):
            sp.wait_ge(*dve_step.at("split", s, l))
            for j, (a, b) in enumerate(zip(Q_PARTS, K_PARTS)):
                sp.dma_start(QKS[s][D * j:D * (j + 1), :, :, :, :], SP[s][:, a:3 + b + 1:3 + b - a, :])\
                    .then_inc(*stack_in[s](l, j))

        with sp.Fori(0, ROUNDS) as i:
            for s in range(STREAMS):
                at = bass.ds(2 * i + s, 1)
                sp.dma_start(HB[s][:, :, :], t["ctx"][at].rearrange(flat)).then_inc(*ctx_in[s](0))
                sp.dma_start(X[s][:, :, :], t["x"][at].rearrange(flat)).then_inc(*x_in[s]())
                sp.dma_start(QK[s][:, 0, :, :].bitcast(I32), t["mask"][at].rearrange(flat)).then_inc(*mask_in[s]("q"))
                sp.dma_start(QK[s][:, 1, :, :].bitcast(I32), t["maskT"][at].rearrange(flat)).then_inc(*mask_in[s]("k"))
                sp.dma_start(m_u8[s][:, :], t["m_cols"][at].rearrange("b p t -> (b p) t")).then_inc(*mask_in[s]("c"))
                sp.dma_start(mr_u8[s][:, :], t["m_rows"][at].rearrange("b o t -> (b o) t"))\
                    .then_inc(*mask_in[s]("all"))
            for step, s, l, n in SCHEDULE:
                at = bass.ds(2 * i + s, 1)
                if step == "split":
                    stack(s, l)
                elif step == "shift":
                    sp.wait_ge(*act_read.at("neg", s, l))
                    for a in range(2):
                        rows_of = MT[s][a * SHIFT * PAIRS:(a + 1) * SHIFT * PAIRS, :]
                        sp.dma_start(QKS[s][ROWS:ROWS + SHIFT, :, 0, a, :], rows_of).then_inc(*shift_in[s](l, a))
                elif step == "T" and l == 2:
                    sp.wait_ge(*bank_filled.at("v", s, 1))
                    sp.dma_start(GP[s][:, :, :], t["gpT"][at].rearrange(flat)).then_inc(*group_in[s]())
                elif step == "T" and l == 4:
                    sp.wait_ge(*dve_step.at("h", s, 4))
                    sp.dma_start(T[s][:, :, :], t["ctxT"][at].rearrange(flat)).then_inc(*ctx_in[s](4))
                elif step == "out":
                    sp.wait_ge(*dve_step.at("h", s, LAYERS))
                    rows_out = x5_dram.rearrange("(b t p) c -> b p t c", t=TT, p=P)[at]
                    sp.dma_start(rows_out.rearrange(flat), X[s][:, :, :]).then_inc(*x_out(s))
            sp.wait_ge(*x_out.at(1))
            sp.wait_ge(arrived, 4 * i + 4)
            sp.sem_inc(rounds_ended, 1)
            for sem in work:
                sp.sem_clear(sem)
            sp.sem_inc(released, 1)


def routed_mixture(nc, ctx, t, known, x5_dram, slots_dram, expert_dram):
    def sb(name, shape, dt=F32):
        return ctx.enter_context(nc.sbuf_tensor(name, shape, dt))

    def signal(name, step=1):
        return Signal(name, ctx.enter_context(nc.semaphore(name)), known, step)

    G = B * S // P
    SLOTS = E1 * CAP
    ST = SLOTS // P
    CH = [(0, P), (P, P), (2 * P, CAP - 2 * P)]
    FC = DFF // P

    x5 = sb("x5", [P, G, C])
    xt = sb("xt", [P, 2, CC, P])
    ident = sb("ident2", [P, P])
    upto = sb("upto", [P, P])
    upto_b = sb("upto_b", [P, P], BF16)
    ones_b = sb("ones_b", [P, P], BF16)
    wg = sb("wg", [P, CC, E1])
    prefer = sb("prefer8", [P, G, E1])
    zero = sb("zero", [P, C])
    lg = sb("lg", [P, 5, G, E1])
    oh = sb("oh", [P, G, E1], BF16)
    run = sb("run", [P, 2, G, E1])
    tot = sb("tot", [P, G, E1])
    red = sb("red", [P, 8, G])
    idx = sb("idx", [P, G], U32)
    w1 = [sb(f"w1_{k}", [P, CC, DFF]) for k in range(2)]
    w2 = [sb(f"w2_{k}", [P, FC, C]) for k in range(2)]
    b1 = sb("b1", [P, E1, FC])
    b2 = sb("b2", [P, E1, C])
    rows = sb("slot_rows_sb", [P, ST, C])
    xs = sb("xs", [P, CC, SLOTS])
    hid = [sb(f"hid{k}", [P, FC, CAP]) for k in range(2)]
    eo = sb("eo", [P, 3, C])
    back = sb("back", [P, G, C])
    st = sb("st2", [P, G, 6])
    mv = sb("mv2", [P, G, 2])
    ve = sb("ve2", [P, G])
    rstd = sb("rstd2", [P, G])
    half = sb("neg_half2", [P, G])
    BANK = [ctx.enter_context(nc.psum_tensor(f"pbank{i}", [P, 512], F32)) for i in range(8)]

    x_in = signal("x5_in", 16)
    const_in = signal("const_in", 16)
    cleared = signal("slots_cleared", 16)
    scattered = signal("scattered", 16)
    slots_in = [signal(f"slots_in{k}", 16) for k in range(4)]
    w_in = [signal(f"w_in{k}", 16) for k in range(2)]
    expert_out = [signal(f"expert_out{k}", 16) for k in range(3)]
    gathered = signal("gathered", 16)
    written = signal("written", 16)
    pe_turned = signal("pe_turned")
    pe_logits = signal("pe_logits")
    pe_counts = signal("pe_counts")
    pe_rows = signal("pe_rows")
    pe_up = signal("pe_up")
    pe_down = signal("pe_down")
    act_turned = signal("act_turned")
    act_exp = signal("act_exp")
    act_rows = signal("act_rows")
    act_up = signal("act_up")
    dve_chain = signal("dve_chain2")
    dve_done = signal("dve_done")
    dve_down = signal("dve_down")
    dve_out = signal("dve_out")
    pool_done = signal("pool_done")
    pool_chain = signal("pool_chain2")

    block = ctx.enter_context(nc.Block())
    UPS = [BANK[k] for k in range(2, 5)]
    DOWNS = [BANK[k] for k in range(5, 8)]

    @block.sync
    def _(sp):
        xv = x5_dram.rearrange("(g p) c -> p g c", p=P)
        for k in range(4):
            sp.dma_start(x5[:, 4 * k:4 * k + 4, :], xv[:, 4 * k:4 * k + 4, :]).then_inc(*x_in(k))
        for dst, name in ((ident, "ident"), (upto, "upto"), (wg, "wg"), (prefer, "prefer8"), (b1, "b1"), (b2, "b2")):
            sp.dma_start(dst.ap(), t[name]).then_inc(*const_in(name))

        def weights(e):
            if e >= 2:
                sp.wait_ge(*pe_down.at(e - 2, 2))
            sp.dma_start(w1[e % 2][:, :, :], t["w1"][e]).then_inc(*w_in[e % 2](e, 1))
            sp.dma_start(w2[e % 2][:, :, :], t["w2"][e]).then_inc(*w_in[e % 2](e, 2))

        weights(0)
        weights(1)
        sp.wait_ge(*scattered.at(G - 1))
        sv = slots_dram.rearrange("(n p) c -> p n c", p=P)
        for k in range(4):
            sp.dma_start(rows[:, 5 * k:5 * k + 5, :], sv[:, 5 * k:5 * k + 5, :]).then_inc(*slots_in[k]("in"))
        for e in range(E1):
            for j, (c0, m) in enumerate(CH):
                sp.wait_ge(*dve_down.at(e, j))
                sp.dma_start(expert_dram[e * CAP + c0:e * CAP + c0 + m, :], eo[0:m, j, :])\
                    .then_inc(*expert_out[j](e))
            if e + 2 < E1:
                weights(e + 2)
        for g in range(G):
            sp.wait_ge(*dve_out.at(g))
            sp.dma_start(t["out"].rearrange("(g p) c -> g p c", p=P)[g], back[:, g, :]).then_inc(*written(g))
        sp.wait_ge(*written.at(G - 1))

    def logits(pe, g):
        pe.wait_ge(*act_turned.at(g))
        for ci in range(CC):
            mm = pe.matmul(BANK[2][:, g * E1:(g + 1) * E1], xt[:, g % 2, ci, :], wg[:, ci, :],
                           start=ci == 0, stop=ci == CC - 1)
        mm.then_inc(*pe_logits(g))

    @block.tensor
    def _(pe):
        pe.wait_ge(*const_in.at("b2"))
        for g in range(G):
            pe.wait_ge(*x_in.at(3))
            if g >= 2:
                pe.wait_ge(*act_turned.at(g - 2))
            for c in range(CC):
                mm = pe.transpose(BANK[g % 2][:, c * P:(c + 1) * P], x5[:, g, c * P:(c + 1) * P], ident[:, :])
            mm.then_inc(*pe_turned(g))
            if g >= 1:
                logits(pe, g - 1)
        logits(pe, G - 1)
        pe.wait_ge(*dve_done.at("onehot"))
        flat = oh[:, :, :].rearrange("p g e -> p (g e)")
        pe.matmul(BANK[3][:, 0:P], upto_b[:, :], flat, start=True, stop=True)
        pe.matmul(BANK[4][:, 0:P], ones_b[:, :], flat, start=True, stop=True).then_inc(*pe_counts("all"))
        for n in range(ST // 2):
            pe.wait_ge(*slots_in[(2 * n) // 5].at("in"))
            pe.wait_ge(*slots_in[(2 * n + 1) // 5].at("in"))
            if n >= 2:
                pe.wait_ge(*act_rows.at(n - 2))
            for c in range(CC):
                for k in range(2):
                    mm = pe.transpose(BANK[n % 2][:, (2 * c + k) * P:(2 * c + k + 1) * P],
                                      rows[:, 2 * n + k, c * P:(c + 1) * P], ident[:, :])
            mm.then_inc(*pe_rows(n))
        ups = 0
        for e in range(E1):
            pe.wait_ge(*act_rows.at(min(ST // 2 - 1, ((e + 1) * CAP - 1) // (2 * P))))
            pe.wait_ge(*w_in[e % 2].at(e, 2))
            for f in range(FC):
                if ups >= 3:
                    pe.wait_ge(*act_up.at(*divmod(ups - 3, FC)))
                elif ups in (1, 2):
                    pe.wait_ge(*dve_done.at("counted"))
                for ci in range(CC):
                    mm = pe.matmul(UPS[ups % 3][:, 0:CAP], w1[e % 2][:, ci, f * P:(f + 1) * P],
                                   xs[:, ci, e * CAP:(e + 1) * CAP], start=ci == 0, stop=ci == CC - 1)
                mm.then_inc(*pe_up(e, f))
                ups += 1
            pe.wait_ge(*act_up.at(e, FC - 1))
            for j, (c0, m) in enumerate(CH):
                if e >= 1:
                    pe.wait_ge(*dve_down.at(e - 1, j))
                for f in range(FC):
                    mm = pe.matmul(DOWNS[j][0:m, 0:C], hid[e % 2][:, f, c0:c0 + m], w2[e % 2][:, f, :],
                                   start=f == 0, stop=f == FC - 1)
                mm.then_inc(*pe_down(e, j))

    @block.scalar
    def _(act):
        for g in range(G):
            act.wait_ge(*pe_turned.at(g))
            if g >= 2:
                act.wait_ge(*pe_logits.at(g - 2))
            act.activation(xt[:, g % 2, :, :].rearrange("p a b -> p (a b)"), BANK[g % 2][:, 0:2 * P], ACT.Copy)\
               .then_inc(*act_turned(g))
        act.wait_ge(*dve_done.at("sub"))
        act.activation(lg[:, 1, :, :], lg[:, 0, :, :], ACT.Exp).then_inc(*act_exp("e"))
        for n in range(ST // 2):
            act.wait_ge(*pe_rows.at(n))
            act.activation(xs[:, :, 2 * n * P:(2 * n + 2) * P], BANK[n % 2][:, :].rearrange("p (a b) -> p a b", a=CC),
                           ACT.Copy).then_inc(*act_rows(n))
        for e in range(E1):
            for f in range(FC):
                act.wait_ge(*pe_up.at(e, f))
                if e >= 2:
                    act.wait_ge(*pe_down.at(e - 2, 2))
                act.activation(hid[e % 2][:, f, :], UPS[(e * FC + f) % 3][:, 0:CAP], ACT.Relu,
                               bias=b1[:, e, f:f + 1]).then_inc(*act_up(e, f))

    @block.vector
    def _(dve):
        def then(ins):
            ins.then_inc(*dve_chain())
            dve.wait_ge(dve_chain.sem, dve_chain.count)

        def wide(k):
            return red[:, k, :].unsqueeze(2).to_broadcast([P, G, E1])

        L = lambda k: lg[:, k, :, :]
        R = lambda k: red[:, k, :]
        dve.memset(zero[:, :], 0.0).then_inc(*dve_done("zero"))
        dve.memset(ones_b[:, :], 1.0)
        dve.memset(back[:, :, :], 0.0).then_inc(*dve_done("back"))
        dve.memset(half[:, :], -0.5).then_inc(*dve_done("half"))
        dve.wait_ge(*const_in.at("b2"))
        then(dve.tensor_copy(upto_b[:, :], upto[:, :]))
        dve.wait_ge(*pe_logits.at(G - 1))
        then(dve.tensor_copy(L(2), BANK[2][:, 0:P].rearrange("p (g e) -> p g e", e=E1)))
        then(dve.tensor_reduce(R(0), L(2), AX.X, ALU.max))
        dve.tensor_tensor(L(0), L(2), wide(0), ALU.subtract).then_inc(*dve_done("sub"))
        then(dve.tensor_tensor(L(3), L(2), wide(0), ALU.is_equal))
        then(dve.tensor_tensor(L(3), L(3), prefer[:, :, :], ALU.mult))
        then(dve.tensor_reduce(R(1), L(3), AX.X, ALU.max))
        then(dve.tensor_tensor(L(4), prefer[:, :, :], wide(1), ALU.is_equal))
        dve.tensor_copy(oh[:, :, :], L(4)).then_inc(*dve_done("onehot"))
        dve.wait_ge(*act_exp.at("e"))
        then(dve.tensor_reduce(R(2), L(1), AX.X, ALU.add))
        then(dve.reciprocal(R(2), R(2)))
        dve.wait_ge(*pe_counts.at("all"))
        tv = BANK[4][:, 0:P].rearrange("p (g e) -> p g e", e=E1)
        then(dve.tensor_copy(tot[:, :, :], tv))
        src, k, n = tot[:, :, :], 1, 0
        while k < G:
            dst = run[:, n % 2, :, :]
            dve.tensor_copy(dst[:, 0:k, :], src[:, 0:k, :])
            then(dve.tensor_tensor(dst[:, k:G, :], src[:, k:G, :], src[:, 0:G - k, :], ALU.add))
            src, k, n = dst, 2 * k, n + 1
        then(dve.tensor_tensor(src, src, tot[:, :, :], ALU.subtract))
        then(dve.tensor_tensor(src, src, BANK[3][:, 0:P].rearrange("p (g e) -> p g e", e=E1), ALU.add))
        then(dve.tensor_tensor(src, src, L(4), ALU.mult))
        a = dve.tensor_reduce(R(3), src, AX.X, ALU.add)
        a.then_inc(*dve_done("counted"))
        dve.wait_ge(*dve_done.at("counted"))
        then(dve.tensor_scalar(R(4), R(1), -float(CAP), float(E1 * CAP - 1), ALU.mult, ALU.add))
        then(dve.tensor_tensor(R(4), R(4), R(3), ALU.add))
        then(dve.tensor_scalar(R(5), R(3), float(CAP), float(2 * SLOTS), ALU.is_gt, ALU.mult))
        then(dve.tensor_tensor(R(4), R(4), R(5), ALU.add))
        dve.tensor_copy(idx[:, :], R(4)).then_inc(*dve_done("idx"))
        for e in range(E1):
            for j, (c0, m) in enumerate(CH):
                dve.wait_ge(*pe_down.at(e, j))
                if e >= 1:
                    dve.wait_ge(*expert_out[j].at(e - 1))
                dve.tensor_tensor(eo[0:m, j, :], DOWNS[j][0:m, 0:C], b2[0:m, e, :], ALU.add)\
                   .then_inc(*dve_down(e, j))
        dve.wait_ge(*gathered.at(G - 1))
        for g in range(G):
            a = dve.scalar_tensor_tensor(out=x5[:, g, :], in0=back[:, g, :], scalar=red[:, 2, g:g + 1],
                                         in1=x5[:, g, :], op0=ALU.mult, op1=ALU.add)
        then(a)
        for g in range(G):
            a = dve.bn_stats(st[:, g, :], x5[:, g, :])
        then(a)
        for g in range(G):
            a = dve.bn_aggr(mv[:, g, :], st[:, g, :])
        a.then_inc(*dve_done("stats"))
        dve.wait_ge(*pool_done.at("rstd"))
        for g in range(G):
            dve.tensor_scalar(back[:, g, :], x5[:, g, :], mv[:, g, 0:1], rstd[:, g:g + 1], ALU.subtract, ALU.mult)\
               .then_inc(*dve_out(g))

    @block.gpsimd
    def _(pool):
        pool.wait_ge(*dve_done.at("zero"))
        for n in range(ST):
            pool.dma_start(slots_dram[n * P:(n + 1) * P, :], zero[:, :]).then_inc(*cleared(n))
        pool.wait_ge(*cleared.at(ST - 1))
        pool.wait_ge(*dve_done.at("idx"))
        for g in range(G):
            pool.indirect_dma_start(slots_dram, bass.IndirectOffsetOnAxis(ap=idx[:, g:g + 1], axis=0), x5[:, g, :],
                                    None, bounds_check=SLOTS - 1, oob_is_err=False).then_inc(*scattered(g))
        for j in range(3):
            pool.wait_ge(*expert_out[j].at(E1 - 1))
        pool.wait_ge(*dve_done.at("back"))
        for g in range(G):
            pool.indirect_dma_start(back[:, g, :], None, expert_dram,
                                    bass.IndirectOffsetOnAxis(ap=idx[:, g:g + 1], axis=0),
                                    bounds_check=SLOTS - 1, oob_is_err=False).then_inc(*gathered(g))
        pool.wait_ge(*dve_done.at("stats"))
        a = pool.tensor_scalar(ve[:, :], mv[:, :, 1], 1e-5, None, ALU.add)
        a.then_inc(*pool_chain())
        pool.wait_ge(pool_chain.sem, pool_chain.count)
        pool.tensor_tensor(rstd[:, :], ve[:, :], half[:, :], ALU.pow).then_inc(*pool_done("rstd"))


def layouts(inp):
    a = {k: np.asarray(v) for k, v in inp.items()}
    f = np.float32
    order = np.array([(hh * 2 + c) * D + d for c in range(CC) for d in range(D) for hh in range(H // CC)])
    chunked = lambda w: w.reshape(-1, P, w.shape[1]).transpose(1, 0, 2)
    w0 = a["L0_attn_W"]
    qkv = [(w0[:C].T, w0[C:2 * C].T, w0[2 * C:].T),
           (a["L0_xattn_Wq"].T, a["L0_xattn_Wk"].T, a["L0_xattn_Wv"].T),
           (a["L0_ffn_wq"].T, a["L0_ffn_wk"].T, a["L0_ffn_wv"].T),
           (a["L1_attn_Wq"].T, a["L1_attn_Wk"].T, a["L1_attn_Wv"].T),
           (a["L1_xattn_wq_k"], a["L1_xattn_wk_k"], a["L1_xattn_wv_k"])]
    ws = []
    for q, k, v in qkv:
        ws += [q[:, order], k[:, order], v]
    ws += [a["L0_xattn_Wo"].T, a["L0_ffn_wo"].T, a["L1_attn_Wo"].T, a["L1_xattn_wo_k"]]
    out = {"proj": np.stack([chunked(w) for w in ws], 1)}
    two = lambda v: v.reshape(2, P).T
    b0 = a["L0_attn_b"]
    cs = [two(a["L0_xattn_g1"]), two(a["L0_xattn_b1"]), two(a["L0_xattn_g2"]), two(a["L0_xattn_b2"]),
          two(a["L0_ffn_n1_w"]), two(a["L0_ffn_n2_w"]), two(a["L1_attn_ln_w"]), two(a["L1_attn_ln_b"]),
          two(b0[:C][order]), two(b0[C:2 * C][order]), two(a["L1_attn_bq"][order]), two(a["L1_attn_bk"][order]),
          two(a["L1_xattn_wq_b"][order]), two(a["L1_xattn_wk_b"][order]),
          np.stack([np.repeat(a["L0_ffn_qn_w"], 8), np.repeat(a["L0_ffn_kn_w"], 8)], 1)]
    cs.append(np.zeros((P, 32 - 2 * len(cs)), f))
    out["cols"] = np.concatenate(cs, 1)
    rs = [b0[2 * C:], a["L0_xattn_bo"], a["L1_attn_bv"], a["L1_attn_bo"], a["L1_xattn_wv_b"], a["L1_xattn_wo_b"]]
    out["rows"] = np.broadcast_to(np.stack(rs)[None], (P, 6, C))
    for name, src in (("up0", "e0_up"), ("up1a", "e1_w1"), ("up1b", "e1_w2"), ("l1", "e2_l1"), ("l2", "e2_l2"),
                      ("l3", "e2_l3"), ("down3", "e3_down"), ("up3", "e3_up"), ("gate", "gate_w")):
        out[name] = chunked(a["L0_ffn_" + src].T)
    out["downs"] = np.stack([chunked(a["L0_ffn_" + n].T[:, SKIP:]) for n in ("e0_down", "e1_down", "e2_l4", "e3_out")], 1)
    out["x"], out["ctx"] = a["x"], a["ctx_1024"]
    out["ctxT"] = a["ctx_1024"].transpose(0, 2, 1)
    m = a["mask_BxSxS2_ik1"]
    tiles = lambda v: v.reshape(B, TT, P, S).transpose(0, 2, 1, 3)
    out["mask"] = tiles(m)
    out["maskT"] = tiles(m.transpose(0, 2, 1))
    out["gpT"] = tiles(a["fside_BxSxS2_0"].transpose(0, 2, 1))
    mb = np.ascontiguousarray(a["mask_BxS2_bf1"]).view(np.uint8)
    out["m_cols"] = mb.reshape(B, TT, P).transpose(0, 2, 1)
    out["m_rows"] = mb.reshape(B, 1, S)
    out["wg"] = chunked(a["L1_ffn_wg"])
    out["w1"] = a["L1_ffn_w1"].reshape(E1, CC, P, DFF).transpose(0, 2, 1, 3)
    out["w2"] = a["L1_ffn_w2"].reshape(E1, DFF // P, P, C).transpose(0, 2, 1, 3)
    out["b1"] = a["L1_ffn_b1"].reshape(E1, DFF // P, P).transpose(2, 0, 1)
    out["b2"] = np.broadcast_to(a["L1_ffn_b2"][None], (P, E1, C))
    i = np.arange(P)
    out["ident"] = np.eye(P, dtype=f)
    out["rope_swap"] = (i[:, None] == (i[None, :] ^ (H // CC))).astype(f)
    out["head_ones"] = (i[:, None] % (H // CC) == i[None, :] % (H // CC)).astype(f)
    out["causal_q"] = np.where(i[None, :] > i[:, None], f(LOW), f(0)).astype(f)
    out["causal_k"] = np.ascontiguousarray(out["causal_q"].T)
    out["upto"] = (i[:, None] <= i[None, :]).astype(f)
    freq = (f(1.0) / np.power(f(10000.0), np.arange(0, D, 2, dtype=f) / f(D))).astype(f)
    angle = (np.arange(S, dtype=f)[None, :] * freq[:, None]).astype(f)
    d = i // (H // CC)
    out["rope_cos"] = np.cos(angle)[d // 2].astype(f)
    out["rope_sin"] = (np.sin(angle)[d // 2] * np.where(d % 2 == 0, -1.0, 1.0)[:, None]).astype(f)
    out["prefer"] = np.broadcast_to(np.array([4, 3, 2, 1], f), (P, TT, 4))
    out["prefer8"] = np.broadcast_to(np.arange(E1, 0, -1).astype(f), (P, B * S // P, E1))
    return {k: np.ascontiguousarray(v) for k, v in out.items()}


def program(nc, arrays, known):
    t = {}
    for name, v in arrays.items():
        t[name] = nc.dram_tensor(f"in_{name}", v.shape, mybir.dt.from_np(v.dtype), kind="ExternalInput").ap()
    t["out"] = nc.dram_tensor("out_x", [B * S, C], F32, kind="ExternalOutput").ap()
    for name in ("x", "ctx", "ctxT"):
        t[name] = t[name].rearrange("b (t p) c -> b p t c", p=P)
    build(nc, t, known)
    return nc


def kernel(**inputs):
    import concourse.bacc as bacc
    from concourse.bass_utils import run_bass_kernel_spmd
    arrays = layouts(inputs)
    known = {"pass": False}
    program(bacc.Bacc("TRN2", target_bir_lowering=False, num_devices=1), arrays, known)
    known["pass"] = True
    nc = program(bacc.Bacc("TRN2", target_bir_lowering=False, num_devices=1), arrays, known)
    r = run_bass_kernel_spmd(nc, [{f"in_{k}": v for k, v in arrays.items()}], core_ids=[0])
    return r.results[0]["out_x"].reshape(B, S, C)
```

```python
from contextlib import ExitStack

import numpy as np

import concourse.bass as bass
from concourse import mybir

F32 = mybir.dt.float32
F32R = mybir.dt.float32r
BF16 = mybir.dt.bfloat16
I32 = mybir.dt.int32
U32 = mybir.dt.uint32
U8 = mybir.dt.uint8
ALU = mybir.AluOpType
ACT = mybir.ActivationFunctionType
AX = mybir.AxisListType

P = 128
B, S, C = 8, 256, 256
H, D = 16, 16
CC = C // P
TT = S // P
PAIRS = H // 2
LAYERS = 5
STREAMS = 2
HID = 512
E1, DFF, CAP = 8, 1024, int(1.25 * B * S / 8)
KEEP = 192
SKIP = C - KEEP
Q_PARTS = (0, 0, 1, 1, 0, 2)
K_PARTS = (0, 1, 0, 1, 2, 0)
ROWS = 16 * len(Q_PARTS)
SHIFT = 3
LOW = -1.0e30
CAUSAL = (0, 2)
SELF_LN = (1, 2, 3)


class Signal:

    def __init__(self, name, sem, known, step=1):
        self.name, self.sem, self.known, self.step, self.count = name, sem, known, step, 0

    def __call__(self, *label):
        key = self.name, self.known["part"], label
        self.count += self.step
        assert self.known["pass"] or not label or key not in self.known, key
        self.known[key] = self.count
        return self.sem, self.step

    def at(self, *label):
        key = self.name, self.known["part"], label
        assert not self.known["pass"] or key in self.known, key
        return self.sem, self.known.get(key, self.step)


def build(nc, t, known):
    known["part"] = "first"
    outer = ExitStack()
    with outer:
        x5_dram = nc.dram_tensor("x5_rows", [B * S, C], F32, kind="Internal").ap()
        slots_dram = nc.dram_tensor("slot_rows", [E1 * CAP, C], F32, kind="Internal").ap()
        expert_dram = nc.dram_tensor("expert_rows", [E1 * CAP, C], F32, kind="Internal").ap()
        with ExitStack() as ctx:
            attention_layers(nc, ctx, t, known, x5_dram)
        known["part"] = "routed"
        with ExitStack() as ctx:
            routed_mixture(nc, ctx, t, known, x5_dram, slots_dram, expert_dram)


START, PARTS, SHIFTED, EXP = -1, PAIRS, PAIRS + 1, PAIRS + 2
OVER = {0: 0, 1: 1, 2: 0, 3: 1, 4: 1}


def schedule():
    def between(s, l):
        n = l + 1
        if l == 0:
            steps = {START: ["y", "y1", "w"], 1: ["k", "stat"], 4: ["norm"], 6: ["T"], SHIFTED: ["q"], EXP: ["split"]}
        elif l == 1:
            steps = {START: ["y", "y1"], 2: ["yT"], 3: ["w", "stat"], 5: ["norm"], 7: ["T"], SHIFTED: ["q", "k"],
                     EXP: ["again"], EXP + 2: ["spread", "split"]}
        elif l == 2:
            steps = {START: ["y", "y1"], 2: ["yT"], 3: ["w"], 4: ["stat"], 5: ["norm"], 7: ["Tf"],
                     SHIFTED: ["gate", "e0", "route"], EXP: ["e3a"], EXP + 1: ["down"]}
        elif l == 3:
            steps = {START: ["y", "y1"], 2: ["yT"], 3: ["w"], 4: ["stat"], 5: ["norm"], 7: ["T"], SHIFTED: ["k", "q"],
                     EXP: ["split"]}
        else:
            steps = {START: ["y", "y1"], 2: ["yT"], 3: ["w"], 4: ["stat"], 5: ["norm"], 7: ["out"]}
        layer = {x: n for x in ("T", "q", "k", "again", "spread", "split")}
        named = {"y1": ("y", s, l, 1), "Tf": ("T", s, "f", 0)}
        return {place: [named.get(x, (x, s, layer.get(x, l), 0)) for x in xs] for place, xs in steps.items()}

    def begin(s, places=(0, 0, 0, 0, 2, 0, 1, SHIFTED, SHIFTED)):
        steps = (("ones", s, 0, 0), ("load", s, 0, "ctx"), ("load", s, 0, "x"), ("context", s, 0, 0), ("TC", s, 0, 0), ("T", s, 0, 0),
                 ("q", s, 0, 0), ("k", s, 0, 0), ("split", s, 0, 0))
        at = {}
        for place, step in zip(places, steps):
            at.setdefault(place, []).append(step)
        return at

    def merged(*ats):
        return {place: sum([at.get(place, []) for at in ats], []) for at in ats for place in at}

    def after_experts(s, places):
        steps = [("stat", s, "f", 0), ("norm", s, "f", 0)] + [(x, s, 3, 0) for x in ("T", "q", "k", "again", "split")]
        return {p: [x] for p, x in zip(places, steps)}

    def attend(s, l, other, begun=True, then=None):
        yield from other.get(START, ())
        for p in range(OVER[l] if begun else 0, PAIRS):
            yield ("max", s, l, p)
            yield from other.get(p, ())
        yield ("parts", s, l, 0)
        yield from other.get(PARTS, ())
        yield ("v", s, l, 0)
        yield ("shift", s, l, 0)
        yield ("v read", s, l, 0)
        yield from other.get(SHIFTED, ())
        for p in range(PAIRS):
            yield ("exp", s, l, p)
            if then and p >= PAIRS - OVER[then[1]]:
                yield ("max", *then, p - PAIRS + OVER[then[1]])
            if p >= 2:
                yield ("mix", s, l, p - 2)
            yield from other.get(EXP + p, ())
        yield ("mix", s, l, PAIRS - 2)
        yield ("mix", s, l, PAIRS - 1)

    def experts(s, other, names):
        places = PLACES[len(names)]
        for n, (name, e) in enumerate(names):
            yield (name, s, 2, e)
            for k in places[n]:
                yield from other.get(k, ())

    FIRST = [("e2a", 0), ("e3b", 0), ("e2b", 0), ("down", 3), ("e2c", 0), ("e1a", 0), ("down", 2), ("e1b", 0),
             ("down", 1)]
    SECOND = [("e0", 0), ("e2a", 0), ("e3a", 0), ("down", 0), ("e2b", 0), ("e3b", 0), ("e2c", 0), ("down", 3),
              ("e1a", 0), ("down", 2), ("e1b", 0), ("down", 1)]
    PLACES = {9: [[START], [2], [3], [4, 5], [7], [SHIFTED], [], [], []],
              12: [[0], [1], [3], [4], [5], [6, 7], [8], [], [], [], [], []]}
    first = sum(begin(0).values(), [])
    order = [("load", 1, 0, "ctx"), ("load", 1, 0, "x"), ("ones", 1, 0, 0)]
    order += attend(0, 0, {k: [x for x in v if x[0] not in ("load", "ones")] for k, v in begin(1, (0, 0, 0, 2, EXP + 2, 3, 4, SHIFTED, EXP)).items()},
                    begun=False, then=(1, 0))
    order += attend(1, 0, between(0, 0), then=(0, 1))
    order += attend(0, 1, between(1, 0), then=(1, 1))
    order += attend(1, 1, between(0, 1), then=(0, 2))
    order += attend(0, 2, between(1, 1), then=(1, 2))
    order += attend(1, 2, between(0, 2))
    kept = {k: [x for x in v if x[0] not in ("e0", "e3a", "down")] for k, v in between(1, 2).items()}
    order += experts(0, kept, FIRST)
    order += experts(1, after_experts(0, (0, 1, 3, 4, 5, 6, 7)), SECOND)
    order += attend(0, 3, after_experts(1, (0, 1, 3, 4, 5, PARTS, EXP)), begun=False, then=(1, 3))
    order += attend(1, 3, between(0, 3), then=(0, 4))
    order += attend(0, 4, between(1, 3), then=(1, 4))
    order += attend(1, 4, merged(between(0, 4), begin(0, (8, 3, 7, PARTS, EXP, EXP + 1, EXP + 2, EXP + 3, EXP + 4))))
    for _, steps in sorted(between(1, 4).items()):
        order += steps
    return first, order


def attention_layers(nc, ctx, t, known, x5_dram):
    def sb(name, shape, dt=F32):
        return ctx.enter_context(nc.sbuf_tensor(name, shape, dt))

    work, signals = [], []

    def signal(name, step=1):
        sem = ctx.enter_context(nc.semaphore(name))
        work.append(sem)
        signals.append(Signal(name, sem, known, step))
        return signals[-1]

    ident = sb("ident", [P, P])
    ident_b = sb("ident_b", [P, P], BF16)
    causal_q = sb("causal_q", [P, P], BF16)
    causal_k = sb("causal_k", [P, P], BF16)
    rope_swap = sb("rope_swap", [P, P])
    head_sum = sb("head_sum", [P, 2 * CC, 2 * H])
    head_spread = sb("head_spread", [2 * H, 2 * CC, P])
    rope_cos = sb("rope_cos", [P, S])
    rope_sin = sb("rope_sin", [P, S])
    ones_row = sb("ones_row", [1, P], BF16)
    sum_cols = sb("sum_cols", [P, 32])
    neg_half = sb("neg_half", [P, 2, TT])
    eps_col = sb("eps_col", [P, 1])
    cols = sb("cols", [P, 32])
    rows = sb("rows", [P, 6, C])
    proj = sb("proj", [P, 19, CC, C])
    up0 = sb("up0", [P, 2, HID])
    up1a = sb("up1a", [P, 2, HID])
    up1b = sb("up1b", [P, 2, HID])
    l1 = sb("l1", [P, 2, HID])
    l2 = sb("l2", [P, 4, HID])
    l3 = sb("l3", [P, 4, HID])
    down3 = sb("down3", [P, 2, C])
    up3 = sb("up3", [P, 2, HID])
    downs = sb("downs", [P, 4, 4, KEEP])
    gate = sb("gate", [P, CC, 4])
    prefer = sb("prefer", [P, TT, 4])

    X = [sb(f"x{s}", [P, TT, C]) for s in range(STREAMS)]
    HB = [sb(f"h{s}", [P, TT, C]) for s in range(STREAMS)]
    HT = [sb(f"hT{s}", [P, CC, S]) for s in range(STREAMS)]
    T = [sb(f"t{s}", [P, TT, C]) for s in range(STREAMS)]
    QK = [sb(f"qk{s}", [P, 2, CC, S]) for s in range(STREAMS)]
    SP = sb("split", [P, 6, CC * S], BF16)
    QKS = [sb(f"stack{s}", [ROWS + SHIFT, H // 2, 2, 2, S], BF16) for s in range(STREAMS)]
    V = [sb(f"v{s}", [P, TT, H, 32]) for s in range(STREAMS)]
    GP = [sb(f"gp{s}", [P, TT, S]) for s in range(STREAMS)]
    NQ = [sb(f"nq{s}", [P, TT, S], BF16) for s in range(STREAMS)]
    NK = [sb(f"nk{s}", [P, TT, S], BF16) for s in range(STREAMS)]
    PR = sb("probs", [P, 5, 2, TT, S])
    HIDDEN = [PR[:, k, :, :, :].rearrange("p a b c -> p (a b) c") for k in range(5)]
    m_u8 = [sb(f"m_u8{s}", [P, TT], U8) for s in range(STREAMS)]
    mr_u8 = [sb(f"mr_u8{s}", [1, S], U8) for s in range(STREAMS)]
    m_col = [sb(f"m_col{s}", [P, TT]) for s in range(STREAMS)]
    m_row = [sb(f"m_row{s}", [1, S], BF16) for s in range(STREAMS)]
    ST = [sb(f"st{s}", [P, TT, 6]) for s in range(STREAMS)]
    MV = [sb(f"mv{s}", [P, TT, 2]) for s in range(STREAMS)]
    VE = [sb(f"ve{s}", [P, 2, TT]) for s in range(STREAMS)]
    RSTD = [sb(f"rstd{s}", [P, 2, TT]) for s in range(STREAMS)]
    MX = [sb(f"mx{s}", [P, H, TT]) for s in range(STREAMS)]
    MB = [sb(f"max_parts{s}", [P, TT, 2, SHIFT, H // 2], BF16) for s in range(STREAMS)]
    MT = [sb(f"mT{s}", [SHIFT * H, S], BF16) for s in range(STREAMS)]
    RS = [sb(f"rs{s}", [P, TT, H]) for s in range(STREAMS)]
    NT = [sb(f"nT{s}", [2 * H, S]) for s in range(STREAMS)]
    GT = [sb(f"gt{s}", [P, 10, TT, 4]) for s in range(STREAMS)]
    GM = [sb(f"gmx{s}", [P, 6, TT]) for s in range(STREAMS)]

    SLOT = [ctx.enter_context(nc.psum_tensor(f"slot{i}", [P, TT, S], F32)) for i in range(4)]
    BANK = [ctx.enter_context(nc.psum_tensor(f"bank{i}", [P, 2, S], F32)) for i in range(4)]

    bank_filled = signal("bank_filled")
    slot_filled = signal("slot_filled")
    mixed = signal("mixed")
    act_read = signal("act_read")
    dve_read = signal("dve_read")
    exped = signal("exped")
    maxed = signal("maxed")
    dve_step = signal("dve_step")
    act_step = signal("act_step")
    pool_step = signal("pool_step")
    dve_chain = signal("dve_chain")
    pool_chain = signal("pool_chain")
    x_in = [signal(f"x_in{s}", 16) for s in range(STREAMS)]
    mask_in = [signal(f"mask_in{s}", 16) for s in range(STREAMS)]
    ctx_in = [signal(f"ctx_in{s}", 16) for s in range(STREAMS)]
    group_in = [signal(f"group_in{s}", 16) for s in range(STREAMS)]
    stack_in = [signal(f"stack_in{s}", 16) for s in range(STREAMS)]
    shift_in = [[signal(f"shift_in{s}{a}", 16) for a in range(2)] for s in range(STREAMS)]
    x_out = [signal(f"x_out{s}", 16) for s in range(STREAMS)]
    consts_in = ctx.enter_context(nc.semaphore("consts_in"))
    weights_in = [ctx.enter_context(nc.semaphore(f"weights_in{l}")) for l in range(LAYERS + 1)]
    arrived = ctx.enter_context(nc.semaphore("arrived"))
    rounds_ended = ctx.enter_context(nc.semaphore("rounds_ended"))
    released = ctx.enter_context(nc.semaphore("released"))

    COL = {n: i for i, n in enumerate(
        ["g1", "b1", "g2", "b2", "n1", "n2", "lw", "lb", "bqA", "bkA", "bqD", "bkD", "bqE", "bkE", "qn"])}
    GAIN = {1: ("g1", "b1"), 2: ("n1", None), 3: ("lw", "lb"), "f": ("n2", None)}
    QB = {0: "bqA", 3: "bqD", 4: "bqE"}
    KB = {0: "bkA", 3: "bkD", 4: "bkE"}

    def col(name, c=0):
        i = 2 * COL[name] + c
        return cols[:, i:i + 1]

    VROW = {0: 0, 3: 2, 4: 4}
    OROW = {1: 1, 3: 3, 4: 5}
    wq = lambda l: 3 * l
    wk = lambda l: 3 * l + 1
    wv = lambda l: 3 * l + 2
    wo = lambda l: 14 + l
    queries = lambda s, h: QKS[s][:, h // 2, 0, h % 2, :]
    keys = lambda s, h: QKS[s][:, h // 2, 1, h % 2, :]
    eps_f, eps_n = 1.1920929e-07, 1e-5

    CONSTS = [(ident, "ident"), (rope_swap, "rope_swap"), (head_sum, "head_sum"), (head_spread, "head_spread"), (rope_cos, "rope_cos"),
              (rope_sin, "rope_sin"), (cols, "cols"), (rows, "rows"), (gate, "gate"), (prefer, "prefer")]
    EXPERTS = [(up0, "up0"), (l1, "l1"), (l2, "l2"), (downs, "downs"), (down3, "down3"), (l3, "l3"), (up3, "up3"),
               (up1a, "up1a"), (up1b, "up1b")]
    with nc.Block() as block:
        @block.sync
        def _(sp):
            sp.dma_start(X[0][:, 0, 0:P], t["causal_q"]).then_inc(consts_in, 16)
            sp.dma_start(X[0][:, 1, 0:P], t["causal_k"]).then_inc(consts_in, 16)
            for dst, name in CONSTS:
                sp.dma_start(dst.ap(), t[name]).then_inc(consts_in, 16)
            sp.dma_start(proj[:, 0:3, :, :], t["proj"][:, 0:3, :, :]).then_inc(weights_in[0], 16)
            sp.wait_ge(consts_in, 16 * (len(CONSTS) + 2))

        @block.gpsimd
        def _(pool):
            pool.memset(neg_half[:, :, :], -0.5)
            pool.memset(eps_col[:, :], eps_f)
            pool.memset(sum_cols[:, 0:D], 0.0)
            pool.memset(sum_cols[:, D:32], 1.0)

        @block.vector
        def _(dve):
            for s in range(STREAMS):
                dve.memset(QKS[s][ROWS:ROWS + SHIFT, :, 1, :, :], 1.0)
            dve.memset(ones_row[:, :], 1.0)
            dve.wait_ge(consts_in, 16 * (len(CONSTS) + 2))
            dve.tensor_copy(ident_b[:, :], ident[:, :])
            dve.tensor_copy(causal_q[:, :], X[0][:, 0, 0:P])
            dve.tensor_copy(causal_k[:, :], X[0][:, 1, 0:P])
            for name in ("bqA", "bqD", "bqE", "qn"):
                at = cols[:, 2 * COL[name]:2 * COL[name] + (1 if name == "qn" else 2)]
                dve.tensor_scalar(at, at, 0.25, None, ALU.mult)

    block = ctx.enter_context(nc.Block())
    ROUNDS = B // STREAMS
    FIRST, ROUND = schedule()

    def start(part):
        known["part"] = part
        for s in signals:
            s.count = 0

    def finish(eng, parts):
        eng.drain()
        eng.sem_inc(arrived, 1)
        eng.wait_ge(released, parts)

    def shift_transfer(s, a):
        return QKS[s][ROWS:ROWS + SHIFT, :, 0, a, :], MT[s][a * SHIFT * PAIRS:(a + 1) * SHIFT * PAIRS, :]

    def carried(s, l):
        return (s, l) == (0, 0)

    def bank_of(*label):
        return BANK[known.get(("bank", known["part"], label), 0)]

    def slot_of(*label):
        return SLOT[known.get(("slot", known["part"], label), 0)]

    def mixing(s, l, p):
        return mixed.at(s, l, p) if p % 2 == 0 else bank_filled.at("o", s, l, p // 2)

    READER = {"T": act_read, "TC": act_read, "q": act_read, "k": act_read, "neg": act_read, "sums": act_read, "q2": dve_read, "k2": dve_read, "o": act_read,
              "y": dve_read, "yT": act_read, "w": dve_read, "gate": dve_read, "e0": act_read, "e1a": act_read,
              "e1b": dve_read, "e2a": act_read, "e2b": act_read, "e2c": act_read, "e3a": act_read, "e3b": act_read,
              "down": dve_read}

    def reader(label):
        kind, s, l = label[:3]
        if kind == "v":
            return dve_read if l in VROW else act_read
        return READER[kind]

    @block.tensor
    def _(pe):
        last_in_bank = [None] * 4
        last_in_slot = [None] * len(SLOT)
        turns = {"bank": 0, "slot": 0}

        def bank(*label):
            at = turns["bank"] % 4
            turns["bank"] += 1
            if last_in_bank[at] is not None:
                pe.wait_ge(*reader(last_in_bank[at]).at(*last_in_bank[at]))
            last_in_bank[at] = label
            known["bank", known["part"], label] = at
            return BANK[at]

        def slot(phase, *label):
            k = turns["slot"] % len(SLOT)
            turns["slot"] += 1
            if last_in_slot[k] is not None:
                was, lab = last_in_slot[k]
                pe.wait_ge(*(maxed if was == "max" else exped).at(*lab))
            last_in_slot[k] = (phase, label)
            known["slot", known["part"], (phase, *label)] = k
            return SLOT[k]

        def transposes(label, src):
            ps = bank(*label)
            for c in range(CC):
                for tt in range(TT):
                    mm = pe.transpose(ps[:, c, tt * P:(tt + 1) * P], src[:, tt, c * P:(c + 1) * P], ident[:, :])
            mm.then_inc(*bank_filled(*label))

        def turn(s, l):
            if l == 0:
                pe.wait_ge(*x_in[s].at())
                transposes(("T", s, l), X[s])
                return
            pe.wait_ge(*dve_step.at("h", s, l))
            transposes(("T", s, l), X[s] if l == 4 else HB[s])

        def turn_context(s):
            pe.wait_ge(*dve_step.at("hc", s))
            transposes(("TC", s, 0), HB[s])

        def source(s, l):
            if l == 1:
                if s == 1:
                    pe.wait_ge(*act_read.at("TC", s, 0))
                return GP[s]
            if l == 4:
                pe.wait_ge(*ctx_in[s].at(4))
                return T[s]
            return HT[s]

        def project(kind, s, l, w, src):
            ps = bank(kind, s, l)
            for co in range(CC):
                for ci in range(CC):
                    mm = pe.matmul(ps[:, co, :], proj[:, w, ci, co * P:(co + 1) * P], src[:, ci, :],
                                   start=ci == 0, stop=ci == CC - 1)
            mm.then_inc(*bank_filled(kind, s, l))

        def project_rows(kind, s, l, w, src):
            ps = bank(kind, s, l)
            for tt in range(TT):
                for ci in range(CC):
                    mm = pe.matmul(ps[:, tt, :], src[:, ci, tt * P:(tt + 1) * P], proj[:, w, ci, :],
                                   start=ci == 0, stop=ci == CC - 1)
            mm.then_inc(*bank_filled(kind, s, l))

        def rotary_partners(s, l):
            for n, kind in enumerate(("q", "k")):
                pe.wait_ge(*act_read.at(kind, s, l))
                ps = bank(kind + "2", s, l)
                pe.matmul(ps[:, :, :], rope_swap[:, :], QK[s][:, n, :, :], start=True, stop=True)\
                    .then_inc(*bank_filled(kind + "2", s, l))

        def head_sums(s):
            ps = bank("sums", s, 2)
            pe.wait_ge(*act_step.at("sqk", s))
            for n in range(2):
                for c in range(CC):
                    mm = pe.matmul(ps[0:2 * H, 0, :], head_sum[:, n * CC + c, :], (HB, T)[n][s][:, c, :],
                                   start=n + c == 0, stop=n * CC + c == 2 * CC - 1)
            mm.then_inc(*bank_filled("sums", s, 2))

        def spread_inverses(s):
            pe.wait_ge(*dve_step.at("inverse", s))
            for n, kind in enumerate(("q", "k")):
                ps = bank(kind + "2", s, 2)
                for c in range(CC):
                    mm = pe.matmul(ps[:, c, :], head_spread[:, n * CC + c, :], NT[s][:, :], start=True, stop=True)
                mm.then_inc(*bank_filled(kind + "2", s, 2))

        def scores_for_max(s, l, p):
            if p == 0:
                if not carried(s, l):
                    pe.wait_ge(*stack_in[s].at(l, len(Q_PARTS) - 1))
                if l == 1 and s == 1:
                    pe.wait_ge(*pool_step.at("m_row", s))
            for h in (2 * p, 2 * p + 1):
                ps = slot("max", s, l, h)
                for qt in range(TT):
                    n = (qt + 1) * P if l in CAUSAL else S
                    masked = l in CAUSAL or l in (1, 4)
                    mm = pe.matmul(ps[:, qt, 0:n], queries(s, h)[0:ROWS, qt * P:(qt + 1) * P],
                                   keys(s, h)[0:ROWS, 0:n], start=True, stop=not masked)
                    if l in CAUSAL:
                        mm = pe.matmul(ps[:, qt, qt * P:n], ident_b[:, :], causal_q[:, :],
                                       start=False, stop=True)
                    elif l == 1:
                        mm = pe.matmul(ps[:, qt, :], ones_row[:, :], m_row[s][:, :], start=False, stop=True)
                    elif l == 4:
                        mm = pe.matmul(ps[:, qt, :], ident_b[:, :], NQ[s][:, qt, :], start=False, stop=True)
                mm.then_inc(*slot_filled("max", s, l, h))

        def turn_maxima(s, l):
            ps = bank("neg", s, l)
            out = ps[:, 0, :].bitcast(BF16)
            pe.wait_ge(*dve_step.at("parts", s, l))
            for qt in range(TT):
                mm = pe.transpose(out[0:SHIFT * H, qt * P:(qt + 1) * P],
                                  MB[s][:, qt, :, :, :].rearrange("p a b c -> p (a b c)"), ident_b[:, :])
            mm.then_inc(*bank_filled("neg", s, l))

        def scores_for_exp(s, l, p):
            if p == 0:
                pe.wait_ge(*shift_in[s][0].at(l))
                pe.wait_ge(*shift_in[s][1].at(l))
            for h in (2 * p, 2 * p + 1):
                ps = slot("exp", s, l, h)
                for kt in range(TT):
                    q0 = kt * P if l in CAUSAL else 0
                    masked = l in CAUSAL or l == 4
                    mm = pe.matmul(ps[:, kt, q0:S], keys(s, h)[:, kt * P:(kt + 1) * P],
                                   queries(s, h)[:, q0:S], start=True, stop=not masked)
                    if l in CAUSAL:
                        mm = pe.matmul(ps[:, kt, kt * P:(kt + 1) * P], ident_b[:, :], causal_k[:, :],
                                       start=False, stop=True)
                    elif l == 4:
                        mm = pe.matmul(ps[:, kt, :], ident_b[:, :], NK[s][:, kt, :], start=False, stop=True)
                mm.then_inc(*slot_filled("exp", s, l, h))

        def mix_values(s, l, p):
            if p == 0:
                pe.wait_ge(*reader(("v", s, l)).at("v", s, l))
            if p % 2 == 0:
                bank("o", s, l, p // 2)
            pe.wait_ge(*exped.at(s, l, 2 * p + 1))
            if l == 4:
                pe.wait_ge(*dve_step.at("weighted", s, p))
                pe.wait_ge(*pool_step.at("weighted", s, p))
            k = p % 3
            for a in range(2):
                h = 2 * p + a
                row = 32 * (h % 4)
                out = bank_of("o", s, l, p // 2)[row:row + 32, 0, :]
                if l == 4:
                    for kt in range(TT):
                        pe.matmul(out, sum_cols[:, :], PR[:, k, a, kt, :], start=kt == 0, stop=False)
                    for kt in range(TT):
                        mm = pe.matmul(out, V[s][:, kt, h, :], PR[:, 3 + p % 2, a, kt, :], start=False,
                                       stop=kt == TT - 1)
                else:
                    for kt in range(TT):
                        q0 = kt * P if l in CAUSAL else 0
                        mm = pe.matmul(out[:, q0:S], V[s][:, kt, h, :], PR[:, k, a, kt, q0:S],
                                       start=kt == 0, stop=kt == TT - 1)
            if p % 2 == 0:
                mm.then_inc(*mixed(s, l, p))
            else:
                mm.then_inc(*bank_filled("o", s, l, p // 2))

        def turn_outputs(s, l, qt):
            if qt == 0:
                pe.wait_ge(*act_read.at("o", s, l, PAIRS // 2 - 1))
            O = QK[s][:, :, :, :].rearrange("p a b c -> p (a b) c")
            ps = bank("y", s, l, qt)
            for g in range(4):
                mm = pe.transpose(ps[:, g // 2, (g % 2) * P:(g % 2 + 1) * P], O[:, g, qt * P:(qt + 1) * P],
                                  ident[:, :])
            mm.then_inc(*bank_filled("y", s, l, qt))

        def expert(kind, s, w, src, kc, halves=2):
            for half in range(halves):
                ps = bank(kind, s, 2, half)
                for j in range(2):
                    o = (2 * half + j) * P
                    for k in range(kc):
                        mm = pe.matmul(ps[:, j, :], w[:, k, o:o + P], src[:, k, :], start=k == 0, stop=k == kc - 1)
                mm.then_inc(*bank_filled(kind, s, 2, half))

        def expert_down(s, e, src):
            ps = bank("down", s, 2, e)
            for tt in range(TT):
                for k in range(4):
                    mm = pe.matmul(ps[:, tt, 0:KEEP], src[:, k, tt * P:(tt + 1) * P], downs[:, e, k, :],
                                   start=k == 0, stop=k == 3)
            mm.then_inc(*bank_filled("down", s, 2, e))

        def run(steps):
            last_in_bank[:] = [None] * len(BANK)
            last_in_slot[:] = [None] * len(SLOT)
            for step, s, l, n in steps:
                if step == "T":
                    turn(s, l)
                elif step == "TC":
                    turn_context(s)
                elif step == "q":
                    pe.wait_ge(weights_in[l], 16 * (1 + (l > 0)))
                    pe.wait_ge(*act_read.at("T", s, l))
                    project("q", s, l, wq(l), HT[s])
                elif step == "k":
                    pe.wait_ge(weights_in[l], 16 * (1 + (l > 0)))
                    project("k", s, l, wk(l), source(s, l))
                elif step == "v":
                    project_rows("v", s, l, wv(l), source(s, l))
                elif step == "again" and l == 2:
                    head_sums(s)
                elif step == "spread":
                    spread_inverses(s)
                elif step == "again" and l == 3:
                    rotary_partners(s, l)
                elif step == "max":
                    scores_for_max(s, l, n)
                elif step == "shift":
                    turn_maxima(s, l)
                elif step == "exp":
                    scores_for_exp(s, l, n)
                elif step == "mix":
                    mix_values(s, l, n)
                elif step == "y":
                    turn_outputs(s, l, n)
                elif step == "yT":
                    pe.wait_ge(*dve_read.at("y", s, l, TT - 1))
                    transposes(("yT", s, l), HB[s])
                elif step == "w" and l > 0:
                    pe.wait_ge(*act_read.at("yT", s, l))
                    project_rows("w", s, l, wo(l), HT[s])
                elif step == "gate":
                    pe.wait_ge(weights_in[LAYERS], 16 * len(EXPERTS))
                    pe.wait_ge(*act_read.at("T", s, "f"))
                    ps = bank("gate", s, 2)
                    for tt in range(TT):
                        for ci in range(CC):
                            mm = pe.matmul(ps[:, tt, 0:4], HT[s][:, ci, tt * P:(tt + 1) * P], gate[:, ci, :],
                                           start=ci == 0, stop=ci == CC - 1)
                    mm.then_inc(*bank_filled("gate", s, 2))
                elif step == "e0":
                    expert("e0", s, up0, HT[s], 2)
                elif step == "e2a":
                    expert("e2a", s, l1, HT[s], 2)
                elif step == "e2b":
                    pe.wait_ge(*act_read.at("e2a", s, 2, 1))
                    expert("e2b", s, l2, HIDDEN[0], 4)
                elif step == "e2c":
                    pe.wait_ge(*act_read.at("e2b", s, 2, 1))
                    expert("e2c", s, l3, HIDDEN[1], 4)
                elif step == "e3a":
                    expert("e3a", s, down3, HT[s], 2, 1)
                elif step == "e3b":
                    pe.wait_ge(*act_read.at("e3a", s, 2, 0))
                    expert("e3b", s, up3, HIDDEN[4], 2)
                elif step == "e1a":
                    expert("e1a", s, up1a, HT[s], 2)
                elif step == "e1b":
                    expert("e1b", s, up1b, HT[s], 2)
                elif step == "down":
                    src, made = {0: (3, act_read.at("e0", s, 2, 1)), 2: (0, act_read.at("e2c", s, 2, 1)),
                                 3: (2, act_read.at("e3b", s, 2, 1)), 1: (3, dve_read.at("e1b", s, 2, 1))}[n]
                    pe.wait_ge(*made)
                    expert_down(s, n, HIDDEN[src])

        start("first")
        run(FIRST)
        finish(pe, 1)
        start("round")
        with pe.Fori(0, ROUNDS) as i:
            run(ROUND)
            finish(pe, i + 2)

    @block.scalar
    def _(act):
        free = {k: None for k in range(5)}

        def take(k, reader_is_through):
            if free[k] is not None:
                act.wait_ge(*free[k])
            free[k] = reader_is_through

        def read_turned(kind, s, l, dst, names):
            act.wait_ge(*bank_filled.at(kind, s, l))
            ps = bank_of(kind, s, l)
            if names is None:
                act.activation(dst[:, :, :], ps[:, :, :], ACT.Copy).then_inc(*act_read(kind, s, l))
                return
            gain, bias = names
            for c in range(CC):
                a = act.activation(dst[:, c, :], ps[:, c, :], ACT.Identity, scale=col(gain, c),
                                   bias=col(bias, c) if bias else 0.0)
            a.then_inc(*act_read(kind, s, l))

        def read_projected(kind, s, l):
            n = "qk".index(kind)
            act.wait_ge(*bank_filled.at(kind, s, l))
            if l == 0:
                act.wait_ge(*pool_step.at("nk", s))
            ps = bank_of(kind, s, l)
            scale = 0.25 if kind == "q" and l != 2 else 1.0
            bias = (QB, KB)[n].get(l)
            part = SP[:, 3 * n, :].rearrange("p (c t) -> p c t", c=CC)
            if l == 2:
                act.wait_ge(*pool_step.at("x", s, l))
                act.activation((HB, T)[n][s][:, :, :], ps[:, :, :], ACT.Square).then_inc(*act_step("sq" + kind, s))
            if bias is None:
                if l == 2:
                    scale = col("qn", n)
                else:
                    act.activation(part, ps[:, :, :], ACT.Identity, scale=scale)
                a = act.activation(QK[s][:, n, :, :], ps[:, :, :], ACT.Identity, scale=scale)
            else:
                for c in range(CC):
                    if l != 3:
                        act.activation(part[:, c, :], ps[:, c, :], ACT.Identity, bias=col(bias, c), scale=scale)
                    a = act.activation(QK[s][:, n, c, :], ps[:, c, :], ACT.Identity, bias=col(bias, c), scale=scale)
            a.then_inc(*act_read(kind, s, l))

        def exponentials(s, l, p):
            take(p % 3, mixing(s, l, p))
            for a in range(2):
                h = 2 * p + a
                act.wait_ge(*slot_filled.at("exp", s, l, h))
                ps = slot_of("exp", s, l, h)
                dst = PR[:, p % 3, a, :, :]
                if l in CAUSAL or l == 1:
                    for kt in range(TT):
                        q0 = kt * P if l in CAUSAL else 0
                        e = act.activation(dst[:, kt, q0:S], ps[:, kt, q0:S], ACT.Exp,
                                           bias=m_col[s][:, kt:kt + 1] if l == 1 else 0.0)
                else:
                    e = act.activation(dst, ps[:, :, :], ACT.Exp)
                e.then_inc(*exped(s, l, h))

        def hidden(kind, s, k, func, through, halves=2):
            take(k, through)
            for half in range(halves):
                act.wait_ge(*bank_filled.at(kind, s, 2, half))
                act.activation(HIDDEN[k][:, 2 * half:2 * half + 2, :], bank_of(kind, s, 2, half)[:, :, :], func)\
                   .then_inc(*act_read(kind, s, 2, half))

        def run(steps):
            for k in free:
                free[k] = None
            for step, s, l, n in steps:
                if step == "T":
                    read_turned("T", s, l, HT[s], GAIN.get(l))
                elif step == "TC":
                    read_turned("TC", s, 0, GP[s], ("g2", "b2"))
                elif step in ("q", "k"):
                    read_projected(step, s, l)
                elif step == "v read" and l not in VROW:
                    act.wait_ge(*bank_filled.at("v", s, l))
                    for tt in range(TT):
                        a = act.activation(V[s][:, tt, :, 0:D],
                                           bank_of("v", s, l)[:, tt, :].rearrange("p (h d) -> p h d", d=D), ACT.Copy)
                    a.then_inc(*act_read("v", s, l))
                elif step == "again" and l == 2:
                    act.wait_ge(*bank_filled.at("sums", s, l))
                    act.activation(NT[s][:, :], bank_of("sums", s, l)[0:2 * H, 0, :], ACT.Sqrt,
                                   bias=eps_col[0:2 * H, :], scale=1.0 / D).then_inc(*act_read("sums", s, l))
                elif step == "shift":
                    act.wait_ge(*bank_filled.at("neg", s, l))
                    src = bank_of("neg", s, l)[:, 0, :].bitcast(BF16)[0:SHIFT * H, 0:S]
                    act.activation(MT[s][:, :], src, ACT.Copy).then_inc(*act_read("neg", s, l))
                    act.wait_ge(*act_read.at("neg", s, l))
                    act.dma_start(*shift_transfer(s, 0)).then_inc(*shift_in[s][0](l))
                elif step == "exp":
                    exponentials(s, l, n)
                elif step == "mix" and n % 2 == 1:
                    act.wait_ge(*bank_filled.at("o", s, l, n // 2))
                    O = QK[s][:, :, :, :].rearrange("p a b c -> p (a b) c")
                    act.activation(O[:, n // 2, :], bank_of("o", s, l, n // 2)[:, 0, :], ACT.Copy).then_inc(*act_read("o", s, l, n // 2))
                elif step == "yT":
                    read_turned("yT", s, l, HT[s], None)
                elif step == "route":
                    act.wait_ge(*dve_step.at("gate_sub", s))
                    act.activation(GT[s][:, 1, :, :], GT[s][:, 0, :, :], ACT.Exp).then_inc(*act_step("gate_exp", s))
                elif step == "e0":
                    hidden("e0", s, 3, ACT.Gelu, bank_filled.at("down", s, 2, 0))
                elif step == "e2a":
                    hidden("e2a", s, 0, ACT.Gelu, bank_filled.at("e2b", s, 2, 1))
                elif step == "e2b":
                    hidden("e2b", s, 1, ACT.Gelu, bank_filled.at("e2c", s, 2, 1))
                elif step == "e2c":
                    hidden("e2c", s, 0, ACT.Gelu, bank_filled.at("down", s, 2, 2))
                elif step == "e3a":
                    hidden("e3a", s, 4, ACT.Gelu, bank_filled.at("e3b", s, 2, 1), 1)
                elif step == "e3b":
                    hidden("e3b", s, 2, ACT.Gelu, bank_filled.at("down", s, 2, 3))
                elif step == "e1a":
                    hidden("e1a", s, 3, ACT.Silu, bank_filled.at("down", s, 2, 1))

        start("first")
        run(FIRST)
        for l in range(1, LAYERS):
            act.dma_start(proj[:, 3 * l:3 * l + 3, :, :], t["proj"][:, 3 * l:3 * l + 3, :, :])\
               .then_inc(weights_in[l], 16)
            act.dma_start(proj[:, wo(l), :, :], t["proj"][:, wo(l), :, :]).then_inc(weights_in[l], 16)
            if l == 2:
                for dst, name in EXPERTS:
                    act.dma_start(dst.ap(), t[name]).then_inc(weights_in[LAYERS], 16)
        finish(act, 1)
        start("round")
        with act.Fori(0, ROUNDS) as i:
            run(ROUND)
            finish(act, i + 2)

    @block.vector
    def _(dve):
        def then(ins):
            ins.then_inc(*dve_chain())
            dve.wait_ge(dve_chain.sem, dve_chain.count)

        def later(ins):
            ins.then_inc(*dve_chain())
            return dve_chain.count

        def read(count):
            dve.wait_ge(dve_chain.sem, count)

        def statistics(s, src, label, mean_square):
            for tt in range(TT):
                a = dve.bn_stats(ST[s][:, tt, :], src[:, tt, :])
            then(a)
            for tt in range(TT):
                a = dve.bn_aggr(MV[s][:, tt, :], ST[s][:, tt, :])
            if mean_square:
                then(a)
                then(dve.tensor_tensor(VE[s][:, 0, :], MV[s][:, :, 0], MV[s][:, :, 0], ALU.mult))
                a = dve.tensor_tensor(MV[s][:, :, 1], VE[s][:, 0, :], MV[s][:, :, 1], ALU.add)
            a.then_inc(*dve_step("stat", *label))

        def centred(s, src, dst, which):
            for tt in range(TT):
                a = dve.tensor_scalar(dst[:, tt, :], src[:, tt, :], MV[s][:, tt, 0:1], RSTD[s][:, which, tt:tt + 1],
                                      ALU.subtract, ALU.mult)
            return a

        def normalise(s, l, after):
            dve.wait_ge(*pool_step.at("rstd", s, l))
            if after in SELF_LN:
                centred(s, T[s], HB[s], 1).then_inc(*dve_step("h", s, after))
            else:
                centred(s, T[s], X[s], 0).then_inc(*dve_step("h", s, after))

        def read_values(s, l):
            dve.wait_ge(*bank_filled.at("v", s, l))
            ps = bank_of("v", s, l)
            if l == 4 or s == 1:
                dve.wait_ge(*pool_step.at("v_zeros" if l == 4 else "v_ones", s))
            for tt in range(TT):
                a = dve.tensor_tensor(V[s][:, tt, :, 0:D], ps[:, tt, :].rearrange("p (h d) -> p h d", d=D),
                                      rows[:, VROW[l], :].rearrange("p (h d) -> p h d", d=D), ALU.add)
            a.then_inc(*dve_read("v", s, l))

        def partners(s, l):
            for n, kind in enumerate(("q", "k")):
                dve.wait_ge(*bank_filled.at(kind + "2", s, l))
                dve.wait_ge(*pool_step.at("x", s, l))
                sin = rope_sin[:, :].unsqueeze(1).to_broadcast([P, CC, S])
                dve.tensor_tensor((HB, T)[n][s][:, :, :], bank_of(kind + "2", s, l)[:, :, :], sin, ALU.mult)\
                   .then_inc(*dve_read(kind + "2", s, l))

        def rotate(s, l):
            done = []
            for n, kind in enumerate(("q", "k")):
                dve.wait_ge(*dve_read.at(kind + "2", s, l))
                dve.wait_ge(*pool_step.at("cos" + kind, s, l))
                done.append(later(dve.tensor_tensor(QK[s][:, n, :, :], QK[s][:, n, :, :], (HB, T)[n][s][:, :, :],
                                                    ALU.add)))
            return done

        def normalise_heads(s, l):
            for n, kind in enumerate(("q", "k")):
                dve.wait_ge(*bank_filled.at(kind + "2", s, l))
                dve.wait_ge(*act_read.at(kind, s, l))
                dve.tensor_tensor(QK[s][:, n, :, :], QK[s][:, n, :, :], bank_of(kind + "2", s, l)[:, :, :], ALU.mult)\
                   .then_inc(*dve_read(kind + "2", s, l))

        def split(s, l):
            full = [QK[s][:, n, :, :].rearrange("p a b -> p (a b)") for n in range(2)]
            part = [[SP[:, 3 * n + j, :] for j in range(3)] for n in range(2)]
            done = rotate(s, l) if l == 3 else None
            for n, kind in enumerate("qk"):
                if l in (2, 3):
                    if l == 3:
                        read(done[n])
                    else:
                        dve.wait_ge(*dve_read.at(kind + "2", s, l))
                    dve.tensor_copy(part[n][0], full[n]).then_inc(*dve_step("first " + kind, s, l))
                    dve.wait_ge(*dve_step.at("first " + kind, s, l))
                else:
                    dve.wait_ge(*act_read.at(kind, s, l))
                then(dve.tensor_tensor(full[n], full[n], part[n][0], ALU.subtract))
                dve.tensor_copy(part[n][1], full[n]).then_inc(*dve_step("second " + kind, s, l))
            dve.wait_ge(*dve_step.at("second k", s, l))
            for n in range(2):
                a = dve.tensor_tensor(part[n][2], full[n], part[n][1], ALU.subtract)
            a.then_inc(*dve_step("split", s, l))

        def maximum(s, l, p):
            for h in (2 * p, 2 * p + 1):
                dve.wait_ge(*slot_filled.at("max", s, l, h))
                ps = slot_of("max", s, l, h)
                if l in CAUSAL:
                    for qt in range(TT):
                        a = dve.tensor_reduce(MX[s][:, h, qt:qt + 1], ps[:, qt, 0:(qt + 1) * P], AX.X, ALU.max)
                else:
                    a = dve.tensor_reduce(MX[s][:, h, :], ps[:, :, :], AX.X, ALU.max)
                a.then_inc(*maxed(s, l, h))

        def maxima_parts(s, l):
            m = MX[s][:, :, :].rearrange("p (h a) q -> p q a h", a=2)
            dve.wait_ge(*maxed.at(s, l, H - 1))
            then(dve.tensor_scalar(MB[s][:, :, :, 0, :], m, -1.0, None, ALU.mult))
            then(dve.tensor_tensor(m, m, MB[s][:, :, :, 0, :], ALU.add))
            then(dve.tensor_scalar(MB[s][:, :, :, 1, :], m, -1.0, None, ALU.mult))
            then(dve.tensor_tensor(m, m, MB[s][:, :, :, 1, :], ALU.add))
            dve.tensor_scalar(MB[s][:, :, :, 2, :], m, -1.0, None, ALU.mult).then_inc(*dve_step("parts", s, l))

        def outputs(s, l, qt):
            dve.wait_ge(*bank_filled.at("y", s, l, qt))
            ps = bank_of("y", s, l, qt)[:, :, :].rearrange("p a (b e) -> p (a b) e", e=32)
            then(dve.reciprocal(RS[s][:, qt, :].unsqueeze(2), ps[:, :, D:D + 1]))
            dst = HB[s][:, qt, :].rearrange("p (h d) -> p h d", d=D)
            dve.tensor_tensor(dst, ps[:, :, 0:D], RS[s][:, qt, :].unsqueeze(2).to_broadcast([P, H, D]), ALU.mult)\
               .then_inc(*dve_read("y", s, l, qt))

        def residual(s, l):
            t_, x_ = T[s][:, :, :], X[s][:, :, :]
            if l == 0:
                dve.wait_ge(*dve_read.at("y", s, l, TT - 1))
                then(dve.tensor_tensor(t_, x_, HB[s][:, :, :], ALU.add))
                return
            dve.wait_ge(*bank_filled.at("w", s, l))
            ps = bank_of("w", s, l)
            if l == 2:
                dve.wait_ge(*pool_step.at("x", s, 2))
                dve.tensor_copy(T[s][:, :, 0:SKIP], X[s][:, :, 0:SKIP])
                dve.tensor_tensor(T[s][:, :, SKIP:C], ps[:, :, SKIP:C], X[s][:, :, SKIP:C], ALU.add)\
                   .then_inc(*dve_read("w", s, l))
            else:
                dve.wait_ge(*pool_step.at("xb", s, l))
                dve.tensor_tensor(t_, ps[:, :, :], x_, ALU.add).then_inc(*dve_read("w", s, l))
            dve.wait_ge(*dve_read.at("w", s, l))

        def routing(s):
            g = lambda k: GT[s][:, k, :, :]
            m = lambda k: GM[s][:, k, :]
            wide = lambda k: GM[s][:, k, :].unsqueeze(2).to_broadcast([P, TT, 4])
            dve.wait_ge(*dve_read.at("gate", s, 2))
            then(dve.tensor_tensor(g(3), g(2), wide(0), ALU.is_equal))
            then(dve.tensor_tensor(g(3), g(3), prefer[:, :, :], ALU.mult))
            then(dve.tensor_reduce(m(1), g(3), AX.X, ALU.max))
            then(dve.tensor_tensor(g(4), prefer[:, :, :], wide(1), ALU.is_equal))
            then(dve.tensor_scalar(g(5), g(4), -3.4028235e38, None, ALU.mult))
            then(dve.tensor_tensor(g(5), g(0), g(5), ALU.add))
            then(dve.tensor_reduce(m(2), g(5), AX.X, ALU.max))
            then(dve.tensor_tensor(g(6), g(5), wide(2), ALU.is_equal))
            then(dve.tensor_tensor(g(6), g(6), prefer[:, :, :], ALU.mult))
            then(dve.tensor_reduce(m(3), g(6), AX.X, ALU.max))
            then(dve.tensor_tensor(g(7), prefer[:, :, :], wide(3), ALU.is_equal))
            then(dve.tensor_tensor(g(7), g(7), g(4), ALU.add))
            dve.wait_ge(*act_step.at("gate_exp", s))
            then(dve.tensor_reduce(m(4), g(1), AX.X, ALU.add))
            then(dve.reciprocal(m(4), m(4)))
            then(dve.tensor_tensor(g(8), g(1), wide(4), ALU.mult))
            then(dve.tensor_tensor(g(8), g(8), g(7), ALU.mult))
            then(dve.tensor_reduce(m(5), g(8), AX.X, ALU.add))
            then(dve.tensor_scalar(m(5), m(5), 1e-8, None, ALU.add))
            then(dve.reciprocal(m(5), m(5)))
            then(dve.tensor_tensor(g(9), g(8), wide(5), ALU.mult))

        def read_gate(s):
            dve.wait_ge(*bank_filled.at("gate", s, 2))
            dve.tensor_scalar(GT[s][:, 2, :, :], bank_of("gate", s, 2)[:, :, 0:4], 3.4028235e38, -3.4028235e38,
                              ALU.min, ALU.max).then_inc(*dve_read("gate", s, 2))
            dve.wait_ge(*dve_read.at("gate", s, 2))
            then(dve.tensor_reduce(GM[s][:, 0, :], GT[s][:, 2, :, :], AX.X, ALU.max))
            dve.tensor_tensor(GT[s][:, 0, :, :], GT[s][:, 2, :, :],
                              GM[s][:, 0, :].unsqueeze(2).to_broadcast([P, TT, 4]), ALU.subtract)\
               .then_inc(*dve_step("gate_sub", s))

        def add_expert(s, e):
            dve.wait_ge(*bank_filled.at("down", s, 2, e))
            ps = bank_of("down", s, 2, e)
            for tt in range(TT):
                acc = T[s][:, tt, SKIP:C]
                a = dve.scalar_tensor_tensor(out=acc, in0=ps[:, tt, 0:KEEP], scalar=GT[s][:, 9, tt, e:e + 1], in1=acc,
                                             op0=ALU.mult, op1=ALU.add)
            a.then_inc(*dve_read("down", s, 2, e))
            dve.wait_ge(*dve_read.at("down", s, 2, e))

        def run(steps):
            for step, s, l, n in steps:
                if step == "context":
                    dve.wait_ge(*ctx_in[s].at(0))
                    statistics(s, HB[s], (s, "c"), False)
                    dve.wait_ge(*pool_step.at("rstd", s, "c"))
                    centred(s, HB[s], HB[s], 0).then_inc(*dve_step("hc", s))
                elif step == "v read" and l in VROW:
                    read_values(s, l)
                elif step == "again" and l == 2:
                    dve.wait_ge(*act_read.at("sums", s, l))
                    dve.reciprocal(NT[s][:, :], NT[s][:, :]).then_inc(*dve_step("inverse", s))
                elif step == "spread":
                    normalise_heads(s, l)
                elif step == "again" and l == 3:
                    partners(s, l)
                elif step == "split":
                    split(s, l)
                elif step == "max":
                    maximum(s, l, n)
                elif step == "parts":
                    maxima_parts(s, l)
                elif step == "exp" and l == 4:
                    dve.wait_ge(*exped.at(s, l, 2 * n))
                    dve.wait_ge(*group_in[s].at())
                    if n >= 2:
                        dve.wait_ge(*mixing(s, l, n - 2))
                    elif s == 1:
                        dve.wait_ge(*mixing(0, l, PAIRS - 2 + n))
                    dve.tensor_tensor(PR[:, 3 + n % 2, 0, :, :], PR[:, n % 3, 0, :, :], GP[s][:, :, :], ALU.mult)\
                       .then_inc(*dve_step("weighted", s, n))
                elif step == "y":
                    outputs(s, l, n)
                elif step == "w":
                    residual(s, l)
                elif step == "stat":
                    statistics(s, T[s], (s, l), l == 2)
                elif step == "norm" and l == 2:
                    dve.wait_ge(*pool_step.at("rstd", s, 2))
                    for tt in range(TT):
                        a = dve.tensor_scalar(HB[s][:, tt, :], T[s][:, tt, :], RSTD[s][:, 0, tt:tt + 1], None, ALU.mult)
                    a.then_inc(*dve_step("h", s, "f"))
                    dve.wait_ge(*dve_step.at("h", s, "f"))
                    then(dve.tensor_tensor(T[s][:, :, :], T[s][:, :, :], X[s][:, :, :], ALU.add))
                elif step == "norm":
                    normalise(s, l, 3 if l == "f" else l + 1)
                elif step == "gate":
                    read_gate(s)
                elif step == "route":
                    routing(s)
                elif step == "e1b":
                    for half in range(2):
                        dve.wait_ge(*bank_filled.at("e1b", s, 2, half))
                        dve.wait_ge(*act_read.at("e1a", s, 2, half))
                        hid = HIDDEN[3][:, 2 * half:2 * half + 2, :]
                        dve.tensor_tensor(hid, bank_of("e1b", s, 2, half)[:, :, :], hid, ALU.mult)\
                           .then_inc(*dve_read("e1b", s, 2, half))
                elif step == "down":
                    add_expert(s, n)

        start("first")
        run(FIRST)
        finish(dve, 1)
        start("round")
        with dve.Fori(0, ROUNDS) as i:
            run(ROUND)
            finish(dve, i + 2)

    @block.gpsimd
    def _(pool):
        def then(ins):
            ins.then_inc(*pool_chain())
            pool.wait_ge(pool_chain.sem, pool_chain.count)

        def inverse_roots(s, l, eps, again=None):
            pool.wait_ge(*dve_step.at("stat", s, l))
            a = pool.tensor_scalar(VE[s][:, 0, :], MV[s][:, :, 1], eps, None, ALU.add)
            n = 1
            if again is not None:
                a = pool.tensor_scalar(VE[s][:, 1, :], MV[s][:, :, 1], 1.0 + again, eps * again, ALU.mult, ALU.add)
                n = 2
            then(a)
            pool.tensor_tensor(RSTD[s][:, 0:n, :], VE[s][:, 0:n, :], neg_half[:, 0:n, :], ALU.pow)\
                .then_inc(*pool_step("rstd", s, l))

        def centred(s, l, after):
            for tt in range(TT):
                a = pool.tensor_scalar(X[s][:, tt, :], T[s][:, tt, :], MV[s][:, tt, 0:1], RSTD[s][:, 0, tt:tt + 1],
                                       ALU.subtract, ALU.mult)
            a.then_inc(*pool_step("x", s, after))

        def run(steps):
            for step, s, l, n in steps:
                if step == "ones":
                    if known["part"] == "round" and s == 0:
                        pool.wait_ge(*mixing(0, 4, PAIRS - 1))
                    pool.memset(V[s][:, :, :, D:32], 1.0).then_inc(*pool_step("v_ones", s))
                elif step == "context":
                    inverse_roots(s, "c", eps_n)
                    pool.wait_ge(*mask_in[s].at("all"))
                    for dst, src in ((NQ[s], QK[s][:, 0, :, :]), (NK[s], QK[s][:, 1, :, :])):
                        a = pool.tensor_scalar(dst[:, :, :], src.bitcast(I32), 1.0e9, -1.0e9, ALU.mult, ALU.add)
                    a.then_inc(*pool_step("nk", s))
                    then(pool.tensor_scalar(m_col[s][:, :], m_u8[s][:, :], -LOW, LOW, ALU.mult, ALU.add))
                    pool.tensor_scalar(m_row[s][:, :], mr_u8[s][:, :], -LOW, LOW, ALU.mult, ALU.add)\
                        .then_inc(*pool_step("m_row", s))
                    pool.wait_ge(*pool_step.at("m_row", s))
                elif step == "stat":
                    if l == 2:
                        inverse_roots(s, l, eps_f)
                    else:
                        inverse_roots(s, l, eps_n, {0: eps_n, 1: eps_f, "f": eps_n}.get(l))
                        if l in (0, 1, "f"):
                            pool.wait_ge(*pool_step.at("rstd", s, l))
                            centred(s, l, 3 if l == "f" else l + 1)
                elif step == "q" and l == 4:
                    pool.wait_ge(*mixing(s, 3, PAIRS - 1))
                    pool.memset(V[s][:, :, :, D:32], 0.0).then_inc(*pool_step("v_zeros", s))
                elif step == "again" and l == 3:
                    for k, kind in enumerate(("q", "k")):
                        pool.wait_ge(*bank_filled.at(kind + "2", s, l))
                        qk = QK[s][:, k, :, :]
                        pool.tensor_tensor(qk, qk, rope_cos[:, :].unsqueeze(1).to_broadcast([P, CC, S]), ALU.mult)\
                            .then_inc(*pool_step("cos" + kind, s, l))
                elif step == "exp" and l == 4:
                    pool.wait_ge(*exped.at(s, l, 2 * n + 1))
                    pool.wait_ge(*group_in[s].at())
                    if n >= 2:
                        pool.wait_ge(*mixing(s, l, n - 2))
                    elif s == 1:
                        pool.wait_ge(*mixing(0, l, PAIRS - 2 + n))
                    pool.tensor_tensor(PR[:, 3 + n % 2, 1, :, :], PR[:, n % 3, 1, :, :], GP[s][:, :, :], ALU.mult)\
                        .then_inc(*pool_step("weighted", s, n))
                elif step == "split" and l in OROW:
                    pool.wait_ge(*(dve_step.at("h", s, l) if l == 4 else pool_step.at("x", s, l)))
                    pool.wait_ge(*bank_filled.at("T", s, l))
                    x_ = X[s][:, :, :]
                    if l == 3:
                        then(pool.tensor_tensor(x_, x_, x_, ALU.add))
                    b_ = rows[:, OROW[l], :].unsqueeze(1).to_broadcast([P, TT, C])
                    pool.tensor_tensor(x_, x_, b_, ALU.add).then_inc(*pool_step("xb", s, l))

        start("first")
        run(FIRST)
        finish(pool, 1)
        start("round")
        with pool.Fori(0, ROUNDS) as i:
            run(ROUND)
            finish(pool, i + 2)

    @block.sync
    def _(sp):
        flat = "b p t c -> (b p) t c"

        def stack(s, l):
            for j, (a, b) in enumerate(zip(Q_PARTS, K_PARTS)):
                if j == 0 and l in (2, 3):
                    sp.wait_ge(*dve_step.at("first k", s, l))
                elif j == 0:
                    sp.wait_ge(*act_read.at("k", s, l))
                    sp.wait_ge(*act_read.at("q", s, l))
                elif max(a, b) > max(Q_PARTS[j - 1], K_PARTS[j - 1]):
                    sp.wait_ge(*dve_step.at(("second k", "split")[max(a, b) - 1], s, l))
                sp.dma_start(QKS[s][D * j:D * (j + 1), :, :, :, :], SP[:, a:3 + b + 1:3 + b - a, :])\
                    .then_inc(*stack_in[s](l, j))

        def load(s, what, at):
            again = known["part"] == "round" and s == 0
            if what == "ctx":
                if again:
                    sp.wait_ge(*bank_filled.at("yT", s, 4))
                sp.dma_start(HB[s][:, :, :], t["ctx"][at].rearrange(flat)).then_inc(*ctx_in[s](0))
                if again:
                    sp.wait_ge(*bank_filled.at("y", s, 4, TT - 1))
                sp.dma_start(QK[s][:, 0, :, :].bitcast(I32), t["mask"][at].rearrange(flat)).then_inc(*mask_in[s]("q"))
                sp.dma_start(QK[s][:, 1, :, :].bitcast(I32), t["maskT"][at].rearrange(flat)).then_inc(*mask_in[s]("k"))
                sp.dma_start(m_u8[s][:, :], t["m_cols"][at].rearrange("b p t -> (b p) t")).then_inc(*mask_in[s]("c"))
                sp.dma_start(mr_u8[s][:, :], t["m_rows"][at].rearrange("b o t -> (b o) t"))\
                    .then_inc(*mask_in[s]("all"))
            else:
                if again:
                    sp.wait_ge(*x_out[s].at())
                sp.dma_start(X[s][:, :, :], t["x"][at].rearrange(flat)).then_inc(*x_in[s]())

        def run(steps, batch):
            for step, s, l, n in steps:
                at = bass.ds(batch + s, 1)
                if step == "load":
                    load(s, n, bass.ds(batch + 2, 1) if s == 0 and steps is ROUND else at)
                elif step == "split":
                    stack(s, l)
                elif step == "shift":
                    sp.wait_ge(*act_read.at("neg", s, l))
                    sp.dma_start(*shift_transfer(s, 1)).then_inc(*shift_in[s][1](l))
                elif step == "T" and l == 2:
                    sp.wait_ge(*bank_filled.at("v", s, 1))
                    sp.dma_start(GP[s][:, :, :], t["gpT"][at].rearrange(flat)).then_inc(*group_in[s]())
                elif step == "norm" and l == 3:
                    sp.wait_ge(*dve_step.at("h", s, 4))
                    sp.dma_start(T[s][:, :, :], t["ctxT"][at].rearrange(flat)).then_inc(*ctx_in[s](4))
                elif step == "out":
                    sp.wait_ge(*dve_step.at("h", s, LAYERS))
                    rows_out = x5_dram.rearrange("(b t p) c -> b p t c", t=TT, p=P)[at]
                    sp.dma_start(rows_out.rearrange(flat), X[s][:, :, :]).then_inc(*x_out[s]())

        def clear():
            for sem in work:
                sp.sem_clear(sem)
            sp.sem_inc(released, 1)

        start("first")
        run(FIRST, 0)
        sp.wait_ge(*stack_in[0].at(0, len(Q_PARTS) - 1))
        sp.wait_ge(arrived, 4)
        clear()
        start("round")
        with sp.Fori(0, ROUNDS) as i:
            run(ROUND, 2 * i)
            sp.wait_ge(*stack_in[0].at(0, len(Q_PARTS) - 1))
            sp.wait_ge(*x_out[1].at())
            sp.wait_ge(arrived, 4 * i + 8)
            sp.sem_inc(rounds_ended, 1)
            clear()


def routed_mixture(nc, ctx, t, known, x5_dram, slots_dram, expert_dram):
    def sb(name, shape, dt=F32):
        return ctx.enter_context(nc.sbuf_tensor(name, shape, dt))

    def signal(name, step=1):
        return Signal(name, ctx.enter_context(nc.semaphore(name)), known, step)

    G = B * S // P
    SLOTS = E1 * CAP
    ST = SLOTS // P
    CH = [(0, P), (P, P), (2 * P, CAP - 2 * P)]
    FC = DFF // P

    x5 = sb("x5", [P, G, C])
    ident = sb("ident2", [P, P])
    upto = sb("upto", [P, P])
    upto_b = sb("upto_b", [P, P], BF16)
    ones_b = sb("ones_b", [P, P], BF16)
    wg = sb("wg", [P, CC, E1])
    prefer = sb("prefer8", [P, G, E1])
    zero = sb("zero", [P, C])
    lg = sb("lg", [P, 5, G, E1])
    oh = sb("oh", [P, G, E1], BF16)
    run = sb("run", [P, 2, G, E1])
    tot = sb("tot", [P, G, E1])
    red = sb("red", [P, 8, G])
    idx = sb("idx", [P, G], U32)
    w1 = sb("w1", [P, CC, DFF])
    w2 = sb("w2", [P, FC, C])
    b1 = sb("b1", [P, E1, FC])
    b2 = sb("b2", [P, E1, C])
    w1_high = sb("w1_high", [P, CC, DFF], F32R)
    w1_low = sb("w1_low", [P, CC, DFF], F32R)
    w2_high = sb("w2_high", [P, FC, C], F32R)
    w2_low = sb("w2_low", [P, FC, C], F32R)
    rows = sb("slot_rows_sb", [P, ST, C])
    xt = rows[:, 0:8, :].rearrange("p (a b c) d -> p a b (c d)", a=4, b=CC)
    xs_high = sb("xs_high", [P, CC, SLOTS], F32R)
    xs_low = sb("xs_low", [P, CC, SLOTS], F32R)
    hid = sb("hid", [P, 3, CAP])
    hid_low = [sb(f"hid_low{k}", [P, FC, CAP], F32R) for k in range(2)]
    hid_high = [sb(f"hid_high{k}", [P, FC, CAP], F32R) for k in range(2)]
    eo = sb("eo", [P, 3, C])
    back = rows[:, 0:G, :]
    st = sb("st2", [P, G, 6])
    mv = sb("mv2", [P, G, 2])
    ve = sb("ve2", [P, G])
    rstd = sb("rstd2", [P, G])
    half = sb("neg_half2", [P, G])
    BANK = [ctx.enter_context(nc.psum_tensor(f"pbank{i}", [P, 512], F32)) for i in range(8)]

    x_in = [signal(f"x5_in{k}", 16) for k in range(4)]
    const_in = signal("const_in", 16)
    cleared = signal("slots_cleared", 16)
    scattered = signal("scattered", 16)
    slots_in = [signal(f"slots_in{k}", 16) for k in range(4)]
    w_in = {name: signal(f"{name}_in", 16) for name in ("w1", "w2")}
    expert_out = [signal(f"expert_out{k}", 16) for k in range(3)]
    gathered = [signal(f"gathered{k}", 16) for k in range(4)]
    written = signal("written", 16)
    pe_turned = signal("pe_turned")
    pe_logits = signal("pe_logits")
    pe_counts = signal("pe_counts")
    pe_rows = signal("pe_rows")
    pe_up = signal("pe_up")
    pe_down = signal("pe_down")
    act_turned = signal("act_turned")
    dve_turned = signal("dve_turned")
    act_exp = signal("act_exp")
    act_rows = signal("act_rows")
    act_up = signal("act_up")
    act_high = signal("act_high")
    dve_rows = signal("dve_rows")
    dve_low = signal("dve_low")
    dve_hid = signal("dve_hid")
    dve_chain = signal("dve_chain2")
    dve_done = signal("dve_done")
    dve_down = signal("dve_down")
    dve_out = signal("dve_out")
    pool_done = signal("pool_done")
    pool_chain = signal("pool_chain2")

    block = ctx.enter_context(nc.Block())
    UPS = [BANK[k] for k in range(2, 5)]
    DOWNS = [BANK[k] for k in range(5, 8)]

    @block.sync
    def _(sp):
        xv = x5_dram.rearrange("(g p) c -> p g c", p=P)
        for k in range(4):
            sp.dma_start(x5[:, 4 * k:4 * k + 4, :], xv[:, 4 * k:4 * k + 4, :]).then_inc(*x_in[k]())
        for dst, name in ((ident, "ident"), (upto, "upto"), (wg, "wg"), (prefer, "prefer8"), (b1, "b1"), (b2, "b2")):
            sp.dma_start(dst.ap(), t[name]).then_inc(*const_in(name))

        def weights(e):
            for name, dst in (("w1", w1), ("w2", w2)):
                if e >= 1:
                    sp.wait_ge(*dve_low.at(name, e - 1))
                sp.dma_start(dst[:, :, :], t[name][e]).then_inc(*w_in[name](e))

        weights(0)
        weights(1)
        sp.wait_ge(*scattered.at(G - 1))
        sv = slots_dram.rearrange("(n p) c -> p n c", p=P)
        for k in range(4):
            sp.dma_start(rows[:, 5 * k:5 * k + 5, :], sv[:, 5 * k:5 * k + 5, :]).then_inc(*slots_in[k]("in"))
        for e in range(E1):
            if 1 <= e < E1 - 1:
                weights(e + 1)
            for j, (c0, m) in enumerate(CH):
                sp.wait_ge(*dve_down.at(e, j))
                sp.dma_start(expert_dram[e * CAP + c0:e * CAP + c0 + m, :], eo[0:m, j, :])\
                    .then_inc(*expert_out[j](e))
        ov = t["out"].rearrange("(g p) c -> p g c", p=P)
        for k in range(4):
            sp.wait_ge(*dve_out.at(k))
            sp.dma_start(ov[:, 4 * k:4 * k + 4, :], back[:, 4 * k:4 * k + 4, :]).then_inc(*written(k))
        sp.wait_ge(*written.at(3))

    TURN = [BANK[k] for k in (0, 1, 5, 6)]

    def logits(pe, n):
        pe.wait_ge(*turned_by(n).at(n))
        for k in range(2):
            g = 2 * n + k
            for ci in range(CC):
                mm = pe.matmul(BANK[2][:, g * E1:(g + 1) * E1], xt[:, n % 4, ci, k * P:(k + 1) * P], wg[:, ci, :],
                               start=ci == 0, stop=ci == CC - 1)
        mm.then_inc(*pe_logits(n))

    def turned_by(n):
        return (act_turned, dve_turned)[n % 2]

    @block.tensor
    def _(pe):
        pe.wait_ge(*const_in.at("b2"))
        for n in range(G // 2):
            pe.wait_ge(*x_in[n // 2].at())
            if n >= 4:
                pe.wait_ge(*turned_by(n).at(n - 4))
            for c in range(CC):
                for k in range(2):
                    mm = pe.transpose(TURN[n % 4][:, (2 * c + k) * P:(2 * c + k + 1) * P],
                                      x5[:, 2 * n + k, c * P:(c + 1) * P], ident[:, :])
            mm.then_inc(*pe_turned(n))
            if n >= 2:
                logits(pe, n - 2)
        logits(pe, G // 2 - 2)
        logits(pe, G // 2 - 1)
        pe.wait_ge(*dve_done.at("onehot"))
        flat = oh[:, :, :].rearrange("p g e -> p (g e)")
        pe.matmul(BANK[3][:, 0:P], upto_b[:, :], flat, start=True, stop=True)
        pe.matmul(BANK[4][:, 0:P], ones_b[:, :], flat, start=True, stop=True).then_inc(*pe_counts("all"))
        for n in range(ST // 2):
            pe.wait_ge(*slots_in[(2 * n) // 5].at("in"))
            pe.wait_ge(*slots_in[(2 * n + 1) // 5].at("in"))
            if n >= 4:
                pe.wait_ge(*dve_rows.at(n - 4))
            for c in range(CC):
                for k in range(2):
                    mm = pe.transpose(TURN[n % 4][:, (2 * c + k) * P:(2 * c + k + 1) * P],
                                      rows[:, 2 * n + k, c * P:(c + 1) * P], ident[:, :])
            mm.then_inc(*pe_rows(n))

        def products(out, left, right, start, stop):
            pe.matmul(out, left[0], right[1], start=start, stop=False)
            pe.matmul(out, left[1], right[0], start=False, stop=False)
            return pe.matmul(out, left[0], right[0], start=False, stop=stop)

        ups = 0
        for e in range(E1):
            pe.wait_ge(*dve_rows.at(min(ST // 2 - 1, ((e + 1) * CAP - 1) // (2 * P))))
            pe.wait_ge(*dve_low.at("w1", e))
            at = slice(e * CAP, (e + 1) * CAP)
            for f in range(FC):
                if ups >= 3:
                    pe.wait_ge(*act_up.at(*divmod(ups - 3, FC)))
                elif ups in (1, 2):
                    pe.wait_ge(*dve_done.at("counted"))
                fs = slice(f * P, (f + 1) * P)
                for ci in range(CC):
                    mm = products(UPS[ups % 3][:, 0:CAP], (w1_high[:, ci, fs], w1_low[:, ci, fs]),
                                  (xs_high[:, ci, at], xs_low[:, ci, at]), ci == 0, ci == CC - 1)
                mm.then_inc(*pe_up(e, f))
                ups += 1
            pe.wait_ge(*dve_low.at("w2", e))
            if e == 0:
                pe.wait_ge(*dve_rows.at(ST // 2 - 1))
            for j, (c0, m) in enumerate(CH):
                if e >= 1:
                    pe.wait_ge(*dve_down.at(e - 1, j))
                for f in range(FC):
                    if j == 0:
                        pe.wait_ge(*dve_hid.at(e, f))
                    mm = products(DOWNS[j][0:m, 0:C], (hid_high[e % 2][:, f, c0:c0 + m],
                                                      hid_low[e % 2][:, f, c0:c0 + m]),
                                  (w2_high[:, f, :], w2_low[:, f, :]), f == 0, f == FC - 1)
                mm.then_inc(*pe_down(e, j))

    @block.scalar
    def _(act):
        for n in range(0, G // 2, 2):
            act.wait_ge(*pe_turned.at(n))
            if n >= 4:
                act.wait_ge(*pe_logits.at(n - 4))
            act.activation(xt[:, n % 4, :, :].rearrange("p a b -> p (a b)"), TURN[n % 4][:, :], ACT.Copy)\
               .then_inc(*act_turned(n))
        act.wait_ge(*dve_done.at("sub"))
        act.activation(lg[:, 1, :, :], lg[:, 0, :, :], ACT.Exp).then_inc(*act_exp("e"))

        def weights_high(name, e):
            high, full = {"w1": (w1_high, w1), "w2": (w2_high, w2)}[name]
            act.wait_ge(*w_in[name].at(e))
            if e >= 1:
                act.wait_ge(*(pe_up.at(e - 1, FC - 1) if name == "w1" else pe_down.at(e - 1, 2)))
            act.activation(high[:, :, :], full[:, :, :], ACT.Copy).then_inc(*act_high(name, e))

        weights_high("w1", 0)
        weights_high("w2", 0)
        for n in range(ST // 2):
            act.wait_ge(*pe_rows.at(n))
            act.activation(xs_high[:, :, 2 * n * P:(2 * n + 2) * P],
                           TURN[n % 4][:, :].rearrange("p (a b) -> p a b", a=CC), ACT.Copy).then_inc(*act_rows(n))
        for e in range(E1):
            for f in range(FC):
                act.wait_ge(*pe_up.at(e, f))
                if e >= 2:
                    act.wait_ge(*pe_down.at(e - 2, 2))
                if e * FC + f >= 3:
                    act.wait_ge(*dve_hid.at(*divmod(e * FC + f - 3, FC)))
                for dst in (hid[:, (e * FC + f) % 3, :], hid_high[e % 2][:, f, :]):
                    a = act.activation(dst, UPS[(e * FC + f) % 3][:, 0:CAP], ACT.Relu,
                                       bias=b1[:, e, f:f + 1])
                a.then_inc(*act_up(e, f))
            if e + 1 < E1:
                weights_high("w1", e + 1)
                weights_high("w2", e + 1)

    @block.vector
    def _(dve):
        def then(ins):
            ins.then_inc(*dve_chain())
            dve.wait_ge(dve_chain.sem, dve_chain.count)

        def wide(k):
            return red[:, k, :].unsqueeze(2).to_broadcast([P, G, E1])

        L = lambda k: lg[:, k, :, :]
        R = lambda k: red[:, k, :]
        dve.memset(zero[:, :], 0.0).then_inc(*dve_done("zero"))
        dve.memset(ones_b[:, :], 1.0)
        dve.memset(half[:, :], -0.5).then_inc(*dve_done("half"))
        dve.wait_ge(*const_in.at("b2"))
        then(dve.tensor_copy(upto_b[:, :], upto[:, :]))
        for n in range(1, G // 2, 2):
            dve.wait_ge(*pe_turned.at(n))
            if n >= 4:
                dve.wait_ge(*pe_logits.at(n - 4))
            dve.tensor_copy(xt[:, n % 4, :, :].rearrange("p a b -> p (a b)"), TURN[n % 4][:, :])\
               .then_inc(*dve_turned(n))
        dve.wait_ge(*pe_logits.at(G // 2 - 1))
        then(dve.tensor_copy(L(2), BANK[2][:, 0:P].rearrange("p (g e) -> p g e", e=E1)))
        then(dve.tensor_reduce(R(0), L(2), AX.X, ALU.max))
        dve.tensor_tensor(L(0), L(2), wide(0), ALU.subtract).then_inc(*dve_done("sub"))
        then(dve.tensor_tensor(L(3), L(2), wide(0), ALU.is_equal))
        then(dve.tensor_tensor(L(3), L(3), prefer[:, :, :], ALU.mult))
        then(dve.tensor_reduce(R(1), L(3), AX.X, ALU.max))
        then(dve.tensor_tensor(L(4), prefer[:, :, :], wide(1), ALU.is_equal))
        dve.tensor_copy(oh[:, :, :], L(4)).then_inc(*dve_done("onehot"))
        dve.wait_ge(*act_exp.at("e"))
        then(dve.tensor_reduce(R(2), L(1), AX.X, ALU.add))
        then(dve.reciprocal(R(2), R(2)))
        dve.wait_ge(*pe_counts.at("all"))
        tv = BANK[4][:, 0:P].rearrange("p (g e) -> p g e", e=E1)
        then(dve.tensor_copy(tot[:, :, :], tv))
        src, k, n = tot[:, :, :], 1, 0
        while k < G:
            dst = run[:, n % 2, :, :]
            dve.tensor_copy(dst[:, 0:k, :], src[:, 0:k, :])
            then(dve.tensor_tensor(dst[:, k:G, :], src[:, k:G, :], src[:, 0:G - k, :], ALU.add))
            src, k, n = dst, 2 * k, n + 1
        then(dve.tensor_tensor(src, src, tot[:, :, :], ALU.subtract))
        then(dve.tensor_tensor(src, src, BANK[3][:, 0:P].rearrange("p (g e) -> p g e", e=E1), ALU.add))
        then(dve.tensor_tensor(src, src, L(4), ALU.mult))
        a = dve.tensor_reduce(R(3), src, AX.X, ALU.add)
        a.then_inc(*dve_done("counted"))
        dve.wait_ge(*dve_done.at("counted"))
        then(dve.tensor_scalar(R(4), R(1), -float(CAP), float(E1 * CAP - 1), ALU.mult, ALU.add))
        then(dve.tensor_tensor(R(4), R(4), R(3), ALU.add))
        then(dve.tensor_scalar(R(5), R(3), float(CAP), float(2 * SLOTS), ALU.is_gt, ALU.mult))
        then(dve.tensor_tensor(R(4), R(4), R(5), ALU.add))
        dve.tensor_copy(idx[:, :], R(4)).then_inc(*dve_done("idx"))

        def weights_low(name, e):
            low, high, full = {"w1": (w1_low, w1_high, w1), "w2": (w2_low, w2_high, w2)}[name]
            dve.wait_ge(*act_high.at(name, e))
            dve.tensor_tensor(low[:, :, :], full[:, :, :], high[:, :, :], ALU.subtract).then_inc(*dve_low(name, e))

        weights_low("w1", 0)
        weights_low("w2", 0)
        for n in range(ST // 2):
            dve.wait_ge(*act_rows.at(n))
            at = slice(2 * n * P, (2 * n + 2) * P)
            dve.tensor_tensor(xs_low[:, :, at], TURN[n % 4][:, :].rearrange("p (a b) -> p a b", a=CC),
                              xs_high[:, :, at], ALU.subtract).then_inc(*dve_rows(n))
        for e in range(E1):
            for f in range(FC):
                dve.wait_ge(*act_up.at(e, f))
                dve.tensor_tensor(hid_low[e % 2][:, f, :], hid[:, (e * FC + f) % 3, :], hid_high[e % 2][:, f, :],
                                  ALU.subtract).then_inc(*dve_hid(e, f))
            if e + 1 < E1:
                weights_low("w1", e + 1)
            for j, (c0, m) in enumerate(CH):
                dve.wait_ge(*pe_down.at(e, j))
                if e >= 1:
                    dve.wait_ge(*expert_out[j].at(e - 1))
                dve.tensor_tensor(eo[0:m, j, :], DOWNS[j][0:m, 0:C], b2[0:m, e, :], ALU.add)\
                   .then_inc(*dve_down(e, j))
            if e + 1 < E1:
                weights_low("w2", e + 1)
        def normalised(k):
            dve.wait_ge(*pool_done.at("rstd", k))
            for g in range(4 * k, 4 * k + 4):
                a = dve.tensor_scalar(back[:, g, :], x5[:, g, :], mv[:, g, 0:1], rstd[:, g:g + 1], ALU.subtract,
                                      ALU.mult)
            a.then_inc(*dve_out(k))

        for k in range(4):
            dve.wait_ge(*gathered[k].at(4 * k + 3))
            four = range(4 * k, 4 * k + 4)
            for g in four:
                a = dve.scalar_tensor_tensor(out=x5[:, g, :], in0=back[:, g, :], scalar=red[:, 2, g:g + 1],
                                             in1=x5[:, g, :], op0=ALU.mult, op1=ALU.add)
            then(a)
            for g in four:
                a = dve.bn_stats(st[:, g, :], x5[:, g, :])
            then(a)
            for g in four:
                a = dve.bn_aggr(mv[:, g, :], st[:, g, :])
            a.then_inc(*dve_done("stats", k))
            if k >= 1:
                normalised(k - 1)
        normalised(3)

    @block.gpsimd
    def _(pool):
        pool.wait_ge(*dve_done.at("zero"))
        for n in range(ST):
            pool.dma_start(slots_dram[n * P:(n + 1) * P, :], zero[:, :]).then_inc(*cleared(n))
        pool.wait_ge(*cleared.at(ST - 1))
        pool.wait_ge(*dve_done.at("idx"))
        for g in range(G):
            pool.indirect_dma_start(slots_dram, bass.IndirectOffsetOnAxis(ap=idx[:, g:g + 1], axis=0), x5[:, g, :],
                                    None, bounds_check=SLOTS - 1, oob_is_err=False).then_inc(*scattered(g))
        pool.wait_ge(*pe_rows.at(ST // 2 - 1))
        pool.memset(back, 0.0).then_inc(*pool_done("back"))
        for j in range(3):
            pool.wait_ge(*expert_out[j].at(E1 - 1))
        pool.wait_ge(*pool_done.at("back"))
        for g in range(G):
            pool.indirect_dma_start(back[:, g, :], None, expert_dram,
                                    bass.IndirectOffsetOnAxis(ap=idx[:, g:g + 1], axis=0),
                                    bounds_check=SLOTS - 1, oob_is_err=False).then_inc(*gathered[g // 4](g))
        for k in range(4):
            pool.wait_ge(*dve_done.at("stats", k))
            four = slice(4 * k, 4 * k + 4)
            a = pool.tensor_scalar(ve[:, four], mv[:, four, 1], 1e-5, None, ALU.add)
            a.then_inc(*pool_chain())
            pool.wait_ge(pool_chain.sem, pool_chain.count)
            pool.tensor_tensor(rstd[:, four], ve[:, four], half[:, four], ALU.pow).then_inc(*pool_done("rstd", k))


def layouts(inp):
    a = {k: np.asarray(v) for k, v in inp.items()}
    f = np.float32
    order = np.array([(hh * 2 + c) * D + d for c in range(CC) for d in range(D) for hh in range(H // CC)])
    chunked = lambda w: w.reshape(-1, P, w.shape[1]).transpose(1, 0, 2)
    w0 = a["L0_attn_W"]
    qkv = [(w0[:C].T, w0[C:2 * C].T, w0[2 * C:].T),
           (a["L0_xattn_Wq"].T, a["L0_xattn_Wk"].T, a["L0_xattn_Wv"].T),
           (a["L0_ffn_wq"].T, a["L0_ffn_wk"].T, a["L0_ffn_wv"].T),
           (a["L1_attn_Wq"].T, a["L1_attn_Wk"].T, a["L1_attn_Wv"].T),
           (a["L1_xattn_wq_k"], a["L1_xattn_wk_k"], a["L1_xattn_wv_k"])]
    ws = []
    for q, k, v in qkv:
        ws += [q[:, order], k[:, order], v]
    ws += [a["L0_xattn_Wo"].T, a["L0_ffn_wo"].T, a["L1_attn_Wo"].T, a["L1_xattn_wo_k"]]
    out = {"proj": np.stack([chunked(w) for w in ws], 1)}
    two = lambda v: v.reshape(2, P).T
    b0 = a["L0_attn_b"]
    cs = [two(a["L0_xattn_g1"]), two(a["L0_xattn_b1"]), two(a["L0_xattn_g2"]), two(a["L0_xattn_b2"]),
          two(a["L0_ffn_n1_w"]), two(a["L0_ffn_n2_w"]), two(a["L1_attn_ln_w"]), two(a["L1_attn_ln_b"]),
          two(b0[:C][order]), two(b0[C:2 * C][order]), two(a["L1_attn_bq"][order]), two(a["L1_attn_bk"][order]),
          two(a["L1_xattn_wq_b"][order]), two(a["L1_xattn_wk_b"][order]),
          np.stack([np.repeat(a["L0_ffn_qn_w"], 8), np.repeat(a["L0_ffn_kn_w"], 8)], 1)]
    cs.append(np.zeros((P, 32 - 2 * len(cs)), f))
    out["cols"] = np.concatenate(cs, 1)
    rs = [b0[2 * C:], a["L0_xattn_bo"], a["L1_attn_bv"], a["L1_attn_bo"], a["L1_xattn_wv_b"], a["L1_xattn_wo_b"]]
    out["rows"] = np.broadcast_to(np.stack(rs)[None], (P, 6, C))
    for name, src in (("up0", "e0_up"), ("up1a", "e1_w1"), ("up1b", "e1_w2"), ("l1", "e2_l1"), ("l2", "e2_l2"),
                      ("l3", "e2_l3"), ("down3", "e3_down"), ("up3", "e3_up"), ("gate", "gate_w")):
        out[name] = chunked(a["L0_ffn_" + src].T)
    out["downs"] = np.stack([chunked(a["L0_ffn_" + n].T[:, SKIP:]) for n in ("e0_down", "e1_down", "e2_l4", "e3_out")], 1)
    ahead = lambda v: np.concatenate([v, v[:1]])
    out["x"], out["ctx"] = ahead(a["x"]), ahead(a["ctx_1024"])
    out["ctxT"] = a["ctx_1024"].transpose(0, 2, 1)
    m = a["mask_BxSxS2_ik1"]
    tiles = lambda v: v.reshape(B, TT, P, S).transpose(0, 2, 1, 3)
    out["mask"] = ahead(tiles(m))
    out["maskT"] = ahead(tiles(m.transpose(0, 2, 1)))
    out["gpT"] = tiles(a["fside_BxSxS2_0"].transpose(0, 2, 1))
    mb = np.ascontiguousarray(a["mask_BxS2_bf1"]).view(np.uint8)
    out["m_cols"] = ahead(mb.reshape(B, TT, P).transpose(0, 2, 1))
    out["m_rows"] = ahead(mb.reshape(B, 1, S))
    out["wg"] = chunked(a["L1_ffn_wg"])
    out["w1"] = a["L1_ffn_w1"].reshape(E1, CC, P, DFF).transpose(0, 2, 1, 3)
    out["w2"] = a["L1_ffn_w2"].reshape(E1, DFF // P, P, C).transpose(0, 2, 1, 3)
    out["b1"] = a["L1_ffn_b1"].reshape(E1, DFF // P, P).transpose(2, 0, 1)
    out["b2"] = np.broadcast_to(a["L1_ffn_b2"][None], (P, E1, C))
    i = np.arange(P)
    out["ident"] = np.eye(P, dtype=f)
    out["rope_swap"] = (i[:, None] == (i[None, :] ^ (H // CC))).astype(f)
    j = np.arange(2 * H)[:, None, None]
    out["head_spread"] = (j == np.arange(2 * CC)[:, None] * (H // CC) + i % (H // CC)).astype(f)
    out["head_sum"] = out["head_spread"].transpose(2, 1, 0)
    out["causal_q"] = np.where(i[None, :] > i[:, None], f(LOW), f(0)).astype(f)
    out["causal_k"] = np.ascontiguousarray(out["causal_q"].T)
    out["upto"] = (i[:, None] <= i[None, :]).astype(f)
    freq = (f(1.0) / np.power(f(10000.0), np.arange(0, D, 2, dtype=f) / f(D))).astype(f)
    angle = (np.arange(S, dtype=f)[None, :] * freq[:, None]).astype(f)
    d = i // (H // CC)
    out["rope_cos"] = np.cos(angle)[d // 2].astype(f)
    out["rope_sin"] = (np.sin(angle)[d // 2] * np.where(d % 2 == 0, -1.0, 1.0)[:, None]).astype(f)
    out["prefer"] = np.broadcast_to(np.array([4, 3, 2, 1], f), (P, TT, 4))
    out["prefer8"] = np.broadcast_to(np.arange(E1, 0, -1).astype(f), (P, B * S // P, E1))
    return {k: np.ascontiguousarray(v) for k, v in out.items()}


def program(nc, arrays, known):
    t = {}
    for name, v in arrays.items():
        t[name] = nc.dram_tensor(f"in_{name}", v.shape, mybir.dt.from_np(v.dtype), kind="ExternalInput").ap()
    t["out"] = nc.dram_tensor("out_x", [B * S, C], F32, kind="ExternalOutput").ap()
    for name in ("x", "ctx", "ctxT"):
        t[name] = t[name].rearrange("b (t p) c -> b p t c", p=P)
    build(nc, t, known)
    return nc


def kernel(**inputs):
    import concourse.bacc as bacc
    from concourse.bass_utils import run_bass_kernel_spmd
    arrays = layouts(inputs)
    known = {"pass": False}
    program(bacc.Bacc("TRN2", target_bir_lowering=False, num_devices=1), arrays, known)
    known["pass"] = True
    nc = program(bacc.Bacc("TRN2", target_bir_lowering=False, num_devices=1), arrays, known)
    r = run_bass_kernel_spmd(nc, [{f"in_{k}": v for k, v in arrays.items()}], core_ids=[0])
    return r.results[0]["out_x"].reshape(B, S, C)
```
